# Optimizing a Trainium2 kernel written in Bass

```python
import numpy as np
import jax
import jax.numpy as jnp

def _softmax(x, axis=-1):
    return jax.nn.softmax(x, axis=axis)

def _gelu(x):
    return jax.nn.gelu(x, approximate=True)

def _silu(x):
    return jax.nn.silu(x)

def _sigmoid(x):
    return jax.nn.sigmoid(x)

def _layernorm(x, axis=-1, eps=1e-05):
    m = jnp.mean(x, axis=axis, keepdims=True)
    v = jnp.var(x, axis=axis, keepdims=True)
    return (x - m) / jnp.sqrt(v + eps)

def _scatter_add(tgt, idx, src, axis=0):
    return tgt.at[idx].add(src)

def _segment_sum(src, seg, n):
    return jax.ops.segment_sum(src, seg, n)
kernel_name = 'mk_adaln_ffn_d2_seqx_r8_6aba30'

def setup_inputs(seed: int=0):
    np.random.seed(seed)
    _w = jnp.asarray

    def _rec_inputs():
        import jax
        import jax.numpy as jnp
        _rk = jax.random.key(seed)
        x = -0.0003929 + 0.9999 * jax.random.normal(jax.random.fold_in(_rk, 1), (32, 32, 512), jnp.float32)
        _lenS = 32 - jax.random.randint(jax.random.fold_in(_rk, 7), (32,), 0, max(1, 32 // 4) + 1, jnp.int32)
        _lenS2 = 32 - jax.random.randint(jax.random.fold_in(_rk, 8), (32,), 0, max(1, 32 // 4) + 1, jnp.int32)
        itok_B_8_3872 = jax.random.randint(jax.random.fold_in(_rk, 11), (32,), 8, 3873, jnp.int32)
        itok_Bx16_0_63 = jax.random.randint(jax.random.fold_in(_rk, 12), (32, 16), 0, 64, jnp.int32)
        itok_B_207_1644 = jax.random.randint(jax.random.fold_in(_rk, 13), (32,), 207, 1645, jnp.int32)
        return (x, itok_B_8_3872, itok_Bx16_0_63, itok_B_207_1644)
    x, itok_B_8_3872, itok_Bx16_0_63, itok_B_207_1644 = _rec_inputs()

    def _L0_cond_setup():
        import math
        import jax, jax.numpy as jnp
        import numpy as np
        H, N, B, L = (32, 64, 16, 512)
        DT_MIN, DT_MAX = (0.001, 0.1)

        def _get_kernel(log_dt, C, log_A_real, A_imag, length):
            Cc = C[..., 0] + 1j * C[..., 1]
            dt = jnp.exp(log_dt)
            A = -jnp.exp(log_A_real) + 1j * A_imag
            dtA = A * dt[:, None]
            P = dtA[:, :, None] * jnp.arange(length, dtype=jnp.float32)
            Cs = Cc * (jnp.exp(dtA) - 1.0) / A
            K = 2.0 * jnp.einsum('hn,hnl->hl', Cs, jnp.exp(P)).real
            return K
        key = jax.random.key(seed)
        ks = jax.random.split(key, 6)
        u = jax.random.normal(ks[0], (B, H, L), dtype=jnp.float32)
        length = jax.random.randint(ks[1], (B,), 0, L)
        log_dt = jax.random.uniform(ks[2], (H,), dtype=jnp.float32) * (math.log(DT_MAX) - math.log(DT_MIN)) + math.log(DT_MIN)
        C = jax.random.normal(ks[3], (H, N, 2), dtype=jnp.float32)
        log_A_real = jnp.log(0.5 * jnp.ones((H, N), dtype=jnp.float32))
        A_imag = math.pi * jnp.broadcast_to(jnp.arange(N, dtype=jnp.float32), (H, N))
        D = jax.random.normal(ks[4], (H,), dtype=jnp.float32)
        return {'u': u, 'length': length, 'log_dt': log_dt, 'C': C, 'log_A_real': log_A_real, 'A_imag': A_imag, 'D': D}
    _L0_cond_all = _L0_cond_setup()
    _L0_cond_in = {k: v for k, v in _L0_cond_all.items() if k in ('log_dt', 'C', 'log_A_real', 'A_imag', 'D')}
    del _L0_cond_all

    def _L0_ffn_setup():
        import jax, jax.numpy as jnp
        import numpy as np
        TOP_K = 2
        SCALING = 32.0 / 64.0
        key = jax.random.key(seed)
        ks = jax.random.split(key, 6)
        Bsz, S, Din, Dout, R, E = (4, 256, 512, 512, 64, 16)
        x = jax.random.normal(ks[0], (Bsz, S, Din), dtype=jnp.float32)
        base_w = jax.random.normal(ks[1], (Dout, Din), dtype=jnp.float32) * 0.02
        base_b = jax.random.normal(ks[2], (Dout,), dtype=jnp.float32) * 0.02
        A = jax.random.normal(ks[3], (R, Din), dtype=jnp.float32) * (1.0 / np.sqrt(Din))
        B = jax.random.normal(ks[4], (E, Dout, R), dtype=jnp.float32) * 0.02
        router_w = jax.random.normal(ks[5], (E, Din), dtype=jnp.float32) * 0.02
        return {'x': x, 'base_w': base_w, 'base_b': base_b, 'A': A, 'B': B, 'router_w': router_w}
    _L0_ffn_all = _L0_ffn_setup()
    _L0_ffn_in = {k: v for k, v in _L0_ffn_all.items() if k in ('base_w', 'base_b', 'A', 'B', 'router_w')}
    del _L0_ffn_all

    def _L1_cond_setup():
        import jax, jax.numpy as jnp
        import numpy as np
        B, S, HID = (4, 128, 512)
        D, HQ, HK = (128, 32, 8)
        PAGES, PSIZE, NPP = (64, 32, 16)
        THETA = 10000.0
        EPS = 1e-06
        SCALE = 1.0 / float(np.sqrt(D))

        def _rmsnorm(t, w):
            var = jnp.mean(t * t, axis=-1, keepdims=True)
            return t * jax.lax.rsqrt(var + EPS) * w

        def _rope(t, pos):
            inv_freq = 1.0 / THETA ** (jnp.arange(0, D, 2, dtype=jnp.float32) / D)
            freqs = pos[..., None].astype(jnp.float32) * inv_freq
            cos = jnp.cos(freqs)[:, :, None, :]
            sin = jnp.sin(freqs)[:, :, None, :]
            t1, t2 = (t[..., :D // 2], t[..., D // 2:])
            return jnp.concatenate([t1 * cos - t2 * sin, t2 * cos + t1 * sin], axis=-1)
        key = jax.random.key(seed)
        ks = jax.random.split(key, 10)
        x = jax.random.normal(ks[0], (B, S, HID), jnp.float32)
        Wq = jax.random.normal(ks[1], (HQ * D, HID), jnp.float32) * 0.02
        Wk = jax.random.normal(ks[2], (HK * D, HID), jnp.float32) * 0.02
        Wv = jax.random.normal(ks[3], (HK * D, HID), jnp.float32) * 0.02
        Wo = jax.random.normal(ks[4], (HID, HQ * D), jnp.float32) * 0.02
        q_norm_w = jax.random.uniform(ks[5], (D,), jnp.float32)
        k_norm_w = jax.random.uniform(ks[6], (D,), jnp.float32)
        k_cache = jax.random.normal(ks[7], (PAGES, PSIZE, HK, D), jnp.float32)
        v_cache = jax.random.normal(ks[8], (PAGES, PSIZE, HK, D), jnp.float32)
        block_table = jnp.arange(B * NPP, dtype=jnp.int32).reshape(B, NPP)
        cache_seqlens = jax.random.randint(ks[9], (B,), 0, 475).astype(jnp.int32)
        return dict(x=x, Wq=Wq, Wk=Wk, Wv=Wv, Wo=Wo, q_norm_w=q_norm_w, k_norm_w=k_norm_w, k_cache=k_cache, v_cache=v_cache, block_table=block_table, cache_seqlens=cache_seqlens)
    _L1_cond_all = _L1_cond_setup()
    _L1_cond_in = {k: v for k, v in _L1_cond_all.items() if k in ('Wq', 'Wk', 'Wv', 'Wo', 'q_norm_w', 'k_norm_w', 'k_cache', 'v_cache')}
    del _L1_cond_all

    def _L1_ffn_setup():
        import jax, jax.numpy as jnp
        import numpy as np
        N_EXPERTS = 8
        TOP_K = 2
        D_MODEL = 512
        RANK = 64
        key = jax.random.key(seed)
        k0, k1, k2, k3 = jax.random.split(key, 4)
        inputs = jax.random.normal(k0, (4, 256, D_MODEL), dtype=jnp.float32)
        gate_w = jax.random.normal(k1, (N_EXPERTS, D_MODEL), dtype=jnp.float32) * 0.02
        lora_A = jax.random.normal(k2, (N_EXPERTS, RANK, D_MODEL), dtype=jnp.float32) * 0.02
        lora_B = jax.random.normal(k3, (N_EXPERTS, D_MODEL, RANK), dtype=jnp.float32) * 0.02
        return {'inputs': inputs, 'gate_w': gate_w, 'lora_A': lora_A, 'lora_B': lora_B}
    _L1_ffn_all = _L1_ffn_setup()
    _L1_ffn_in = {k: v for k, v in _L1_ffn_all.items() if k in ('gate_w', 'lora_A', 'lora_B')}
    del _L1_ffn_all
    return {'x': x, 'itok_B_8_3872': itok_B_8_3872, 'itok_Bx16_0_63': itok_Bx16_0_63, 'itok_B_207_1644': itok_B_207_1644, 'L0_cond_log_dt': _L0_cond_in['log_dt'], 'L0_cond_C': _L0_cond_in['C'], 'L0_cond_log_A_real': _L0_cond_in['log_A_real'], 'L0_cond_A_imag': _L0_cond_in['A_imag'], 'L0_cond_D': _L0_cond_in['D'], 'L0_ffn_base_w': _L0_ffn_in['base_w'], 'L0_ffn_base_b': _L0_ffn_in['base_b'], 'L0_ffn_A': _L0_ffn_in['A'], 'L0_ffn_B': _L0_ffn_in['B'], 'L0_ffn_router_w': _L0_ffn_in['router_w'], 'L1_cond_Wq': _L1_cond_in['Wq'], 'L1_cond_Wk': _L1_cond_in['Wk'], 'L1_cond_Wv': _L1_cond_in['Wv'], 'L1_cond_Wo': _L1_cond_in['Wo'], 'L1_cond_q_norm_w': _L1_cond_in['q_norm_w'], 'L1_cond_k_norm_w': _L1_cond_in['k_norm_w'], 'L1_cond_k_cache': _L1_cond_in['k_cache'], 'L1_cond_v_cache': _L1_cond_in['v_cache'], 'L1_ffn_gate_w': _L1_ffn_in['gate_w'], 'L1_ffn_lora_A': _L1_ffn_in['lora_A'], 'L1_ffn_lora_B': _L1_ffn_in['lora_B']}

def reference(x, itok_B_8_3872, itok_Bx16_0_63, itok_B_207_1644, L0_cond_log_dt, L0_cond_C, L0_cond_log_A_real, L0_cond_A_imag, L0_cond_D, L0_ffn_base_w, L0_ffn_base_b, L0_ffn_A, L0_ffn_B, L0_ffn_router_w, L1_cond_Wq, L1_cond_Wk, L1_cond_Wv, L1_cond_Wo, L1_cond_q_norm_w, L1_cond_k_norm_w, L1_cond_k_cache, L1_cond_v_cache, L1_ffn_gate_w, L1_ffn_lora_A, L1_ffn_lora_B):
    import jax
    import jax.numpy as jnp

    def _L0_cond_ref(u, length, log_dt, C, log_A_real, A_imag, D):
        import math
        import jax, jax.numpy as jnp
        import numpy as np
        H, N, B, L = (32, 64, 16, 512)
        DT_MIN, DT_MAX = (0.001, 0.1)

        def _get_kernel(log_dt, C, log_A_real, A_imag, length):
            Cc = C[..., 0] + 1j * C[..., 1]
            dt = jnp.exp(log_dt)
            A = -jnp.exp(log_A_real) + 1j * A_imag
            dtA = A * dt[:, None]
            P = dtA[:, :, None] * jnp.arange(length, dtype=jnp.float32)
            Cs = Cc * (jnp.exp(dtA) - 1.0) / A
            K = 2.0 * jnp.einsum('hn,hnl->hl', Cs, jnp.exp(P)).real
            return K
        Bq, Hq, Lq = u.shape
        mask = (jnp.arange(Lq) < length[:, None]).astype(u.dtype)
        u_m = u * mask[:, None, :]
        kernel = _get_kernel(log_dt, C, log_A_real, A_imag, Lq)
        n = 2 * Lq
        k_f = jnp.fft.rfft(kernel, n=n)
        u_f = jnp.fft.rfft(u_m, n=n)
        y = jnp.fft.irfft(u_f * k_f, n=n)[..., :Lq]
        y = y + u_m * D[:, None]
        return y * mask[:, None, :]

    def _L0_ffn_ref(x, base_w, base_b, A, B, router_w):
        import jax, jax.numpy as jnp
        import numpy as np
        TOP_K = 2
        SCALING = 32.0 / 64.0
        base_out = jnp.einsum('bsi,oi->bso', x, base_w) + base_b
        res_hidden = jnp.einsum('bsi,ri->bsr', x, A)
        logits = jnp.einsum('bsi,ei->bse', x, router_w)
        probs = jax.nn.softmax(logits, axis=-1)
        topw, topi = jax.lax.top_k(probs, TOP_K)
        topw = topw / (jnp.sum(topw, axis=-1, keepdims=True) + 1e-06)
        num_experts = B.shape[0]
        combine = jnp.sum(jax.nn.one_hot(topi, num_experts, dtype=x.dtype) * topw[..., None], axis=-2)
        delta = jnp.einsum('bse,bsr,eor->bso', combine, res_hidden, B)
        return base_out + delta * SCALING

    def _L1_cond_ref(x, Wq, Wk, Wv, Wo, q_norm_w, k_norm_w, k_cache, v_cache, block_table, cache_seqlens):
        import jax, jax.numpy as jnp
        import numpy as np
        B, S, HID = (4, 128, 512)
        D, HQ, HK = (128, 32, 8)
        PAGES, PSIZE, NPP = (64, 32, 16)
        THETA = 10000.0
        EPS = 1e-06
        SCALE = 1.0 / float(np.sqrt(D))

        def _rmsnorm(t, w):
            var = jnp.mean(t * t, axis=-1, keepdims=True)
            return t * jax.lax.rsqrt(var + EPS) * w

        def _rope(t, pos):
            inv_freq = 1.0 / THETA ** (jnp.arange(0, D, 2, dtype=jnp.float32) / D)
            freqs = pos[..., None].astype(jnp.float32) * inv_freq
            cos = jnp.cos(freqs)[:, :, None, :]
            sin = jnp.sin(freqs)[:, :, None, :]
            t1, t2 = (t[..., :D // 2], t[..., D // 2:])
            return jnp.concatenate([t1 * cos - t2 * sin, t2 * cos + t1 * sin], axis=-1)
        bsz, seqlen, _ = x.shape
        q = jnp.einsum('bsd,ed->bse', x, Wq).reshape(bsz, seqlen, HQ, D)
        k = jnp.einsum('bsd,ed->bse', x, Wk).reshape(bsz, seqlen, HK, D)
        v = jnp.einsum('bsd,ed->bse', x, Wv).reshape(bsz, seqlen, HK, D)
        q = _rmsnorm(q, q_norm_w)
        k = _rmsnorm(k, k_norm_w)
        pos = cache_seqlens[:, None] + jnp.arange(seqlen)[None, :]
        q = _rope(q, pos)
        k = _rope(k, pos)
        L = NPP * PSIZE
        kc = k_cache[block_table].reshape(bsz, L, HK, D)
        vc = v_cache[block_table].reshape(bsz, L, HK, D)
        k_all = jnp.concatenate([kc, k], axis=1)
        v_all = jnp.concatenate([vc, v], axis=1)
        valid_c = jnp.arange(L)[None, :] < cache_seqlens[:, None]
        valid = jnp.concatenate([valid_c, jnp.ones((bsz, seqlen), dtype=bool)], axis=1)
        rep = HQ // HK
        k_all = jnp.repeat(k_all, rep, axis=2)
        v_all = jnp.repeat(v_all, rep, axis=2)
        scores = jnp.einsum('bqhd,bkhd->bhqk', q, k_all) * SCALE
        scores = jnp.where(valid[:, None, None, :], scores, -1e+30)
        probs = jax.nn.softmax(scores, axis=-1)
        o = jnp.einsum('bhqk,bkhd->bqhd', probs, v_all)
        o = o.reshape(bsz, seqlen, HQ * D)
        return jnp.einsum('bse,de->bsd', o, Wo)

    def _L1_ffn_ref(inputs, gate_w, lora_A, lora_B):
        import jax, jax.numpy as jnp
        import numpy as np
        N_EXPERTS = 8
        TOP_K = 2
        D_MODEL = 512
        RANK = 64
        x = inputs.reshape(-1, inputs.shape[-1])
        T = x.shape[0]
        gate_probs = jax.nn.softmax(x @ gate_w.T, axis=-1)
        weights, sel = jax.lax.top_k(gate_probs, TOP_K)
        weights = weights / jnp.sum(weights, axis=-1, keepdims=True)
        w_full = jnp.zeros((T, N_EXPERTS), dtype=x.dtype).at[jnp.arange(T)[:, None], sel].add(weights)
        out = jnp.zeros((T, D_MODEL), dtype=x.dtype)
        for e in range(N_EXPERTS):
            y = x @ lora_A[e].T @ lora_B[e].T
            out = out + w_full[:, e:e + 1] * y
        return out.reshape(inputs.shape[:-1] + (D_MODEL,))
    x = x + _L0_ffn_ref(_L0_cond_ref(x, itok_B_8_3872, L0_cond_log_dt, L0_cond_C, L0_cond_log_A_real, L0_cond_A_imag, L0_cond_D), L0_ffn_base_w, L0_ffn_base_b, L0_ffn_A, L0_ffn_B, L0_ffn_router_w)
    x = x + _L1_ffn_ref(_L1_cond_ref(x, L1_cond_Wq, L1_cond_Wk, L1_cond_Wv, L1_cond_Wo, L1_cond_q_norm_w, L1_cond_k_norm_w, L1_cond_k_cache, L1_cond_v_cache, itok_Bx16_0_63, itok_B_207_1644), L1_ffn_gate_w, L1_ffn_lora_A, L1_ffn_lora_B)
    return x

_drawn_inputs = setup_inputs


def setup_inputs(seed=0):
    import zlib

    import numpy as np

    out = dict(_drawn_inputs(seed))
    spreads = {'L0_cond_log_A_real': (-0.6931471824645996, 0.2)}
    factors = {'L0_ffn_base_b': 3.59,
     'L1_cond_Wq': 8.0,
     'L1_cond_Wk': 8.0,
     'L1_cond_Wv': 8.0,
     'L1_cond_Wo': 8.0,
     'L1_cond_q_norm_w': 8.0,
     'L1_cond_k_norm_w': 8.0,
     'L1_cond_k_cache': 8.0,
     'L1_cond_v_cache': 8.0,
     'L1_ffn_gate_w': 8.0,
     'L1_ffn_lora_A': 8.0,
     'L1_ffn_lora_B': 8.0}
    for name, (base, spread) in spreads.items():
        noise = np.random.default_rng([zlib.crc32(name.encode()), seed]).standard_normal(out[name].shape)
        drawn = base * np.exp(spread * noise) if base else spread * noise
        out[name] = jnp.asarray(drawn.astype(out[name].dtype))
    for name, factor in factors.items():
        out[name] = (out[name] * factor).astype(out[name].dtype)
    return out
```

```python
from contextlib import ExitStack

import numpy as np

import concourse.bass as bass
from concourse import mybir

ALU = mybir.AluOpType
ACT = mybir.ActivationFunctionType
AX_X = mybir.AxisListType.X
F32 = mybir.dt.float32
I32 = mybir.dt.int32
U32 = mybir.dt.uint32

P = 128
B, S, HID = 32, 32, 512
TOK = B * S
NT = TOK // P
NJ = HID // P
BT4 = P // S
NSTATE = 64
E0, R0 = 16, 64
E1, R1 = 8, 64
D, HQ, HK = 128, 32, 8
REP = HQ // HK
PAGES, PSIZE, NPP = 64, 32, 16
L = NPP * PSIZE
KEYS = L + S
KR, KQ = 32, 16
KPAD = 640
SCALE = float(np.float32(1.0 / np.sqrt(D)))
EPS = 1e-6
MAGIC = 12582912.0
TWO_PI_HI = 6.28125
TWO_PI_LO = float(2.0 * np.pi - 6.28125)
INV_TWO_PI = float(1.0 / (2.0 * np.pi))
PI_F = float(np.float32(3.1415925))
LN2_HI = 0.693359375
LN2_LO = float(np.log(2.0) - 0.693359375)
NEG = -1e30

C_ID = 0
C_F = C_ID + P
C_FR = C_F + NJ
C_M = C_FR + NJ
C_S = C_M + KR + KQ
C_P = C_S + 1
C_IF = C_P + 1
C_POS = C_IF + D // 2
C_S0 = C_POS + KEYS
NCONST = C_S0 + (E0 // 2) * P


def constants():
    c = np.zeros((P, NCONST), np.float32)
    p = np.arange(P)
    c[:, C_ID:C_ID + P] = np.eye(P)
    for j in range(NJ):
        c[:, C_F + j] = j * P + p
        c[:, C_FR + j] = j * P + P - 1 - p
    c[:, C_M:C_M + KR] = np.arange(KR)
    c[:, C_M + KR:C_M + KR + KQ] = KR * np.arange(KQ)
    c[:, C_S] = p % S
    c[:, C_P] = p
    half = np.arange(0, D, 2, dtype=np.float32) / np.float32(D)
    c[:, C_IF:C_IF + D // 2] = np.float32(1.0) / np.power(np.float32(10000.0), half)
    c[:, C_POS:C_POS + L] = np.arange(L)
    c[:, C_POS + L:C_POS + KEYS] = -1
    for e in range(E0):
        c[e, C_S0 + e * R0:C_S0 + (e + 1) * R0] = 1
    return c


KB = 256
SLOT = 16 // 2 * KB
M_WK, M_WV = 16 * KB, 32 * KB
M_U, M_Y, M_BW, M_BT = 48 * KB, 64 * KB, 80 * KB, 88 * KB
M_WQ = 48 * KB
M_OT, M_QT, M_KT, M_V = 16 * KB, 32 * KB, 40 * KB, 74 * KB
M_END = 114 * KB


def adaln_program(nc, x, len0, table, seqlens, log_dt, Cc, log_A, A_im, Dskip, base_w, base_b, ffnA, ffnB,
                  router_w, Wq, Wk, Wv, Wo, qnw, knw, k_cache, v_cache, gate_w, lora_A, lora_B, const, out, scratch):
    def dap(t, offset, dims):
        return bass.AP(t.tensor, offset, dims)

    kpad, kT, qT, knT, vn, x1d = (scratch(n, s) for n, s in (
        ("kpad", [S, KPAD]),
        ("kT", [PAGES * P, HK * PSIZE]),
        ("qT", [B, P, HQ * S]),
        ("knT", [B, P, HK * S]),
        ("vn", [B, S, HK * D]),
        ("x1d", [TOK, HID]),
    ))

    with ExitStack() as ctx:
        def sb(name, cols, dt=F32, rows=P):
            return ctx.enter_context(nc.sbuf_tensor(name, [rows, cols], dt))

        def sem(name):
            return ctx.enter_context(nc.semaphore(name))

        cst = sb("cst", NCONST)
        A_ = sb("A_", 64 * KB)
        M_ = sb("M_", M_END)
        x1T = sb("x1T", NJ * TOK)
        small = sb("small", NJ * 152)
        leni = sb("leni", B, I32)
        lenf = sb("lenf", B)
        biasc = sb("biasc", NJ)
        seqi = sb("seqi", B, I32)
        seqf = sb("seqf", B)
        tabi = sb("tabi", B * NPP, I32)
        maskf = tabi[:, 0:NJ * B].bitcast(F32)
        maskr = tabi[:, NJ * B:2 * NJ * B].bitcast(F32)
        idxv = sb("idxv", B * 4, I32)
        idc = sb("idc", BT4 * 20, I32)
        seqc = sb("seqc", BT4)
        stat = sb("stat", 64)
        PS = ctx.enter_context(nc.psum_tensor("PS", [P, 8 * 512], F32))

        def v(t, offset, *dims, p0=0, rows=P, dt=None):
            pitch = t[:, :].ap[0][0]
            return bass.AP(t, p0 * pitch + offset, [[pitch, rows], *[list(d) for d in dims]])

        def bank(k, cols=512, off=0, rows=P):
            return PS[0:rows, k * 512 + off:k * 512 + off + cols]

        ident = cst[:, C_ID:C_ID + P]

        cst_in, len_in, seq_in, tab_in, x_in, par_in, d_in = (sem(n) for n in (
            "cst_in", "len_in", "seq_in", "tab_in", "x_in", "par_in", "d_in"))
        slot_in = [sem("slot_in0"), sem("slot_in1")]
        tp_done = sem("tp_done")
        tp_act, tp_dve = sem("tp_act"), sem("tp_dve")
        kst_out = sem("kst_out")
        chain = sem("chain")
        achain = sem("achain")
        mask_ok, par_t, par_c, exp_arg, exp_ok = (sem(n) for n in ("mask_ok", "par_t", "par_c", "exp_arg", "exp_ok"))
        sin_arg, sin_ok = sem("sin_arg"), sem("sin_ok")
        taps_in, taps_ps, taps_cp, taps_sb, pad_out, taps_out = (sem(n) for n in (
            "taps_in", "taps_ps", "taps_cp", "taps_sb", "pad_out", "taps_out"))
        hank_in = [sem(f"hank_in{i}") for i in range(4)]
        xrev_ok = sem("xrev_ok")
        xf_done, xt_done, xf_cp, xr_cp = sem("xf_done"), sem("xt_done"), sem("xf_cp"), sem("xr_cp")
        conv_done, conv_cp = sem("conv_done"), sem("conv_cp")
        lg_done, cw_ok, ct_done, ct_cp = sem("lg_done"), sem("cw_ok"), sem("ct_done"), sem("ct_cp")
        lx_ok, le_ok = sem("lx_ok"), sem("le_ok")
        rh_done, rh_cp, bc_done, z_ok = sem("rh_done"), sem("rh_cp"), sem("bc_done"), sem("z_ok")
        y_done, x1_ok = sem("y_done"), sem("x1_ok")
        r_done, r_cp, x1_out, x1_back = sem("r_done"), sem("r_cp"), sem("x1_out"), sem("x1_back")
        rope_arg, rope_sin, nw_in = sem("rope_arg"), sem("rope_sin"), sem("nw_in")
        xt_ok, pj_done, pj_read, sq_ok, ms_ok, sd_ok = (sem(n) for n in (
            "xt_ok", "pj_done", "pj_read", "sq_ok", "ms_ok", "sd_ok"))
        ss_ok, nw_ok, rs_ok = sem("ss_ok"), sem("nw_ok"), sem("rs_ok")
        ab_ok, rot_ok, rt_done, rt_cp, v_cp = (sem(n) for n in ("ab_ok", "rot_ok", "rt_done", "rt_cp", "v_cp"))
        st_out = [sem("st_out0"), sem("st_out1")]
        idx_ok, kv_in, q_in = sem("idx_ok"), [sem("kv_in0"), sem("kv_in1")], [sem("q_in0"), sem("q_in1")]
        idc_ok, mrow_ok, seqc_ok = sem("idc_ok"), sem("mrow_ok"), sem("seqc_ok")
        zero_ok, pz_ok = sem("zero_ok"), sem("pz_ok")
        s_done, sm_ok, nm_ok, e_ok, p_ok = (sem(n) for n in ("s_done", "sm_ok", "nm_ok", "e_ok", "p_ok"))
        pt_done, pt_cp, o_done, o_cp = (sem(n) for n in ("pt_done", "pt_cp", "o_done", "o_cp"))
        wo_done, wo_cp, at_done, at_cp = (sem(n) for n in ("wo_done", "wo_cp", "at_done", "at_cp"))
        ha_done, ha_cp, ob_done, ob_cp, out_done = (sem(n) for n in ("ha_done", "ha_cp", "ob_done", "ob_cp", "out_done"))

        def raw(par, k, j, rows=P):
            return v(M_, par * SLOT + k * 512 + j * P, [1, P], rows=rows)

        def slot_all(par):
            return v(M_, par * SLOT, [512, 4], [1, 512])

        def rows_of(w, first):
            return dap(w, first * 512, [[512, P], [P * 512, 4], [1, 512]])

        def dst_small(j):
            return small[:, j * 152:(j + 1) * 152]

        def wide(t, offset):
            return v(t, offset, [1, 512])

        A_PC, A_T, A_BIG = 1024, 1280, 2048
        A_EM = A_BIG + 5 * 768
        A_SR = A_BIG + 7 * 768
        A_X = 32 * KB
        A_KQ = 60 * KB
        NX = KR + KQ

        A_Z1, A_CT, A_RH, A_SM = 0, 40 * KB, 44 * KB, 48 * KB
        A_RP = 16 * KB
        A_TB, A_SQ, A_SK, A_SV = 0, 16 * KB, 48 * KB, 56 * KB
        M_SQ, M_XT, M_RA, M_RB = 0, 4 * KB, 8 * KB, 12 * KB
        M_S, M_P, M_AT, M_MR = 0, 2 * KEYS, 2 * KEYS + 2 * 640, 2 * KEYS + 2 * 640 + 512
        KTB, VB = 17 * 256, 5 * 1024

        block = ctx.enter_context(nc.Block())

        @block.sync
        def _(sp):
            sp.dma_start(v(A_, 0, [P, 2], [1, P], rows=16), dap(Cc, 0, [[P, 16], [16 * P, 2], [1, P]])).then_inc(par_in, 16)
            sp.dma_start(v(A_, 256, [NSTATE, 2], [1, NSTATE], rows=16), dap(log_A, 0, [[NSTATE, 16], [16 * NSTATE, 2], [1, NSTATE]])).then_inc(par_in, 16)
            sp.dma_start(v(A_, 384, [NSTATE, 2], [1, NSTATE], rows=16), dap(A_im, 0, [[NSTATE, 16], [16 * NSTATE, 2], [1, NSTATE]])).then_inc(par_in, 16)
            with nc.allow_non_contiguous_dma(reason="32 numbers"):
                sp.dma_start(v(A_, 512, [1, 2], rows=16), dap(log_dt, 0, [[1, 16], [16, 2]])).then_inc(par_in, 16)
            sp.dma_start(leni[:, :], dap(len0, 0, [[0, P], [1, B]])).then_inc(len_in, 16)
            sp.dma_start(v(stat, 0, [1, S], rows=1), dap(Dskip, 0, [[S, 1], [1, S]])).then_inc(d_in, 16)
            sp.dma_start(v(A_, A_X, [HID, NT], [1, HID]), dap(x, 0, [[HID, P], [P * HID, NT], [1, HID]])).then_inc(x_in, 16)

            def slot(par, n, src):
                if not isinstance(n, int) or n >= 2:
                    sp.wait_ge(tp_done, n * 4 - 4)
                sp.dma_start(slot_all(par), src).then_inc(slot_in[par], 16)

            def slot_experts(par, n, w, first):
                sp.wait_ge(tp_done, n * 4 - 4)
                for e in range(8):
                    sp.dma_start(v(M_, par * SLOT + e * R0, [512, 4], [1, R0]),
                                 dap(w, (first + e) * HID * R0, [[R0, P], [P * R0, 4], [1, R0]])).then_inc(slot_in[par], 16)

            sp.dma_start(v(M_, 0, [1, 512], rows=R0), ffnA).then_inc(slot_in[0], 16)
            sp.dma_start(v(M_, 0, [1, 512], p0=R0, rows=R0), ffnA).then_inc(slot_in[0], 16)
            sp.dma_start(v(M_, 512, [1, 512], rows=E0), router_w).then_inc(slot_in[0], 16)
            sp.dma_start(v(M_, 512, [1, 512], p0=E0, rows=E1), gate_w).then_inc(slot_in[0], 16)
            slot(1, 1, rows_of(base_w, 0))
            for i in range(2):
                slot_experts(i, 2 + i, ffnB, 8 * i)
            for i in range(2):
                slot(i, 4 + i, rows_of(Wk, 512 * i))
            for i in range(2):
                slot(i, 6 + i, rows_of(Wv, 512 * i))

            def keys(i):
                for half in range(2):
                    slot(half, i * 2 + 8 + half,
                         dap(k_cache, i * (512 * HK * D) + half * 512, [[HK * D, P], [P * HK * D, 4], [1, 512]]))
                sp.wait_ge(tp_act, i * 4 + 20)
                sp.wait_ge(tp_dve, i * 4 + 20)
                sp.dma_start(dap(kT, i * (16 * P * 256), [[256, P], [P * 256, 16], [1, 256]]),
                             v(M_, M_Y, [256, 16], [1, 256])).then_inc(kst_out, 16)

            with sp.Fori(0, 4) as i:
                keys(i)

            sp.wait_ge(r_cp, NT)
            sp.dma_start(dap(x1d, 0, [[HID, P], [P * HID, NT], [1, HID]]), v(M_, M_U, [HID, NT], [1, HID])).then_inc(x1_out, 16)

            with sp.Fori(0, 4) as i:
                for par in range(2):
                    slot(par, i * 2 + 16 + par, dap(Wq, i * (1024 * 512) + par * 512 * 512, [[512, P], [P * 512, 4], [1, 512]]))

            def tile_store(t, par):
                sp.wait_ge(rt_cp, t * 10 + 10)
                sp.wait_ge(v_cp, t * 2 + 2)
                sp.dma_start(dap(qT, t * (4 * P * HQ * S), [[HQ * S, P], [P * HQ * S, 4], [1, HQ * S]]),
                             v(A_, A_SQ + 16 * KB * par, [HQ * S, 4], [1, HQ * S])).then_inc(st_out[par], 16)
                sp.dma_start(dap(knT, t * (4 * P * HK * S), [[HK * S, P], [P * HK * S, 4], [1, HK * S]]),
                             v(A_, A_SK + 4 * KB * par, [HK * S, 4], [1, HK * S])).then_inc(st_out[par], 16)
                sp.dma_start(dap(vn, t * (P * HK * D), [[HK * D, P], [1, HK * D]]),
                             v(A_, A_SV + 4 * KB * par, [1, HK * D])).then_inc(st_out[par], 16)

            with sp.Fori(0, 4) as i:
                for par in range(2):
                    tile_store(i * 2 + par, par)

            sp.wait_ge(pj_done, NT * 12)
            sp.wait_ge(rt_done, NT * 10)
            with sp.Fori(0, 4) as i:
                for par in range(2):
                    slot(par, i * 2 + 24 + par,
                         dap(Wo, i * 1024 + par * 512, [[HQ * D, P], [P * HQ * D, 4], [1, 512]]))

            for par in range(2):
                sp.wait_ge(st_out[par], 48 * 4)
            sp.wait_ge(zero_ok, 3)

            def batch_load(b, par, first=False):
                if not first:
                    sp.wait_ge(o_done, b * HK - HK)
                sp.dma_start(v(M_, M_QT + par * HQ * S, [1, HQ * S]), dap(qT, b * (P * HQ * S), [[HQ * S, P], [1, HQ * S]])).then_inc(q_in[par], 16)
                sp.dma_start(v(M_, M_KT + par * KTB + L * HK, [1, HK * S]), dap(knT, b * (P * HK * S), [[HK * S, P], [1, HK * S]])).then_inc(q_in[par], 16)
                sp.dma_start(v(M_, M_V + par * VB + 4096, [1, HK * D], rows=S), dap(vn, b * (S * HK * D), [[HK * D, S], [1, HK * D]])).then_inc(q_in[par], 16)

            for k in range(BT4):
                batch_load(k, k % 2, first=k < 2)
            with sp.Fori(1, NT) as t:
                for k in range(BT4):
                    batch_load(t * BT4 + k, k % 2)

            sp.wait_ge(at_done, NT)
            sp.wait_ge(at_cp, NT)
            slot(0, 32, rows_of(lora_A, 0))
            slot_experts(1, 33, lora_B, 0)
            sp.wait_ge(x1_out, 16)
            sp.dma_start(v(M_, M_KT, [HID, NT], [1, HID]), dap(x1d, 0, [[HID, P], [P * HID, NT], [1, HID]])).then_inc(x1_back, 16)
            for t in range(NT):
                sp.wait_ge(ob_cp, t + 1)
                sp.dma_start(dap(out, t * P * HID, [[HID, P], [1, HID]]), v(M_, M_KT + t * HID, [1, HID])).then_inc(out_done, 16)
            sp.wait_ge(out_done, 16 * NT)

        @block.gpsimd
        def _(pool):
            pool.dma_start(cst[:, :], const).then_inc(cst_in, 16)
            with nc.allow_non_contiguous_dma(reason="a column of 512 numbers"):
                pool.dma_start(biasc[:, :], dap(base_b, 0, [[1, P], [P, NJ]])).then_inc(cst_in, 16)
            pool.dma_start(seqi[:, :], dap(seqlens, 0, [[0, P], [1, B]])).then_inc(seq_in, 16)

            pool.wait_ge(x_in, 16)
            for t in range(NT):
                nc.gpsimd.tensor_copy(v(M_, M_Y + t * HID, [P, NJ], [1, P]),
                                      v(A_, A_X + t * HID + P - 1, [P, NJ], [-1, P])).then_inc(xrev_ok, 1)

            zeros = idxv[0:S, 0:P - 1].bitcast(F32)
            nc.gpsimd.memset(zeros, 0.0).then_inc(zero_ok, 1)
            pool.wait_ge(zero_ok, 1)
            pool.dma_start(dap(kpad, 0, [[KPAD, S], [1, P - 1]]), zeros).then_inc(pad_out, 16)
            pool.wait_ge(taps_sb, 1)
            pool.dma_start(dap(kpad, P - 1, [[KR, KQ], [KPAD, S], [1, KR]]), v(A_, A_KQ, [KR, S], [1, KR], rows=KQ)).then_inc(taps_out, 16)
            pool.wait_ge(taps_out, 16)
            pool.wait_ge(pad_out, 16)
            pool.wait_ge(xt_done, NT)
            for g in range(4):
                pool.dma_start(v(A_, g * 8 * 512, [512, 8], [1, 512]),
                               dap(kpad, g * 8 * KPAD, [[1, P], [KPAD, 8], [1, 512]])).then_inc(hank_in[g], 16)

            pool.wait_ge(conv_done, 8)
            pool.wait_ge(conv_cp, 8)
            pool.dma_start(tabi[:, :], dap(table, 0, [[0, P], [1, B * NPP]])).then_inc(tab_in, 16)
            pool.dma_start(v(A_, A_RP + 5 * 512, [1, D]), dap(qnw, 0, [[0, P], [1, D]])).then_inc(nw_in, 16)
            pool.dma_start(v(A_, A_RP + 5 * 512 + D, [1, D]), dap(knw, 0, [[0, P], [1, D]])).then_inc(nw_in, 16)

            pool.wait_ge(x1_ok, 2 * NJ)
            pool.wait_ge(tp_done, 96)

            def tile(t, par):
                if not isinstance(t, int) or t >= 2:
                    pool.wait_ge(pj_done, t * 12 - 12)
                nc.gpsimd.tensor_copy(v(M_, M_XT + par * 512, [P, NJ], [1, P]),
                                      v(x1T, t * P, [TOK, NJ], [1, P])).then_inc(xt_ok, 1)

            def sums(t):
                for c in range(10):
                    q = c % 2
                    pool.wait_ge(ab_ok, t * 10 + c + 1)
                    nc.gpsimd.tensor_tensor(wide(M_, M_RA + q * 512), wide(M_, M_RA + q * 512),
                                            wide(M_, M_RB + q * 512), ALU.add).then_inc(rot_ok, 1)

            def two_tiles(i):
                tile(i * 2 + 1, 1)
                sums(i * 2)
                tile(i * 2 + 2, 0)
                sums(i * 2 + 1)

            tile(0, 0)
            two_tiles(0)
            with pool.Fori(1, 3) as i:
                two_tiles(i)
            tile(7, 1)
            sums(6)
            sums(7)

            pool.wait_ge(pj_done, NT * 12)
            pool.wait_ge(kst_out, 64)
            for par in range(2):
                nc.gpsimd.memset(v(M_, M_V + par * VB + 4096, [1, 1024]), 0.0).then_inc(zero_ok, 1)
            pool.wait_ge(idx_ok, 1)

            def gather(t, k):
                par = k % 2
                b = t * BT4 + k
                first = isinstance(t, int)
                if not first:
                    pool.wait_ge(kv_in[par], t * 640 - 320 + 320 * (k // 2))
                nc.gpsimd.tensor_copy(idc[:, k * 20:k * 20 + 16], v(tabi, b * NPP, [1, NPP])).then_inc(idc_ok, 1)
                nc.gpsimd.tensor_copy(idc[:, k * 20 + 16:k * 20 + 20], v(idxv, b * 4, [1, 4])).then_inc(idc_ok, 1)
                if not first or k >= 2:
                    pool.wait_ge(o_done, b * HK - HK)
                pool.wait_ge(idc_ok, b * 2 + 2)
                nc.gpsimd.tensor_tensor(stat[:, 61:62], cst[:, 0:1], cst[:, 0:1], ALU.add)
                for s in range(NPP):
                    nc.gpsimd.indirect_dma_start(
                        v(M_, M_KT + par * KTB + s * 256, [1, 256]), None, kT,
                        bass.IndirectOffsetOnAxis(ap=idc[:, k * 20 + s:k * 20 + s + 1].bitcast(U32), axis=0)).then_inc(kv_in[par], 16)
                for s in range(4):
                    nc.gpsimd.indirect_dma_start(
                        v(M_, M_V + par * VB + s * 1024, [1, 1024]), None, v_cache.rearrange("a b c d -> (a b) (c d)"),
                        bass.IndirectOffsetOnAxis(ap=idc[:, k * 20 + 16 + s:k * 20 + 17 + s].bitcast(U32), axis=0)).then_inc(kv_in[par], 16)

            for k in range(BT4):
                gather(0, k)
            with pool.Fori(1, NT) as t:
                for k in range(BT4):
                    gather(t, k)

        @block.tensor
        def _(pe):
            def tp(o, i, rows=P):
                return nc.tensor.transpose(o, i, cst[0:rows, C_ID:C_ID + rows])

            def mm(o, l, r, start, stop):
                return nc.tensor.matmul(o, l, r, start=start, stop=stop)

            def slot_jobs(par, n, landed, small_slot=False):
                pe.wait_ge(slot_in[par], landed)
                for j in range(4):
                    if not isinstance(n, int) or n >= 1:
                        pe.wait_ge((tp_act, tp_dve)[j % 2], n * 2 - 1 + j // 2)
                    for k in range(2 if small_slot else 4):
                        rows = E0 + E1 if small_slot and k else P
                        last = tp(bank(j, rows, k * P), raw(par, k, j, rows), rows)
                    last.then_inc(tp_done, 1)

            pe.wait_ge(cst_in, 32)
            pe.wait_ge(par_in, 64)
            pe.wait_ge(par_t, 1)
            i16 = cst[0:16, C_ID:C_ID + 16]
            for c, src in enumerate((v(A_, 256, [1, P], rows=16), v(A_, 576, [1, P], rows=16), v(A_, 384, [1, P], rows=16),
                                     v(A_, 0, [2, P], rows=16), v(A_, 1, [2, P], rows=16))):
                last = nc.tensor.transpose(bank(7, 16, 16 * c), src, i16)
            last.then_inc(par_c, 1)

            pe.wait_ge(x_in, 16)
            for t in range(NT):
                q = t % 2
                if t >= 2:
                    pe.wait_ge(xf_cp, t - 1)
                for j in range(NJ):
                    last = tp(bank(q, P, j * P), v(A_, A_X + t * HID + j * P, [1, P]))
                last.then_inc(xf_done, 1)
                pe.wait_ge(xrev_ok, t + 1)
                if t >= 2:
                    pe.wait_ge(xr_cp, t - 1)
                for j in range(NJ):
                    last = tp(bank(2 + q, P, j * P), v(M_, M_Y + t * HID + j * P, [1, P]))
                last.then_inc(xt_done, 1)

            pe.wait_ge(taps_in, 1)
            for g in range(2):
                for hh in range(16):
                    o = bank(5 + g, KR, hh * KR, rows=KQ)
                    for c in range(2):
                        last = mm(o, v(A_, A_SR + c * 256 + hh * KQ, [1, KQ], p0=64 * g, rows=64),
                                  v(A_, A_EM + c * 768 + hh * NX, [1, KR], p0=64 * g, rows=64), c == 0, c == 1)
            last.then_inc(taps_ps, 1)

            pe.wait_ge(xf_cp, NT)
            pe.wait_ge(xr_cp, NT)
            slot_jobs(0, 0, 64, small_slot=True)
            for n, landed in ((1, 16), (2, 192), (3, 144), (4, 208), (5, 160), (6, 224), (7, 176)):
                slot_jobs(n % 2, n, landed)
            with pe.Fori(0, 4) as i:
                slot_jobs(0, i * 2 + 8, i * 16 + 240)
                slot_jobs(1, i * 2 + 9, i * 16 + 192)

            for h in range(S):
                g, q = h // 4, h % 4
                if q == 0:
                    if g == 0:
                        pe.wait_ge(taps_sb, 1)
                    if g >= 4:
                        pe.wait_ge(conv_cp, g - 3)
                if h % 8 == 0:
                    pe.wait_ge(hank_in[h // 8], 16)
                for d in range(NJ):
                    last = mm(bank(4 + g % 4, (NJ - d) * B, q * P + d * B),
                              v(A_, h * 512 + d * P, [1, P]),
                              v(M_, M_U + h * B, [TOK, NJ - d], [1, B]), d == 0, d == NJ - 1)
                if q == 3:
                    last.then_inc(conv_done, 1)

            pe.wait_ge(conv_cp, 8)
            for t in range(NT):
                for j in range(NJ):
                    last = mm(bank(4, E0, t * E0), v(M_, M_Y + j * TOK + t * P, [1, P]),
                              v(small, j * 152 + P, [1, E0]), j == 0, j == NJ - 1)
            last.then_inc(lg_done, 1)
            for half in range(2):
                for j in range(NJ):
                    last = mm(bank(5 + half), v(small, j * 152, [1, P]),
                              v(M_, M_Y + j * TOK + half * 512, [1, 512]), j == 0, j == NJ - 1)
                last.then_inc(rh_done, 1)

            def weights_to_experts(n, e):
                pe.wait_ge(cw_ok, n + 1)
                for t in range(NT):
                    last = tp(bank(2 + t // 4, P, (t % 4) * P, rows=e), v(A_, A_SM + 14 * P + t * e, [1, e]))
                last.then_inc(ct_done, 1)

            pe.wait_ge(tp_act, 32)
            pe.wait_ge(tp_dve, 32)
            weights_to_experts(0, E0)
            pe.wait_ge(ct_cp, 1)
            for half in range(2):
                for a in range(E0 // 2):
                    n = half * 8 + a
                    if n >= 2:
                        pe.wait_ge(z_ok, n - 1)
                    mm(bank(2 + n % 2), v(cst, C_S0 + a * P, [1, P], rows=E0),
                       v(A_, A_CT + half * 512, [1, 512], rows=E0), True, True).then_inc(bc_done, 1)
            for half in range(2):
                pe.wait_ge(z_ok, half * 8 + 8)
                for j in range(NJ):
                    n = half * 4 + j
                    if n == 0:
                        pe.wait_ge(rh_cp, 2)
                    if n >= 4:
                        pe.wait_ge(x1_ok, n - 3)
                    o = bank(4 + n % 4)
                    for i in range(NJ):
                        mm(o, v(M_, M_BW + i * 512 + j * P, [1, P]), v(M_, M_Y + i * TOK + half * 512, [1, 512]), i == 0, False)
                    for a in range(E0 // 2):
                        last = mm(o, v(M_, M_BT + a * 512 + j * P, [1, P]),
                                  v(A_ if half else M_, (A_Z1 if half else M_U) + a * 512, [1, 512]), False, a == E0 // 2 - 1)
                    last.then_inc(y_done, 1)

            pe.wait_ge(x1_ok, 8)
            for t in range(NT):
                if t >= 2:
                    pe.wait_ge(r_cp, t - 1)
                for j in range(NJ):
                    last = tp(bank(4 + t % 2, P, j * P), v(x1T, j * TOK + t * P, [1, P]))
                last.then_inc(r_done, 1)

            with pe.Fori(0, 4) as i:
                slot_jobs(0, i * 2 + 16, i * 16 + 304)
                slot_jobs(1, i * 2 + 17, i * 16 + 256)

            pe.wait_ge(tp_act, 48)
            pe.wait_ge(tp_dve, 48)
            pe.wait_ge(r_cp, NT)

            def project_tile(t, par, first):
                pe.wait_ge(xt_ok, t + 1)
                for k in range(12):
                    o = bank(4 + k % 2)
                    if k < 2:
                        if not first:
                            pe.wait_ge(v_cp, t * 2 + k - 1)
                    else:
                        pe.wait_ge(ab_ok, t * 10 + k - 1)
                    for j in range(NJ):
                        if k < 8:
                            w = v(M_, M_WQ + j * 4096 + k * 512, [1, 512])
                        elif k < 10:
                            w = v(M_, M_WK + j * 1024 + (k - 8) * 512, [1, 512])
                        else:
                            w = v(M_, M_WV + j * 1024 + (k - 10) * 512, [1, 512])
                        last = mm(o, v(M_, M_XT + par * 512 + j * P, [1, P]), w, j == 0, j == NJ - 1)
                    last.then_inc(pj_done, 1)
                    if k >= 2:
                        pe.wait_ge(rot_ok, t * 10 + k - 1)
                        if not first or k >= 4:
                            pe.wait_ge(rt_cp, t * 10 + k - 3)
                        for a in range(4):
                            last = tp(bank(6 + k % 2, P, a * P), v(M_, M_RA + (k % 2) * 512 + a * P, [1, P]))
                        last.then_inc(rt_done, 1)

            project_tile(0, 0, True)
            project_tile(1, 1, False)
            with pe.Fori(1, 4) as i:
                project_tile(i * 2, 0, False)
                project_tile(i * 2 + 1, 1, False)

            with pe.Fori(0, 4) as i:
                slot_jobs(0, i * 2 + 24, i * 16 + 368)
                slot_jobs(1, i * 2 + 25, i * 16 + 320)

            pe.wait_ge(tp_act, 64)
            pe.wait_ge(tp_dve, 64)
            pe.wait_ge(rt_cp, NT * 10)
            pe.wait_ge(pz_ok, 1)

            def attend_tile(t, first):
                def scores(u):
                    k, h = u // HK, u % HK
                    par = k % 2
                    if h == 0:
                        pe.wait_ge(kv_in[par], t * 640 + 320 * (k // 2 + 1))
                        pe.wait_ge(q_in[par], t * 96 + 48 * (k // 2 + 1))
                    if not first or u >= 2:
                        pe.wait_ge(sm_ok, t * 32 + u - 1)
                    q = v(M_, M_QT + par * HQ * S + h * P, [1, P])
                    mm(bank(2 * (u % 2)), q, v(M_, M_KT + par * KTB + h * S, [256, NPP], [1, S]), True, True)
                    mm(bank(2 * (u % 2) + 1, S), q, v(M_, M_KT + par * KTB + L * HK + h * S, [1, S]), True, True).then_inc(s_done, 1)

                def turn(u):
                    pe.wait_ge(p_ok, t * 32 + u + 1)
                    if not first or u >= 1:
                        pe.wait_ge(pt_cp, t * 32 + u)
                    for c in range(4):
                        tp(bank(4, P, c * P), v(M_, M_S + (u % 2) * KEYS + c * P, [1, P]))
                    tp(bank(5, P, 0, rows=S), v(M_, M_S + (u % 2) * KEYS + L, [1, S])).then_inc(pt_done, 1)

                def values(u):
                    par, h = (u // HK) % 2, u % HK
                    pe.wait_ge(pt_cp, t * 32 + u + 1)
                    if not first or u >= 1:
                        pe.wait_ge(o_cp, t * 32 + u)
                    for c in range(5):
                        last = mm(bank(6, P), v(M_, M_V + par * VB + c * 1024 + h * D, [1, D]),
                                  v(M_, M_P + (u % 2) * 640 + c * P, [1, P]), c == 0, c == 4)
                    last.then_inc(o_done, 1)

                scores(0)
                scores(1)
                for u in range(32):
                    if u + 2 < 32:
                        scores(u + 2)
                    turn(u)
                    if u >= 1:
                        values(u - 1)
                values(31)
                if not first:
                    pe.wait_ge(at_cp, t)
                pe.wait_ge(o_cp, t * 32 + 32)
                for h in range(HQ):
                    last = mm(bank(7), v(M_, M_OT + h * P, [1, P]), v(A_, h * 512, [1, 512]), h == 0, h == HQ - 1)
                last.then_inc(wo_done, 1)
                pe.wait_ge(wo_cp, t + 1)
                for j in range(NJ):
                    last = tp(bank(7, P, j * P), v(M_, M_AT + j * P, [1, P]))
                last.then_inc(at_done, 1)

            attend_tile(0, True)
            with pe.Fori(1, NT) as t:
                attend_tile(t, False)

            slot_jobs(0, 32, 432)
            slot_jobs(1, 33, 496)
            pe.wait_ge(at_cp, NT)
            for t in range(NT):
                for j in range(NJ):
                    last = mm(bank(4, E1, t * E1), v(x1T, j * TOK + t * P, [1, P]),
                              v(small, j * 152 + P + E0, [1, E1]), j == 0, j == NJ - 1)
            last.then_inc(lg_done, 1)
            pe.wait_ge(tp_act, 68)
            pe.wait_ge(tp_dve, 68)
            weights_to_experts(1, E1)
            pe.wait_ge(ct_cp, 2)
            for half in range(2):
                for a in range(E1 // 2):
                    n = half * 4 + a
                    if n >= 2:
                        pe.wait_ge(z_ok, 16 + n - 1)
                    for j in range(NJ):
                        last = mm(bank(4 + n % 2), v(A_, j * 512 + a * P, [1, P]),
                                  v(x1T, j * TOK + half * 512, [1, 512]), j == 0, j == NJ - 1)
                    last.then_inc(ha_done, 1)
                    mm(bank(2 + n % 2), v(cst, C_S0 + a * P, [1, P], rows=E1),
                       v(A_, A_CT + half * 512, [1, 512], rows=E1), True, True).then_inc(bc_done, 1)
            for t in range(NT):
                half = t // 4
                pe.wait_ge(z_ok, 16 + half * 4 + 4)
                if t >= 2:
                    pe.wait_ge(ob_cp, t - 1)
                for a in range(E1 // 2):
                    last = mm(bank(6 + t % 2), v(M_, M_V + half * 2048 + a * 512 + (t % 4) * P, [1, P]),
                              v(A_, 2048 + a * 512, [1, 512]), a == 0, a == E1 // 2 - 1)
                last.then_inc(ob_done, 1)

        @block.scalar
        def _(act):
            def copy(o, i):
                return nc.scalar.activation(o, i, ACT.Copy)

            for t in range(NT):
                act.wait_ge(xf_done, t + 1)
                copy(v(x1T, t * P, [TOK, NJ], [1, P]), v(PS, (t % 2) * 512, [P, NJ], [1, P])).then_inc(xf_cp, 1)
            act.wait_ge(exp_arg, 1)
            nc.scalar.activation(v(A_, A_BIG + 4 * 768, [1, 768]), v(A_, A_BIG + 4 * 768, [1, 768]), ACT.Exp).then_inc(exp_ok, 1)
            act.wait_ge(sin_arg, 1)
            nc.scalar.activation(v(A_, A_BIG + 768, [1, 768]), v(A_, A_BIG + 3 * 768, [1, 768]), ACT.Sin).then_inc(sin_ok, 1)
            nc.scalar.activation(v(A_, A_BIG + 2 * 768, [1, 768]), v(A_, A_BIG + 3 * 768, [1, 768]), ACT.Sin, scale=0.5).then_inc(sin_ok, 1)
            act.wait_ge(taps_ps, 1)
            copy(v(A_, A_KQ, [1, S * KR], rows=KQ), v(PS, 5 * 512, [1, S * KR], rows=KQ)).then_inc(taps_cp, 1)

            def even_jobs(n, dst):
                for j in (0, 2):
                    act.wait_ge(tp_done, n * 4 + j + 1)
                    copy(*dst(j)).then_inc(tp_act, 1)

            even_jobs(0, lambda j: (dst_small(j), bank(j, 152)))
            even_jobs(1, lambda j: (wide(M_, M_BW + j * 512), bank(j)))
            for i in range(2):
                even_jobs(2 + i, lambda j: (wide(M_, M_BT + (4 * i + j) * 512), bank(j)))
            for i in range(2):
                even_jobs(4 + i, lambda j: (wide(M_, M_WK + j * 1024 + i * 512), bank(j)))
            for i in range(2):
                even_jobs(6 + i, lambda j: (wide(M_, M_WV + j * 1024 + i * 512), bank(j)))

            def stage_keys(i):
                if not isinstance(i, int):
                    act.wait_ge(kst_out, i * 16)
                for half in range(2):
                    even_jobs(i * 2 + 8 + half, lambda j: (
                        v(M_, M_Y + (4 * half + j) * S, [256, 16], [1, S]), v(PS, j * 512, [S, 16], [1, S])))

            stage_keys(0)
            with act.Fori(1, 4) as i:
                stage_keys(i)

            def exp_logits(n, e):
                act.wait_ge(lx_ok, n + 1)
                nc.scalar.activation(v(A_, A_SM + P, [1, NT * e]), v(A_, A_SM, [1, NT * e]), ACT.Exp).then_inc(le_ok, 1)

            for half in range(2):
                act.wait_ge(rh_done, half + 1)
                copy(wide(A_, A_RH + half * 512), bank(5 + half)).then_inc(rh_cp, 1)
            exp_logits(0, E0)
            for t in range(NT):
                act.wait_ge(r_done, t + 1)
                copy(wide(M_, M_U + t * HID), bank(4 + t % 2)).then_inc(r_cp, 1)
            act.wait_ge(rope_arg, 1)
            nc.scalar.activation(wide(A_, A_RP + 1024), wide(A_, A_RP), ACT.Sin).then_inc(rope_sin, 1)
            nc.scalar.activation(wide(A_, A_RP + 1536), wide(A_, A_RP), ACT.Sin, scale=0.5).then_inc(rope_sin, 1)
            act.wait_ge(x1_out, 16)
            with act.Fori(0, 4) as i:
                for par in range(2):
                    even_jobs(i * 2 + 16 + par, lambda j: (wide(M_, i * 1024 + (M_WQ + j * 4096 + par * 512)), bank(j)))

            def norm_tile(t, par):
                first = isinstance(t, int)
                if not first or t >= 2:
                    act.wait_ge(st_out[par], (t * 24 if par == 0 else t * 24 - 24))
                for k in range(12):
                    g = k % 2
                    act.wait_ge(pj_done, t * 12 + k + 1)
                    if k < 10:
                        if not first or t * 10 + k >= 2:
                            act.wait_ge(ms_ok, t * 10 + k - 1)
                        nc.scalar.activation(wide(M_, M_SQ + g * 512), bank(4 + g), ACT.Square).then_inc(sq_ok, 1)
                    else:
                        copy(wide(A_, A_SV + par * 1024 + (k - 10) * 512), bank(4 + g)).then_inc(v_cp, 1)
                    if k >= 2:
                        act.wait_ge(rt_done, t * 10 + k - 1)
                        if k - 2 < 8:
                            o = v(A_, A_SQ + par * 4096 + (k - 2) * 4 * S, [HQ * S, 4], [S, 4], [1, S])
                        else:
                            o = v(A_, A_SK + par * 1024 + (k - 10) * 4 * S, [HK * S, 4], [S, 4], [1, S])
                        copy(o, v(PS, (6 + g) * 512, [S, 4], [P, 4], [1, S])).then_inc(rt_cp, 1)
                    if k < 10:
                        act.wait_ge(ms_ok, t * 10 + k + 1)
                        nc.scalar.activation(stat[:, 32 + g * 4:36 + g * 4], stat[:, g * 4:g * 4 + 4], ACT.Sqrt).then_inc(sd_ok, 1)

            norm_tile(0, 0)
            norm_tile(1, 1)
            with act.Fori(1, 4) as i:
                norm_tile(i * 2, 0)
                norm_tile(i * 2 + 1, 1)

            for par in range(2):
                act.wait_ge(st_out[par], 48 * 4)
            with act.Fori(0, 4) as i:
                for par in range(2):
                    even_jobs(i * 2 + 24 + par, lambda j: (wide(A_, i * 4096 + (par * 2048 + j * 512)), bank(j)))

            def attend_tile(t):
                first = isinstance(t, int)

                def expo(u):
                    g = u % 2
                    act.wait_ge(nm_ok, t * 32 + u + 1)
                    s = v(M_, M_S + g * KEYS, [1, KEYS])
                    nc.scalar.activation(s, s, ACT.Exp, bias=stat[:, 4 + g:5 + g], accum_out=stat[:, 8 + g:9 + g]).then_inc(e_ok, 1)

                def turned(u):
                    act.wait_ge(pt_done, t * 32 + u + 1)
                    if not first or u >= 2:
                        act.wait_ge(o_done, t * 32 + u - 1)
                    copy(v(M_, M_P + (u % 2) * 640, [1, 640]), v(PS, 4 * 512, [1, 640])).then_inc(pt_cp, 1)

                expo(0)
                for u in range(32):
                    if u + 1 < 32:
                        expo(u + 1)
                    turned(u)
                act.wait_ge(wo_done, t + 1)
                if not first:
                    act.wait_ge(at_done, t)
                copy(wide(M_, M_AT), bank(7)).then_inc(wo_cp, 1)

            attend_tile(0)
            with act.Fori(1, NT) as t:
                attend_tile(t)

            act.wait_ge(wo_done, NT)
            even_jobs(32, lambda j: (wide(A_, j * 512), bank(j)))
            even_jobs(33, lambda j: (wide(A_, 2048 + j * 512), bank(j)))
            exp_logits(1, E1)
            for n in range(8):
                act.wait_ge(ha_done, n + 1)
                if n >= 2:
                    act.wait_ge(z_ok, 16 + n - 1)
                copy(wide(A_, A_RH + (n % 2) * 512), bank(4 + n % 2)).then_inc(ha_cp, 1)

        @block.vector
        def _(dve):
            steps = [0]
            ve = nc.vector

            def link(ins):
                steps[0] += 1
                ins.then_inc(chain, 1)
                dve.wait_ge(chain, steps[0])

            def stt(o, a, s, b, op0, op1):
                return ve.scalar_tensor_tensor(out=o, in0=a, scalar=s, in1=b, op0=op0, op1=op1)

            def tt(o, a, b, op):
                return ve.tensor_tensor(o, a, b, op)

            def ts(o, a, s1, op0, s2=None, op1=None):
                return ve.tensor_scalar(o, a, s1, s2, op0, op1) if op1 is not None else ve.tensor_scalar(o, a, s1, None, op0)

            def exp_exact(dst, src, n, t0):
                y, k, r, q, p2 = (v(A_, A_T + t0 + 32 * a, [1, n]) for a in range(5))
                link(ts(y, src, 1.4426950408889634, ALU.mult, MAGIC, ALU.add))
                link(ts(k, y, MAGIC, ALU.subtract, -126.0, ALU.max))
                link(stt(r, k, -LN2_HI, src, ALU.mult, ALU.add))
                link(stt(r, k, -LN2_LO, r, ALU.mult, ALU.add))
                link(ts(q, r, 1.0 / 5040, ALU.mult))
                for c in (1.0 / 720, 1.0 / 120, 1.0 / 24, 1.0 / 6, 0.5, 1.0):
                    link(stt(q, q, c, r, ALU.add, ALU.mult))
                link(ts(v(A_, A_T + t0 + 32 * 4, [1, n]).bitcast(I32), k, 127.0, ALU.add, float(2 ** 23), ALU.mult))
                link(stt(dst, q, 1.0, p2, ALU.add, ALU.mult))

            def reduce_phase(ph, y, r, done):
                link(ts(y, ph, INV_TWO_PI, ALU.mult, MAGIC, ALU.add))
                link(ts(y, y, MAGIC, ALU.subtract))
                link(stt(r, y, -TWO_PI_HI, ph, ALU.mult, ALU.add))
                link(stt(r, y, -TWO_PI_LO, r, ALU.mult, ALU.add))
                ts(r, r, PI_F, ALU.min, -PI_F, ALU.max).then_inc(done, 1)

            dve.wait_ge(par_in, 64)
            ve.tensor_copy(v(A_, 576, [NSTATE, 2], [1, NSTATE], rows=16), v(A_, 512, [1, 2], [0, NSTATE], rows=16)).then_inc(par_t, 1)

            tf = tabi[:, :].bitcast(F32)

            def mk(offset, *dims):
                return bass.AP(tf.tensor, offset, [[tf.ap[0][0], P], *[list(d) for d in dims]])

            dve.wait_ge(len_in, 16)
            dve.wait_ge(cst_in, 32)
            link(ve.tensor_copy(lenf[:, :], leni[:, :]))
            for j in range(NJ):
                link(ts(maskf[:, j * B:(j + 1) * B], lenf[:, :], cst[:, C_F + j:C_F + j + 1], ALU.is_gt))
                link(ts(maskr[:, j * B:(j + 1) * B], lenf[:, :], cst[:, C_FR + j:C_FR + j + 1], ALU.is_gt))

            for t in range(NT):
                dve.wait_ge(xt_done, t + 1)
                for j in range(NJ):
                    last = tt(v(M_, M_U + j * TOK + t * BT4, [1, BT4], [B, S]), v(PS, (2 + t % 2) * 512 + j * P, [S, BT4], [1, S]),
                              mk(NJ * B + j * B + t * BT4, [1, BT4], [0, S]), ALU.mult)
                last.then_inc(xr_cp, 1)

            dve.wait_ge(par_c, 1)
            pc = lambda c, n=16: v(A_, A_PC + 16 * c, [1, n])
            tmp = lambda a, n=16: v(A_, A_T + 32 * a, [1, n])
            big = lambda a: v(A_, A_BIG + 768 * a, [1, 768])
            big3 = lambda a: v(A_, A_BIG + 768 * a, [NX, 16], [1, NX])
            link(ve.tensor_copy(pc(0, 80), bank(7, 80)))
            exp_exact(tmp(5, 32), pc(0, 32), 32, 0)
            ar, dt, zr, zi = tmp(5), v(A_, A_T + 32 * 5 + 16, [1, 16]), tmp(6), tmp(7)
            link(ts(ar, ar, -1.0, ALU.mult))
            link(tt(zr, ar, dt, ALU.mult))
            link(tt(zi, pc(2), dt, ALU.mult))
            over = lambda a: v(A_, A_T + 32 * a, [1, 16], [0, NX])
            steps3 = v(cst, C_M, [0, 16], [1, NX])
            tt(big3(4), over(6), steps3, ALU.mult).then_inc(exp_arg, 1)
            link(tt(big3(0), over(7), steps3, ALU.mult))
            reduce_phase(big(0), big(1), big(3), sin_arg)
            exp_exact(tmp(9), zr, 16, 0)
            dve.wait_ge(sin_ok, 2)
            s1 = v(A_, A_BIG + 768 + 1, [NX, 16])
            h1 = v(A_, A_BIG + 2 * 768 + 1, [NX, 16])
            link(tt(tmp(10), h1, h1, ALU.mult))
            link(tt(tmp(10), tmp(10), tmp(9), ALU.mult))
            link(ts(tmp(11), tmp(9), 1.0, ALU.subtract))
            link(stt(tmp(10), tmp(10), -2.0, tmp(11), ALU.mult, ALU.add))
            link(tt(tmp(11), s1, tmp(9), ALU.mult))
            link(tt(tmp(12), pc(3), tmp(10), ALU.mult))
            link(tt(tmp(13), pc(4), tmp(11), ALU.mult))
            link(tt(tmp(12), tmp(12), tmp(13), ALU.subtract))
            link(tt(tmp(13), pc(3), tmp(11), ALU.mult))
            link(tt(tmp(14), pc(4), tmp(10), ALU.mult))
            link(tt(tmp(13), tmp(13), tmp(14), ALU.add))
            link(tt(tmp(14), ar, ar, ALU.mult))
            link(tt(tmp(15), pc(2), pc(2), ALU.mult))
            link(tt(tmp(14), tmp(14), tmp(15), ALU.add))
            link(ve.reciprocal(tmp(14), tmp(14)))
            link(ts(tmp(14), tmp(14), 2.0, ALU.mult))
            link(tt(tmp(15), tmp(12), ar, ALU.mult))
            link(tt(tmp(16), tmp(13), pc(2), ALU.mult))
            link(tt(tmp(15), tmp(15), tmp(16), ALU.add))
            link(tt(tmp(15), tmp(15), tmp(14), ALU.mult))
            link(tt(tmp(16), tmp(12), pc(2), ALU.mult))
            link(tt(tmp(17), tmp(13), ar, ALU.mult))
            link(tt(tmp(16), tmp(16), tmp(17), ALU.subtract))
            link(tt(tmp(16), tmp(16), tmp(14), ALU.mult))
            link(tt(big(2), big(2), big(2), ALU.mult))
            link(ts(big(2), big(2), -2.0, ALU.mult, 1.0, ALU.add))
            dve.wait_ge(exp_ok, 1)
            link(tt(big(5), big(2), big(4), ALU.mult))
            link(stt(big(6), big(1), -1.0, big(4), ALU.mult, ALU.mult))
            qre = v(A_, A_BIG + 5 * 768 + KR, [NX, 16], [1, KQ])
            qni = v(A_, A_BIG + 6 * 768 + KR, [NX, 16], [1, KQ])
            sre, sni = (v(A_, A_T + 32 * a, [1, 16], [0, KQ]) for a in (15, 16))
            w0, w1 = v(A_, A_BIG, [KQ, 16], [1, KQ]), v(A_, A_BIG + 256, [KQ, 16], [1, KQ])
            fre, fni = v(A_, A_SR, [KQ, 16], [1, KQ]), v(A_, A_SR + 256, [KQ, 16], [1, KQ])
            link(tt(w0, qre, sre, ALU.mult))
            link(tt(w1, qni, sni, ALU.mult))
            link(tt(fre, w0, w1, ALU.subtract))
            link(tt(w0, qni, sre, ALU.mult))
            link(tt(w1, qre, sni, ALU.mult))
            link(tt(w0, w0, w1, ALU.add))
            ts(fni, w0, -1.0, ALU.mult).then_inc(taps_in, 1)
            dve.wait_ge(taps_cp, 1)
            dve.wait_ge(d_in, 16)
            k0 = v(A_, A_KQ, [KR, S], rows=1)
            tt(k0, k0, v(stat, 0, [1, S], rows=1), ALU.add).then_inc(taps_sb, 1)

            def odd_jobs(n, dst):
                for j in (1, 3):
                    dve.wait_ge(tp_done, n * 4 + j + 1)
                    ve.tensor_copy(*dst(j)).then_inc(tp_dve, 1)

            odd_jobs(0, lambda j: (dst_small(j), bank(j, 152)))
            odd_jobs(1, lambda j: (wide(M_, M_BW + j * 512), bank(j)))
            for i in range(2):
                odd_jobs(2 + i, lambda j: (wide(M_, M_BT + (4 * i + j) * 512), bank(j)))
            for i in range(2):
                odd_jobs(4 + i, lambda j: (wide(M_, M_WK + j * 1024 + i * 512), bank(j)))
            for i in range(2):
                odd_jobs(6 + i, lambda j: (wide(M_, M_WV + j * 1024 + i * 512), bank(j)))

            def stage_keys(i):
                if not isinstance(i, int):
                    dve.wait_ge(kst_out, i * 16)
                for half in range(2):
                    odd_jobs(i * 2 + 8 + half, lambda j: (
                        v(M_, M_Y + (4 * half + j) * S, [256, 16], [1, S]), v(PS, j * 512, [S, 16], [1, S])))

            stage_keys(0)
            with dve.Fori(1, 4) as i:
                stage_keys(i)

            dve.wait_ge(kst_out, 64)
            for g in range(8):
                dve.wait_ge(conv_done, g + 1)
                for q in range(4):
                    last = tt(v(M_, M_Y + g * 4 + q, [TOK, NJ], [S, B]), v(PS, (4 + g % 4) * 512 + q * P, [B, NJ], [1, B]),
                              mk(0, [B, NJ], [1, B]), ALU.mult)
                last.then_inc(conv_cp, 1)

            def route(n, e, eps, scale):
                a3 = lambda i: v(A_, A_SM + P * i, [e, NT], [1, e])
                c1 = lambda i: v(A_, A_SM + P * i, [1, NT])
                cb = lambda i: v(A_, A_SM + P * i, [1, NT], [0, e])
                num = v(cst, C_M, [0, NT], [1, e])
                dve.wait_ge(lg_done, n + 1)
                lg = v(PS, 4 * 512, [e, NT], [1, e])
                link(ve.tensor_reduce(c1(2), lg, AX_X, ALU.max))
                tt(a3(0), lg, cb(2), ALU.subtract).then_inc(lx_ok, 1)
                dve.wait_ge(le_ok, n + 1)
                link(ve.tensor_reduce(c1(3), a3(1), AX_X, ALU.add))
                link(ve.reciprocal(c1(3), c1(3)))
                link(tt(a3(4), a3(1), cb(3), ALU.mult))
                link(ve.tensor_reduce(c1(5), a3(4), AX_X, ALU.max))
                link(tt(a3(6), a3(4), cb(5), ALU.is_equal))
                link(stt(a3(6), a3(6), -64.0, num, ALU.mult, ALU.add))
                link(ve.tensor_reduce(c1(7), a3(6), AX_X, ALU.min))
                link(tt(a3(8), a3(6), cb(7), ALU.is_equal))
                link(stt(a3(9), a3(8), -2.0, a3(4), ALU.mult, ALU.add))
                link(ve.tensor_reduce(c1(10), a3(9), AX_X, ALU.max))
                link(tt(a3(11), a3(9), cb(10), ALU.is_equal))
                link(stt(a3(11), a3(11), -64.0, num, ALU.mult, ALU.add))
                link(ve.tensor_reduce(c1(12), a3(11), AX_X, ALU.min))
                link(tt(a3(11), a3(11), cb(12), ALU.is_equal))
                link(tt(a3(8), a3(8), a3(11), ALU.add))
                link(stt(c1(13), c1(5), eps, c1(10), ALU.add, ALU.add))
                link(ve.reciprocal(c1(13), c1(13)))
                link(stt(a3(8), a3(8), scale, a3(4), ALU.mult, ALU.mult))
                tt(a3(14), a3(8), cb(13), ALU.mult).then_inc(cw_ok, 1)
                dve.wait_ge(ct_done, n + 1)
                ve.tensor_copy(v(A_, A_CT, [1, TOK], rows=e), v(PS, 2 * 512, [1, TOK], rows=e)).then_inc(ct_cp, 1)

            route(0, E0, 1e-6, 0.5)
            dve.wait_ge(rh_cp, 2)
            for half in range(2):
                for a in range(E0 // 2):
                    n = half * 8 + a
                    dve.wait_ge(bc_done, n + 1)
                    tt(wide(A_ if half else M_, (A_Z1 if half else M_U) + a * 512), bank(2 + n % 2),
                       wide(A_, A_RH + half * 512), ALU.mult).then_inc(z_ok, 1)
            for half in range(2):
                for j in range(NJ):
                    n = half * 4 + j
                    dve.wait_ge(y_done, n + 1)
                    o = wide(x1T, j * TOK + half * 512)
                    stt(o, bank(4 + n % 4), biasc[:, j:j + 1], o, ALU.add, ALU.add).then_inc(x1_ok, 1)

            dve.wait_ge(seq_in, 16)
            dve.wait_ge(tab_in, 16)
            dve.wait_ge(pad_out, 16)
            for q in range(4):
                r = dict(p0=S * q, rows=S)
                link(ts(v(idxv, 0, [1, B * 4], **r), v(tabi, q, [4, B * 4], **r), float(PSIZE), ALU.mult, v(cst, C_S, [1, 1], **r), ALU.add))
                link(ve.tensor_copy(v(stat, 40, [1, NT], **r), v(seqi, q, [4, NT], **r)))
            ts(tabi[:, :], tabi[:, :], float(P), ALU.mult, cst[:, C_P:C_P + 1], ALU.add).then_inc(idx_ok, 1)
            link(ts(stat[:, 40:40 + NT], stat[:, 40:40 + NT], cst[:, C_S:C_S + 1], ALU.add))
            link(ve.tensor_copy(seqf[:, :], seqi[:, :]))
            dve.wait_ge(y_done, 8)
            rp = lambda a: v(A_, A_RP + a * 512, [64, NT], [1, 64])
            rw = lambda a: wide(A_, A_RP + a * 512)
            link(tt(rp(4), v(stat, 40, [1, NT], [0, 64]), v(cst, C_IF, [0, NT], [1, 64]), ALU.mult))
            reduce_phase(rw(4), rw(1), rw(0), rope_arg)
            dve.wait_ge(nw_in, 32)
            wq, wk = A_RP + 5 * 512, A_RP + 5 * 512 + D
            link(ts(v(A_, wq, [1, D]), v(A_, wq, [1, D]), SCALE, ALU.mult))
            dve.wait_ge(rope_sin, 2)
            link(tt(rw(3), rw(3), rw(3), ALU.mult))
            link(ts(rw(3), rw(3), -2.0, ALU.mult, 1.0, ALU.add))
            link(ts(rw(4), rw(2), -1.0, ALU.mult))
            for c, w in enumerate((wq, wk)):
                wl, wh = (v(A_, w + 64 * a, [0, NT], [1, 64]) for a in range(2))
                to = lambda a: v(A_, A_TB + c * 256 + a * 64, [512, NT], [1, 64])
                link(tt(to(0), rp(3), wl, ALU.mult))
                link(tt(to(1), rp(3), wh, ALU.mult))
                link(tt(to(2), rp(4), wh, ALU.mult))
                link(tt(to(3), rp(2), wl, ALU.mult))

            dve.wait_ge(x1_out, 16)
            with dve.Fori(0, 4) as i:
                for par in range(2):
                    odd_jobs(i * 2 + 16 + par, lambda j: (wide(M_, i * 1024 + (M_WQ + j * 4096 + par * 512)), bank(j)))

            def norm_tile(t):
                def squares(k):
                    g = k % 2
                    s = stat[:, g * 4:g * 4 + 4]
                    dve.wait_ge(sq_ok, t * 10 + k + 1)
                    ve.tensor_reduce(s, v(M_, M_SQ + g * 512, [P, 4], [1, P]), AX_X, ALU.add).then_inc(ss_ok, 1)
                    dve.wait_ge(ss_ok, t * 10 + k + 1)
                    ts(s, s, 1.0 / D, ALU.mult, EPS, ALU.add).then_inc(ms_ok, 1)

                def rotate(k):
                    g = k % 2
                    ms, sd = stat[:, g * 4:g * 4 + 4], stat[:, 32 + g * 4:36 + g * 4]
                    y, z = stat[:, 16 + 8 * g:20 + 8 * g], stat[:, 20 + 8 * g:24 + 8 * g]
                    if not isinstance(t, int) or k >= 2:
                        dve.wait_ge(ab_ok, t * 10 + k - 1)
                    dve.wait_ge(sd_ok, t * 10 + k + 1)
                    ve.reciprocal(y, sd).then_inc(nw_ok, 1)
                    dve.wait_ge(nw_ok, t * 40 + 4 * k + 1)
                    tt(z, y, y, ALU.mult).then_inc(nw_ok, 1)
                    dve.wait_ge(nw_ok, t * 40 + 4 * k + 2)
                    stt(z, z, -0.5, ms, ALU.mult, ALU.mult).then_inc(nw_ok, 1)
                    dve.wait_ge(nw_ok, t * 40 + 4 * k + 3)
                    stt(y, z, 1.5, y, ALU.add, ALU.mult).then_inc(nw_ok, 1)
                    dve.wait_ge(nw_ok, t * 40 + 4 * k + 4)
                    if not isinstance(t, int) or k >= 2:
                        dve.wait_ge(rt_done, t * 10 + k - 1)
                    tb = A_TB + (256 if k >= 8 else 0)
                    for a in range(4):
                        r = stat[:, 16 + 8 * g + a:17 + 8 * g + a]
                        stt(v(M_, M_RA + g * 512 + a * P, [1, P]), bank(4 + g, P, a * P), r,
                            v(A_, t * 512 + tb, [1, P]), ALU.mult, ALU.mult)
                        last = stt(v(M_, M_RB + g * 512 + a * P, [64, 2], [1, 64]), v(PS, (4 + g) * 512 + a * P + 64, [-64, 2], [1, 64]), r,
                                   v(A_, t * 512 + (tb + P), [64, 2], [1, 64]), ALU.mult, ALU.mult)
                    last.then_inc(ab_ok, 1)

                for k in range(10):
                    squares(k)
                    if k >= 1:
                        rotate(k - 1)
                rotate(9)

            norm_tile(0)
            with dve.Fori(1, NT) as t:
                norm_tile(t)

            for par in range(2):
                dve.wait_ge(st_out[par], 48 * 4)
            with dve.Fori(0, 4) as i:
                for par in range(2):
                    odd_jobs(i * 2 + 24 + par, lambda j: (wide(A_, i * 4096 + (par * 2048 + j * 512)), bank(j)))

            dve.wait_ge(rt_cp, NT * 10)
            dve.wait_ge(v_cp, NT * 2)
            ve.memset(bank(5, P), 0.0).then_inc(pz_ok, 1)
            dve.wait_ge(tp_done, 128)

            def attend_tile(t):
                first = isinstance(t, int)
                ve.tensor_copy(seqc[:, :], v(seqf, t * BT4, [1, BT4])).then_inc(seqc_ok, 1)
                dve.wait_ge(seqc_ok, t + 1)
                mrow = v(M_, M_MR, [1, KEYS])

                def mask_max(u):
                    g, k = u % 2, u // HK
                    if u % HK == 0:
                        ts(mrow, v(cst, C_POS, [1, KEYS]), seqc[:, k:k + 1], ALU.is_ge, NEG, ALU.mult).then_inc(mrow_ok, 1)
                        dve.wait_ge(mrow_ok, t * BT4 + k + 1)
                    dve.wait_ge(s_done, t * 32 + u + 1)
                    if not first or u >= 2:
                        dve.wait_ge(pt_done, t * 32 + u - 1)
                    ve.memset(stat[:, 60:61], 0.0)
                    ve.tensor_tensor_reduce(v(M_, M_S + g * KEYS, [1, KEYS]), v(PS, g * 1024, [1, KEYS]), mrow, 1.0, -3.0e38,
                                            ALU.add, ALU.max, stat[:, g:g + 1]).then_inc(sm_ok, 1)
                    dve.wait_ge(sm_ok, t * 32 + u + 1)
                    ts(stat[:, 4 + g:5 + g], stat[:, g:g + 1], -1.0, ALU.mult).then_inc(nm_ok, 1)

                def normalise(u):
                    g = u % 2
                    dve.wait_ge(e_ok, t * 32 + u + 1)
                    ve.reciprocal(stat[:, 12 + g:13 + g], stat[:, 8 + g:9 + g]).then_inc(rs_ok, 1)
                    dve.wait_ge(rs_ok, t * 32 + u + 1)
                    s = v(M_, M_S + g * KEYS, [1, KEYS])
                    ts(s, s, stat[:, 12 + g:13 + g], ALU.mult).then_inc(p_ok, 1)

                def outputs(u):
                    k, h = u // HK, u % HK
                    dve.wait_ge(o_done, t * 32 + u + 1)
                    if u == 0 and not first:
                        dve.wait_ge(wo_done, t)
                    ve.tensor_copy(v(M_, M_OT + h * REP * P + k * S, [P, REP], [1, S]), v(PS, 6 * 512, [S, REP], [1, S])).then_inc(o_cp, 1)

                mask_max(0)
                for u in range(32):
                    if u + 1 < 32:
                        mask_max(u + 1)
                    normalise(u)
                    if u >= 2:
                        outputs(u - 2)
                outputs(30)
                outputs(31)
                dve.wait_ge(at_done, t + 1)
                ve.tensor_copy(v(x1T, t * P, [TOK, NJ], [1, P]), v(PS, 7 * 512, [P, NJ], [1, P])).then_inc(at_cp, 1)

            attend_tile(0)
            with dve.Fori(1, NT) as t:
                attend_tile(t)

            odd_jobs(32, lambda j: (wide(A_, j * 512), bank(j)))
            odd_jobs(33, lambda j: (wide(A_, 2048 + j * 512), bank(j)))
            route(1, E1, 0.0, 1.0)
            for n in range(8):
                half, a = n // 4, n % 4
                dve.wait_ge(bc_done, 16 + n + 1)
                dve.wait_ge(ha_cp, n + 1)
                tt(wide(M_, M_V + half * 2048 + a * 512), bank(2 + n % 2), wide(A_, A_RH + (n % 2) * 512), ALU.mult).then_inc(z_ok, 1)
            dve.wait_ge(x1_back, 16)
            for t in range(NT):
                dve.wait_ge(ob_done, t + 1)
                o = wide(M_, M_KT + t * HID)
                tt(o, bank(6 + t % 2), o, ALU.add).then_inc(ob_cp, 1)


_INS = ['x', 'itok_B_8_3872', 'itok_Bx16_0_63', 'itok_B_207_1644', 'L0_cond_log_dt', 'L0_cond_C', 'L0_cond_log_A_real',
        'L0_cond_A_imag', 'L0_cond_D', 'L0_ffn_base_w', 'L0_ffn_base_b', 'L0_ffn_A', 'L0_ffn_B', 'L0_ffn_router_w',
        'L1_cond_Wq', 'L1_cond_Wk', 'L1_cond_Wv', 'L1_cond_Wo', 'L1_cond_q_norm_w', 'L1_cond_k_norm_w',
        'L1_cond_k_cache', 'L1_cond_v_cache', 'L1_ffn_gate_w', 'L1_ffn_lora_A', 'L1_ffn_lora_B']
SCRATCH_KIND = "Internal"


def kernel(**inputs):
    import concourse.bacc as _bacc
    from concourse.bass_utils import run_bass_kernel_spmd as _run

    nc = _bacc.Bacc("TRN2", target_bir_lowering=False, num_devices=1)
    arrays, args = {}, []
    for name, a in [*((n, inputs[n]) for n in _INS), ("const", constants())]:
        a = np.ascontiguousarray(a)
        arrays[f"in_{name}"] = a
        args.append(nc.dram_tensor(f"in_{name}", a.shape, mybir.dt.from_np(a.dtype), kind="ExternalInput").ap())
    out = nc.dram_tensor("out_0", (B, S, HID), F32, kind="ExternalOutput").ap()

    def scratch(name, shape):
        return nc.dram_tensor(f"scratch_{name}", shape, F32, kind=SCRATCH_KIND).ap()

    adaln_program(nc, *args, out, scratch)
    r = _run(nc, [arrays], core_ids=[0])
    return r.results[0]["out_0"]
```

```python
from contextlib import ExitStack

import numpy as np

import concourse.bass as bass
from concourse import mybir

ALU = mybir.AluOpType
ACT = mybir.ActivationFunctionType
AX_X = mybir.AxisListType.X
F32 = mybir.dt.float32
I32 = mybir.dt.int32
U32 = mybir.dt.uint32

P = 128
B, S, HID = 32, 32, 512
TOK = B * S
NT = TOK // P
NJ = HID // P
BT4 = P // S
NSTATE = 64
E0, R0 = 16, 64
E1, R1 = 8, 64
D, HQ, HK = 128, 32, 8
REP = HQ // HK
PAGES, PSIZE, NPP = 64, 32, 16
L = NPP * PSIZE
KEYS = L + S
KR, KQ = 32, 16
KPAD = 640
SCALE = float(np.float32(1.0 / np.sqrt(D)))
EPS = 1e-6
MAGIC = 12582912.0
TWO_PI_HI = 6.28125
TWO_PI_LO = float(2.0 * np.pi - 6.28125)
INV_TWO_PI = float(1.0 / (2.0 * np.pi))
PI_F = float(np.float32(3.1415925))
LN2_HI = 0.693359375
LN2_LO = float(np.log(2.0) - 0.693359375)
NEG = -1e30

C_ID = 0
C_F = C_ID + P
C_FR = C_F + NJ
C_M = C_FR + NJ
C_S = C_M + KR + KQ
C_P = C_S + 1
C_IF = C_P + 1
C_POS = C_IF + D // 2
C_S0 = C_POS + KEYS
NCONST = C_S0 + (E0 // 2) * P


def constants():
    c = np.zeros((P, NCONST), np.float32)
    p = np.arange(P)
    c[:, C_ID:C_ID + P] = np.eye(P)
    for j in range(NJ):
        c[:, C_F + j] = j * P + p
        c[:, C_FR + j] = j * P + P - 1 - p
    c[:, C_M:C_M + KR] = np.arange(KR)
    c[:, C_M + KR:C_M + KR + KQ] = KR * np.arange(KQ)
    c[:, C_S] = p % S
    c[:, C_P] = p
    half = np.arange(0, D, 2, dtype=np.float32) / np.float32(D)
    c[:, C_IF:C_IF + D // 2] = np.float32(1.0) / np.power(np.float32(10000.0), half)
    c[:, C_POS:C_POS + L] = np.arange(L)
    c[:, C_POS + L:C_POS + KEYS] = -1
    for e in range(E0):
        c[e, C_S0 + e * R0:C_S0 + (e + 1) * R0] = 1
    return c


KB = 256
SLOT = 16 // 2 * KB
M_WK, M_WV = 16 * KB, 32 * KB
M_U, M_Y, M_BW, M_BT = 48 * KB, 64 * KB, 80 * KB, 88 * KB
M_WQ = 48 * KB
M_OT, M_QT, M_KT, M_V = 16 * KB, 32 * KB, 40 * KB, 74 * KB
M_END = 114 * KB


def adaln_program(nc, x, len0, table, seqlens, log_dt, Cc, log_A, A_im, Dskip, base_w, base_b, ffnA, ffnB,
                  router_w, Wq, Wk, Wv, Wo, qnw, knw, k_cache, v_cache, gate_w, lora_A, lora_B, const, out, scratch):
    def dap(t, offset, dims):
        return bass.AP(t.tensor, offset, dims)

    kpad, kT, qT, knT, vn, x1d = (scratch(n, s) for n, s in (
        ("kpad", [S, KPAD]),
        ("kT", [PAGES * P, HK * PSIZE]),
        ("qT", [B, P, HQ * S]),
        ("knT", [B, P, HK * S]),
        ("vn", [B, S, HK * D]),
        ("x1d", [TOK, HID]),
    ))

    with ExitStack() as ctx:
        def sb(name, cols, dt=F32, rows=P):
            return ctx.enter_context(nc.sbuf_tensor(name, [rows, cols], dt))

        def sem(name):
            return ctx.enter_context(nc.semaphore(name))

        cst = sb("cst", NCONST)
        A_ = sb("A_", 64 * KB)
        M_ = sb("M_", M_END)
        x1T = sb("x1T", NJ * TOK)
        small = sb("small", NJ * 152)
        leni = sb("leni", B, I32)
        lenf = sb("lenf", B)
        biasc = sb("biasc", NJ)
        seqi = sb("seqi", B, I32)
        seqf = sb("seqf", B)
        tabi = sb("tabi", B * NPP, I32)
        maskf = tabi[:, 0:NJ * B].bitcast(F32)
        maskr = tabi[:, NJ * B:2 * NJ * B].bitcast(F32)
        idxv = sb("idxv", B * 4, I32)
        idc = sb("idc", BT4 * 20, I32)
        seqc = sb("seqc", BT4)
        stat = sb("stat", 64)
        PS = ctx.enter_context(nc.psum_tensor("PS", [P, 8 * 512], F32))

        def v(t, offset, *dims, p0=0, rows=P, dt=None):
            pitch = t[:, :].ap[0][0]
            return bass.AP(t, p0 * pitch + offset, [[pitch, rows], *[list(d) for d in dims]])

        def bank(k, cols=512, off=0, rows=P):
            return PS[0:rows, k * 512 + off:k * 512 + off + cols]

        ident = cst[:, C_ID:C_ID + P]

        cst_in, len_in, seq_in, tab_in, x_in, par_in, d_in = (sem(n) for n in (
            "cst_in", "len_in", "seq_in", "tab_in", "x_in", "par_in", "d_in"))
        slot_in = [sem("slot_in0"), sem("slot_in1")]
        tp_done = sem("tp_done")
        tp_act, tp_dve = sem("tp_act"), sem("tp_dve")
        kst_out = sem("kst_out")
        chain = sem("chain")
        achain = sem("achain")
        mask_ok, par_t, par_c, exp_arg, exp_ok = (sem(n) for n in ("mask_ok", "par_t", "par_c", "exp_arg", "exp_ok"))
        sin_arg, sin_ok = sem("sin_arg"), sem("sin_ok")
        taps_in, taps_ps, taps_cp, taps_sb, pad_out, taps_out = (sem(n) for n in (
            "taps_in", "taps_ps", "taps_cp", "taps_sb", "pad_out", "taps_out"))
        hank_in = [sem(f"hank_in{i}") for i in range(4)]
        xrev_ok = sem("xrev_ok")
        xf_done, xt_done, xf_cp, xr_cp = sem("xf_done"), sem("xt_done"), sem("xf_cp"), sem("xr_cp")
        conv_done, conv_cp = sem("conv_done"), sem("conv_cp")
        lg_done, cw_ok, ct_done, ct_cp = sem("lg_done"), sem("cw_ok"), sem("ct_done"), sem("ct_cp")
        lx_ok, le_ok = sem("lx_ok"), sem("le_ok")
        rh_done, rh_cp, bc_done, z_ok = sem("rh_done"), sem("rh_cp"), sem("bc_done"), sem("z_ok")
        y_done, x1_ok = sem("y_done"), sem("x1_ok")
        r_done, r_cp, x1_out, x1_back = sem("r_done"), sem("r_cp"), sem("x1_out"), sem("x1_back")
        rope_arg, rope_sin, nw_in = sem("rope_arg"), sem("rope_sin"), sem("nw_in")
        xt_ok, pj_done, sq_ok, ms_ok, sc_ok = (sem(n) for n in ("xt_ok", "pj_done", "sq_ok", "ms_ok", "sc_ok"))
        sd_ok, nw_ok, nf_ok, rs_ok = sem("sd_ok"), sem("nw_ok"), sem("nf_ok"), sem("rs_ok")
        ab_ok, rot_ok, rt_done, rt_cp, v_cp = (sem(n) for n in ("ab_ok", "rot_ok", "rt_done", "rt_cp", "v_cp"))
        st_out = [sem("st_out0"), sem("st_out1")]
        idx_ok = sem("idx_ok")
        k_in, v_in = [sem("k_in0"), sem("k_in1")], [sem("v_in0"), sem("v_in1")]
        q_in, vn_in = [sem("q_in0"), sem("q_in1")], [sem("vn_in0"), sem("vn_in1")]
        idc_ok, mrow_ok, seqc_ok = sem("idc_ok"), sem("mrow_ok"), sem("seqc_ok")
        zero_ok, pz_ok = sem("zero_ok"), sem("pz_ok")
        s_done, sm_ok, nm_ok, e_ok, p_ok = (sem(n) for n in ("s_done", "sm_ok", "nm_ok", "e_ok", "p_ok"))
        pt_done, pt_cp, o_done, o_cp = (sem(n) for n in ("pt_done", "pt_cp", "o_done", "o_cp"))
        wo_done, wo_cp, at_done, at_cp = (sem(n) for n in ("wo_done", "wo_cp", "at_done", "at_cp"))
        ha_done, ha_cp, ob_done, ob_cp, out_done = (sem(n) for n in ("ha_done", "ha_cp", "ob_done", "ob_cp", "out_done"))

        def raw(par, k, j, rows=P):
            return v(M_, par * SLOT + k * 512 + j * P, [1, P], rows=rows)

        def slot_all(par):
            return v(M_, par * SLOT, [512, 4], [1, 512])

        def rows_of(w, first):
            return dap(w, first * 512, [[512, P], [P * 512, 4], [1, 512]])

        def dst_small(j):
            return small[:, j * 152:(j + 1) * 152]

        def wide(t, offset):
            return v(t, offset, [1, 512])

        A_PC, A_T, A_BIG = 1024, 1280, 2048
        A_EM = A_BIG + 5 * 768
        A_SR = A_BIG + 7 * 768
        A_X = 32 * KB
        A_KQ = 60 * KB
        NX = KR + KQ

        A_Z1, A_CT, A_RH, A_SM = 0, 40 * KB, 44 * KB, 48 * KB
        A_RP = 16 * KB
        A_TB, A_SQ, A_SK, A_SV = 0, 16 * KB, 48 * KB, 56 * KB
        M_XN, M_XT, M_RA, M_RB, M_JK = 0, 4 * KB, 8 * KB, 12 * KB, 14 * KB
        M_S, M_P, M_AT, M_MR = 0, 2 * KEYS, 2 * KEYS + 2 * 640, 2 * KEYS + 2 * 640 + 512
        KTB, VB = 17 * 256, 5 * 1024

        block = ctx.enter_context(nc.Block())

        @block.sync
        def _(sp):
            sp.dma_start(v(A_, 0, [P, 2], [1, P], rows=16), dap(Cc, 0, [[P, 16], [16 * P, 2], [1, P]])).then_inc(par_in, 16)
            sp.dma_start(v(A_, 256, [NSTATE, 2], [1, NSTATE], rows=16), dap(log_A, 0, [[NSTATE, 16], [16 * NSTATE, 2], [1, NSTATE]])).then_inc(par_in, 16)
            sp.dma_start(v(A_, 384, [NSTATE, 2], [1, NSTATE], rows=16), dap(A_im, 0, [[NSTATE, 16], [16 * NSTATE, 2], [1, NSTATE]])).then_inc(par_in, 16)
            with nc.allow_non_contiguous_dma(reason="32 numbers"):
                sp.dma_start(v(A_, 512, [1, 2], rows=16), dap(log_dt, 0, [[1, 16], [16, 2]])).then_inc(par_in, 16)
            sp.dma_start(leni[:, :], dap(len0, 0, [[0, P], [1, B]])).then_inc(len_in, 16)
            sp.dma_start(v(stat, 0, [1, S], rows=1), dap(Dskip, 0, [[S, 1], [1, S]])).then_inc(d_in, 16)
            sp.dma_start(v(A_, A_X, [HID, NT], [1, HID]), dap(x, 0, [[HID, P], [P * HID, NT], [1, HID]])).then_inc(x_in, 16)

            def slot(par, n, src):
                if not isinstance(n, int) or n >= 2:
                    sp.wait_ge(tp_done, n * 4 - 4)
                sp.dma_start(slot_all(par), src).then_inc(slot_in[par], 16)

            def slot_experts(par, n, w, first):
                sp.wait_ge(tp_done, n * 4 - 4)
                for e in range(8):
                    sp.dma_start(v(M_, par * SLOT + e * R0, [512, 4], [1, R0]),
                                 dap(w, (first + e) * HID * R0, [[R0, P], [P * R0, 4], [1, R0]])).then_inc(slot_in[par], 16)

            sp.dma_start(v(M_, 0, [1, 512], rows=R0), ffnA).then_inc(slot_in[0], 16)
            sp.dma_start(v(M_, 0, [1, 512], p0=R0, rows=R0), ffnA).then_inc(slot_in[0], 16)
            sp.dma_start(v(M_, 512, [1, 512], rows=E0), router_w).then_inc(slot_in[0], 16)
            sp.dma_start(v(M_, 512, [1, 512], p0=E0, rows=E1), gate_w).then_inc(slot_in[0], 16)
            slot(1, 1, rows_of(base_w, 0))
            for i in range(2):
                slot_experts(i, 2 + i, ffnB, 8 * i)
            for i in range(2):
                slot(i, 4 + i, rows_of(Wk, 512 * i))
            for i in range(2):
                slot(i, 6 + i, rows_of(Wv, 512 * i))

            def keys(i):
                for half in range(2):
                    slot(half, i * 2 + 8 + half,
                         dap(k_cache, i * (512 * HK * D) + half * 512, [[HK * D, P], [P * HK * D, 4], [1, 512]]))
                sp.wait_ge(tp_act, i * 4 + 20)
                sp.wait_ge(tp_dve, i * 4 + 20)
                sp.dma_start(dap(kT, i * (16 * P * 256), [[256, P], [P * 256, 16], [1, 256]]),
                             v(M_, M_Y, [256, 16], [1, 256])).then_inc(kst_out, 16)

            with sp.Fori(0, 4) as i:
                keys(i)

            sp.wait_ge(r_cp, NT)
            sp.dma_start(dap(x1d, 0, [[HID, P], [P * HID, NT], [1, HID]]), v(M_, M_U, [HID, NT], [1, HID])).then_inc(x1_out, 16)

            with sp.Fori(0, 4) as i:
                for par in range(2):
                    slot(par, i * 2 + 16 + par, dap(Wq, i * (1024 * 512) + par * 512 * 512, [[512, P], [P * 512, 4], [1, 512]]))

            def tile_store(t, par):
                sp.wait_ge(rt_cp, t * 10 + 10)
                sp.wait_ge(v_cp, t * 2 + 2)
                sp.dma_start(dap(qT, t * (4 * P * HQ * S), [[HQ * S, P], [P * HQ * S, 4], [1, HQ * S]]),
                             v(A_, A_SQ + 16 * KB * par, [HQ * S, 4], [1, HQ * S])).then_inc(st_out[par], 16)
                sp.dma_start(dap(knT, t * (4 * P * HK * S), [[HK * S, P], [P * HK * S, 4], [1, HK * S]]),
                             v(A_, A_SK + 4 * KB * par, [HK * S, 4], [1, HK * S])).then_inc(st_out[par], 16)
                sp.dma_start(dap(vn, t * (P * HK * D), [[HK * D, P], [1, HK * D]]),
                             v(A_, A_SV + 4 * KB * par, [1, HK * D])).then_inc(st_out[par], 16)

            with sp.Fori(0, 4) as i:
                for par in range(2):
                    tile_store(i * 2 + par, par)

            sp.wait_ge(pj_done, NT * 12)
            sp.wait_ge(rt_done, NT * 10)
            with sp.Fori(0, 4) as i:
                for par in range(2):
                    slot(par, i * 2 + 24 + par,
                         dap(Wo, i * 1024 + par * 512, [[HQ * D, P], [P * HQ * D, 4], [1, 512]]))

            for par in range(2):
                sp.wait_ge(st_out[par], 48 * 4)
            sp.wait_ge(zero_ok, 3)

            def batch_load(b, par, first=False):
                if not first:
                    sp.wait_ge(s_done, b * HK - HK)
                sp.dma_start(v(M_, M_QT + par * HQ * S, [1, HQ * S]), dap(qT, b * (P * HQ * S), [[HQ * S, P], [1, HQ * S]])).then_inc(q_in[par], 16)
                sp.dma_start(v(M_, M_KT + par * KTB + L * HK, [1, HK * S]), dap(knT, b * (P * HK * S), [[HK * S, P], [1, HK * S]])).then_inc(q_in[par], 16)
                if not first:
                    sp.wait_ge(o_done, b * HK - HK)
                sp.dma_start(v(M_, M_V + par * VB + 4096, [1, HK * D], rows=S), dap(vn, b * (S * HK * D), [[HK * D, S], [1, HK * D]])).then_inc(vn_in[par], 16)

            for k in range(BT4):
                batch_load(k, k % 2, first=k < 2)
            with sp.Fori(1, NT) as t:
                for k in range(BT4):
                    batch_load(t * BT4 + k, k % 2)

            sp.wait_ge(at_done, NT)
            sp.wait_ge(at_cp, NT)
            slot(0, 32, rows_of(lora_A, 0))
            slot_experts(1, 33, lora_B, 0)
            sp.wait_ge(x1_out, 16)
            sp.dma_start(v(M_, M_KT, [HID, NT], [1, HID]), dap(x1d, 0, [[HID, P], [P * HID, NT], [1, HID]])).then_inc(x1_back, 16)
            for t in range(NT):
                sp.wait_ge(ob_cp, t + 1)
                sp.dma_start(dap(out, t * P * HID, [[HID, P], [1, HID]]), v(M_, M_KT + t * HID, [1, HID])).then_inc(out_done, 16)
            sp.wait_ge(out_done, 16 * NT)

        @block.gpsimd
        def _(pool):
            pool.dma_start(cst[:, :], const).then_inc(cst_in, 16)
            with nc.allow_non_contiguous_dma(reason="a column of 512 numbers"):
                pool.dma_start(biasc[:, :], dap(base_b, 0, [[1, P], [P, NJ]])).then_inc(cst_in, 16)
            pool.dma_start(seqi[:, :], dap(seqlens, 0, [[0, P], [1, B]])).then_inc(seq_in, 16)

            pool.wait_ge(x_in, 16)
            for t in range(NT):
                nc.gpsimd.tensor_copy(v(M_, M_Y + t * HID, [P, NJ], [1, P]),
                                      v(A_, A_X + t * HID + P - 1, [P, NJ], [-1, P])).then_inc(xrev_ok, 1)

            zeros = idxv[0:S, 0:P - 1].bitcast(F32)
            nc.gpsimd.memset(zeros, 0.0).then_inc(zero_ok, 1)
            pool.wait_ge(zero_ok, 1)
            pool.dma_start(dap(kpad, 0, [[KPAD, S], [1, P - 1]]), zeros).then_inc(pad_out, 16)
            pool.wait_ge(taps_sb, 1)
            pool.dma_start(dap(kpad, P - 1, [[KR, KQ], [KPAD, S], [1, KR]]), v(A_, A_KQ, [KR, S], [1, KR], rows=KQ)).then_inc(taps_out, 16)
            pool.wait_ge(taps_out, 16)
            pool.wait_ge(pad_out, 16)
            pool.wait_ge(xt_done, NT)
            for g in range(4):
                pool.dma_start(v(A_, g * 8 * 512, [512, 8], [1, 512]),
                               dap(kpad, g * 8 * KPAD, [[1, P], [KPAD, 8], [1, 512]])).then_inc(hank_in[g], 16)

            pool.wait_ge(conv_done, 8)
            pool.wait_ge(conv_cp, 8)
            pool.dma_start(tabi[:, :], dap(table, 0, [[0, P], [1, B * NPP]])).then_inc(tab_in, 16)
            pool.dma_start(v(A_, A_RP + 5 * 512, [1, D]), dap(qnw, 0, [[0, P], [1, D]])).then_inc(nw_in, 16)
            pool.dma_start(v(A_, A_RP + 5 * 512 + D, [1, D]), dap(knw, 0, [[0, P], [1, D]])).then_inc(nw_in, 16)

            pool.wait_ge(x1_ok, 2 * NJ)
            pool.wait_ge(tp_done, 96)

            def tile(t, par):
                if not isinstance(t, int) or t >= 2:
                    pool.wait_ge(pj_done, t * 12 - 12)
                nc.gpsimd.tensor_copy(v(M_, M_XT + par * 512, [P, NJ], [1, P]),
                                      v(x1T, t * P, [TOK, NJ], [1, P])).then_inc(xt_ok, 1)

            tile(0, 0)
            tile(1, 1)
            with pool.Fori(1, 4) as i:
                tile(i * 2, 0)
                tile(i * 2 + 1, 1)

            pool.wait_ge(pj_done, NT * 12)
            pool.wait_ge(kst_out, 64)
            for par in range(2):
                nc.gpsimd.memset(v(M_, M_V + par * VB + 4096, [1, 1024]), 0.0).then_inc(zero_ok, 1)
            pool.wait_ge(idx_ok, 1)

            def gather(t, k):
                par = k % 2
                b = t * BT4 + k
                first = isinstance(t, int)
                if not first:
                    pool.wait_ge(v_in[par], t * 128 - 64 + 64 * (k // 2))
                    pool.wait_ge(k_in[par], t * 512 - 256 + 256 * (k // 2))
                nc.gpsimd.tensor_copy(idc[:, k * 20:k * 20 + 16], v(tabi, b * NPP, [1, NPP])).then_inc(idc_ok, 1)
                nc.gpsimd.tensor_copy(idc[:, k * 20 + 16:k * 20 + 20], v(idxv, b * 4, [1, 4])).then_inc(idc_ok, 1)
                if not first or k >= 2:
                    pool.wait_ge(s_done, b * HK - HK)
                pool.wait_ge(idc_ok, b * 2 + 2)
                nc.gpsimd.tensor_tensor(stat[:, 61:62], cst[:, 0:1], cst[:, 0:1], ALU.add)
                for s in range(NPP):
                    nc.gpsimd.indirect_dma_start(
                        v(M_, M_KT + par * KTB + s * 256, [1, 256]), None, kT,
                        bass.IndirectOffsetOnAxis(ap=idc[:, k * 20 + s:k * 20 + s + 1].bitcast(U32), axis=0)).then_inc(k_in[par], 16)
                if not first or k >= 2:
                    pool.wait_ge(o_done, b * HK - HK)
                    nc.gpsimd.tensor_tensor(stat[:, 62:63], cst[:, 0:1], cst[:, 0:1], ALU.add)
                for s in range(4):
                    nc.gpsimd.indirect_dma_start(
                        v(M_, M_V + par * VB + s * 1024, [1, 1024]), None, v_cache.rearrange("a b c d -> (a b) (c d)"),
                        bass.IndirectOffsetOnAxis(ap=idc[:, k * 20 + 16 + s:k * 20 + 17 + s].bitcast(U32), axis=0)).then_inc(v_in[par], 16)

            for k in range(BT4):
                gather(0, k)
            with pool.Fori(1, NT) as t:
                for k in range(BT4):
                    gather(t, k)

        @block.tensor
        def _(pe):
            def tp(o, i, rows=P):
                return nc.tensor.transpose(o, i, cst[0:rows, C_ID:C_ID + rows])

            def mm(o, l, r, start, stop):
                return nc.tensor.matmul(o, l, r, start=start, stop=stop)

            def slot_jobs(par, n, landed, small_slot=False):
                pe.wait_ge(slot_in[par], landed)
                for j in range(4):
                    if not isinstance(n, int) or n >= 1:
                        pe.wait_ge((tp_act, tp_dve)[j % 2], n * 2 - 1 + j // 2)
                    for k in range(2 if small_slot else 4):
                        rows = E0 + E1 if small_slot and k else P
                        last = tp(bank(j, rows, k * P), raw(par, k, j, rows), rows)
                    last.then_inc(tp_done, 1)

            pe.wait_ge(cst_in, 32)
            pe.wait_ge(par_in, 64)
            pe.wait_ge(par_t, 1)
            i16 = cst[0:16, C_ID:C_ID + 16]
            for c, src in enumerate((v(A_, 256, [1, P], rows=16), v(A_, 576, [1, P], rows=16), v(A_, 384, [1, P], rows=16),
                                     v(A_, 0, [2, P], rows=16), v(A_, 1, [2, P], rows=16))):
                last = nc.tensor.transpose(bank(7, 16, 16 * c), src, i16)
            last.then_inc(par_c, 1)

            pe.wait_ge(x_in, 16)
            for t in range(NT):
                q = t % 2
                if t >= 2:
                    pe.wait_ge(xf_cp, t - 1)
                for j in range(NJ):
                    last = tp(bank(q, P, j * P), v(A_, A_X + t * HID + j * P, [1, P]))
                last.then_inc(xf_done, 1)
                pe.wait_ge(xrev_ok, t + 1)
                if t >= 2:
                    pe.wait_ge(xr_cp, t - 1)
                for j in range(NJ):
                    last = tp(bank(2 + q, P, j * P), v(M_, M_Y + t * HID + j * P, [1, P]))
                last.then_inc(xt_done, 1)

            pe.wait_ge(taps_in, 1)
            for g in range(2):
                for hh in range(16):
                    o = bank(5 + g, KR, hh * KR, rows=KQ)
                    for c in range(2):
                        last = mm(o, v(A_, A_SR + c * 256 + hh * KQ, [1, KQ], p0=64 * g, rows=64),
                                  v(A_, A_EM + c * 768 + hh * NX, [1, KR], p0=64 * g, rows=64), c == 0, c == 1)
            last.then_inc(taps_ps, 1)

            pe.wait_ge(xf_cp, NT)
            pe.wait_ge(xr_cp, NT)
            slot_jobs(0, 0, 64, small_slot=True)
            for n, landed in ((1, 16), (2, 192), (3, 144), (4, 208), (5, 160), (6, 224), (7, 176)):
                slot_jobs(n % 2, n, landed)
            with pe.Fori(0, 4) as i:
                slot_jobs(0, i * 2 + 8, i * 16 + 240)
                slot_jobs(1, i * 2 + 9, i * 16 + 192)

            for h in range(S):
                g, q = h // 4, h % 4
                if q == 0:
                    if g == 0:
                        pe.wait_ge(taps_sb, 1)
                    if g >= 4:
                        pe.wait_ge(conv_cp, g - 3)
                if h % 8 == 0:
                    pe.wait_ge(hank_in[h // 8], 16)
                for d in range(NJ):
                    last = mm(bank(4 + g % 4, (NJ - d) * B, q * P + d * B),
                              v(A_, h * 512 + d * P, [1, P]),
                              v(M_, M_U + h * B, [TOK, NJ - d], [1, B]), d == 0, d == NJ - 1)
                if q == 3:
                    last.then_inc(conv_done, 1)

            pe.wait_ge(conv_cp, 8)
            for t in range(NT):
                for j in range(NJ):
                    last = mm(bank(4, E0, t * E0), v(M_, M_Y + j * TOK + t * P, [1, P]),
                              v(small, j * 152 + P, [1, E0]), j == 0, j == NJ - 1)
            last.then_inc(lg_done, 1)
            for half in range(2):
                for j in range(NJ):
                    last = mm(bank(5 + half), v(small, j * 152, [1, P]),
                              v(M_, M_Y + j * TOK + half * 512, [1, 512]), j == 0, j == NJ - 1)
                last.then_inc(rh_done, 1)

            def weights_to_experts(n, e):
                pe.wait_ge(cw_ok, n + 1)
                for t in range(NT):
                    last = tp(bank(2 + t // 4, P, (t % 4) * P, rows=e), v(A_, A_SM + 14 * P + t * e, [1, e]))
                last.then_inc(ct_done, 1)

            pe.wait_ge(tp_act, 32)
            pe.wait_ge(tp_dve, 32)
            weights_to_experts(0, E0)
            pe.wait_ge(ct_cp, 1)
            for half in range(2):
                for a in range(E0 // 2):
                    n = half * 8 + a
                    if n >= 2:
                        pe.wait_ge(z_ok, n - 1)
                    mm(bank(2 + n % 2), v(cst, C_S0 + a * P, [1, P], rows=E0),
                       v(A_, A_CT + half * 512, [1, 512], rows=E0), True, True).then_inc(bc_done, 1)
            for half in range(2):
                pe.wait_ge(z_ok, half * 8 + 8)
                for j in range(NJ):
                    n = half * 4 + j
                    if n == 0:
                        pe.wait_ge(rh_cp, 2)
                    if n >= 4:
                        pe.wait_ge(x1_ok, n - 3)
                    o = bank(4 + n % 4)
                    for i in range(NJ):
                        mm(o, v(M_, M_BW + i * 512 + j * P, [1, P]), v(M_, M_Y + i * TOK + half * 512, [1, 512]), i == 0, False)
                    for a in range(E0 // 2):
                        last = mm(o, v(M_, M_BT + a * 512 + j * P, [1, P]),
                                  v(A_ if half else M_, (A_Z1 if half else M_U) + a * 512, [1, 512]), False, a == E0 // 2 - 1)
                    last.then_inc(y_done, 1)

            pe.wait_ge(x1_ok, 8)
            for t in range(NT):
                if t >= 2:
                    pe.wait_ge(r_cp, t - 1)
                for j in range(NJ):
                    last = tp(bank(4 + t % 2, P, j * P), v(x1T, j * TOK + t * P, [1, P]))
                last.then_inc(r_done, 1)

            with pe.Fori(0, 4) as i:
                slot_jobs(0, i * 2 + 16, i * 16 + 304)
                slot_jobs(1, i * 2 + 17, i * 16 + 256)

            pe.wait_ge(tp_act, 48)
            pe.wait_ge(tp_dve, 48)
            pe.wait_ge(r_cp, NT)

            def project_tile(t, par, first):
                def turn(c):
                    pe.wait_ge(rot_ok, t * 10 + c + 1)
                    if not first or c >= 2:
                        pe.wait_ge(rt_cp, t * 10 + c - 1)
                    for a in range(4):
                        last = tp(bank(6 + c % 2, P, a * P), v(M_, M_RA + (c % 2) * 512 + a * P, [1, P]))
                    last.then_inc(rt_done, 1)

                pe.wait_ge(xt_ok, t + 1)
                for k in range(12):
                    o = bank(k % 4)
                    if k >= 4:
                        pe.wait_ge(sc_ok, t * 10 + k - 3)
                    elif not first and k < 2:
                        pe.wait_ge(sc_ok, t * 10 + k - 1)
                    elif not first:
                        pe.wait_ge(v_cp, t * 2 + k - 3)
                    for j in range(NJ):
                        if k < 8:
                            w = v(M_, M_WQ + j * 4096 + k * 512, [1, 512])
                        elif k < 10:
                            w = v(M_, M_WK + j * 1024 + (k - 8) * 512, [1, 512])
                        else:
                            w = v(M_, M_WV + j * 1024 + (k - 10) * 512, [1, 512])
                        last = mm(o, v(M_, M_XT + par * 512 + j * P, [1, P]), w, j == 0, j == NJ - 1)
                    last.then_inc(pj_done, 1)
                    if k >= 3:
                        turn(k - 3)
                turn(9)

            project_tile(0, 0, True)
            project_tile(1, 1, False)
            with pe.Fori(1, 4) as i:
                project_tile(i * 2, 0, False)
                project_tile(i * 2 + 1, 1, False)

            with pe.Fori(0, 4) as i:
                slot_jobs(0, i * 2 + 24, i * 16 + 368)
                slot_jobs(1, i * 2 + 25, i * 16 + 320)

            pe.wait_ge(tp_act, 64)
            pe.wait_ge(tp_dve, 64)
            pe.wait_ge(rt_cp, NT * 10)
            pe.wait_ge(pz_ok, 1)

            def scores(t, u, first=False):
                k, h = u // HK, u % HK
                par = k % 2
                if h == 0:
                    pe.wait_ge(k_in[par], t * 512 + 256 * (k // 2 + 1))
                    pe.wait_ge(q_in[par], t * 64 + 32 * (k // 2 + 1))
                if not first or u >= 2:
                    pe.wait_ge(sm_ok, t * 32 + u - 1)
                q = v(M_, M_QT + par * HQ * S + h * P, [1, P])
                mm(bank(2 * (u % 2)), q, v(M_, M_KT + par * KTB + h * S, [256, NPP], [1, S]), True, True)
                mm(bank(2 * (u % 2) + 1, S), q, v(M_, M_KT + par * KTB + L * HK + h * S, [1, S]), True, True).then_inc(s_done, 1)

            def turn_output(t):
                pe.wait_ge(wo_cp, t + 1)
                for j in range(NJ):
                    last = tp(bank(7, P, j * P), v(M_, M_AT + j * P, [1, P]))
                last.then_inc(at_done, 1)

            def attend_tile(t, first=False, last_tile=False):
                def turn(u):
                    pe.wait_ge(p_ok, t * 32 + u + 1)
                    if not first or u >= 1:
                        pe.wait_ge(pt_cp, t * 32 + u)
                    for c in range(4):
                        tp(bank(4, P, c * P), v(M_, M_S + (u % 2) * KEYS + c * P, [1, P]))
                    tp(bank(5, P, 0, rows=S), v(M_, M_S + (u % 2) * KEYS + L, [1, S])).then_inc(pt_done, 1)

                def values(u):
                    k, h = u // HK, u % HK
                    par = k % 2
                    if h == 0:
                        pe.wait_ge(v_in[par], t * 128 + 64 * (k // 2 + 1))
                        pe.wait_ge(vn_in[par], t * 32 + 16 * (k // 2 + 1))
                    pe.wait_ge(pt_cp, t * 32 + u + 1)
                    if not first or u >= 1:
                        pe.wait_ge(o_cp, t * 32 + u)
                    for c in range(5):
                        last = mm(bank(6, P), v(M_, M_V + par * VB + c * 1024 + h * D, [1, D]),
                                  v(M_, M_P + (u % 2) * 640 + c * P, [1, P]), c == 0, c == 4)
                    last.then_inc(o_done, 1)

                for u in range(32):
                    if u + 2 < 32:
                        scores(t, u + 2, first)
                    turn(u)
                    if u == 0 and not first:
                        turn_output(t - 1)
                    if u >= 1:
                        values(u - 1)
                values(31)
                if not last_tile:
                    scores(t + 1, 0)
                    scores(t + 1, 1)
                if not first:
                    pe.wait_ge(at_cp, t)
                pe.wait_ge(o_cp, t * 32 + 32)
                for h in range(HQ):
                    last = mm(bank(7), v(M_, M_OT + h * P, [1, P]), v(A_, h * 512, [1, 512]), h == 0, h == HQ - 1)
                last.then_inc(wo_done, 1)

            scores(0, 0, True)
            scores(0, 1, True)
            attend_tile(0, first=True)
            with pe.Fori(1, NT - 1) as t:
                attend_tile(t)
            attend_tile(NT - 1, last_tile=True)
            turn_output(NT - 1)

            slot_jobs(0, 32, 432)
            slot_jobs(1, 33, 496)
            pe.wait_ge(at_cp, NT)
            for t in range(NT):
                for j in range(NJ):
                    last = mm(bank(4, E1, t * E1), v(x1T, j * TOK + t * P, [1, P]),
                              v(small, j * 152 + P + E0, [1, E1]), j == 0, j == NJ - 1)
            last.then_inc(lg_done, 1)
            pe.wait_ge(tp_act, 68)
            pe.wait_ge(tp_dve, 68)
            weights_to_experts(1, E1)
            pe.wait_ge(ct_cp, 2)
            for half in range(2):
                for a in range(E1 // 2):
                    n = half * 4 + a
                    if n >= 2:
                        pe.wait_ge(z_ok, 16 + n - 1)
                    for j in range(NJ):
                        last = mm(bank(4 + n % 2), v(A_, j * 512 + a * P, [1, P]),
                                  v(x1T, j * TOK + half * 512, [1, 512]), j == 0, j == NJ - 1)
                    last.then_inc(ha_done, 1)
                    mm(bank(2 + n % 2), v(cst, C_S0 + a * P, [1, P], rows=E1),
                       v(A_, A_CT + half * 512, [1, 512], rows=E1), True, True).then_inc(bc_done, 1)
            for t in range(NT):
                half = t // 4
                pe.wait_ge(z_ok, 16 + half * 4 + 4)
                if t >= 2:
                    pe.wait_ge(ob_cp, t - 1)
                for a in range(E1 // 2):
                    last = mm(bank(6 + t % 2), v(M_, M_V + half * 2048 + a * 512 + (t % 4) * P, [1, P]),
                              v(A_, 2048 + a * 512, [1, 512]), a == 0, a == E1 // 2 - 1)
                last.then_inc(ob_done, 1)

        @block.scalar
        def _(act):
            def copy(o, i):
                return nc.scalar.activation(o, i, ACT.Copy)

            for t in range(NT):
                act.wait_ge(xf_done, t + 1)
                copy(v(x1T, t * P, [TOK, NJ], [1, P]), v(PS, (t % 2) * 512, [P, NJ], [1, P])).then_inc(xf_cp, 1)
            act.wait_ge(exp_arg, 1)
            nc.scalar.activation(v(A_, A_BIG + 4 * 768, [1, 768]), v(A_, A_BIG + 4 * 768, [1, 768]), ACT.Exp).then_inc(exp_ok, 1)
            act.wait_ge(sin_arg, 1)
            nc.scalar.activation(v(A_, A_BIG + 768, [1, 768]), v(A_, A_BIG + 3 * 768, [1, 768]), ACT.Sin).then_inc(sin_ok, 1)
            nc.scalar.activation(v(A_, A_BIG + 2 * 768, [1, 768]), v(A_, A_BIG + 3 * 768, [1, 768]), ACT.Sin, scale=0.5).then_inc(sin_ok, 1)
            act.wait_ge(taps_ps, 1)
            copy(v(A_, A_KQ, [1, S * KR], rows=KQ), v(PS, 5 * 512, [1, S * KR], rows=KQ)).then_inc(taps_cp, 1)

            def even_jobs(n, dst):
                for j in (0, 2):
                    act.wait_ge(tp_done, n * 4 + j + 1)
                    copy(*dst(j)).then_inc(tp_act, 1)

            even_jobs(0, lambda j: (dst_small(j), bank(j, 152)))
            even_jobs(1, lambda j: (wide(M_, M_BW + j * 512), bank(j)))
            for i in range(2):
                even_jobs(2 + i, lambda j: (wide(M_, M_BT + (4 * i + j) * 512), bank(j)))
            for i in range(2):
                even_jobs(4 + i, lambda j: (wide(M_, M_WK + j * 1024 + i * 512), bank(j)))
            for i in range(2):
                even_jobs(6 + i, lambda j: (wide(M_, M_WV + j * 1024 + i * 512), bank(j)))

            def stage_keys(i):
                if not isinstance(i, int):
                    act.wait_ge(kst_out, i * 16)
                for half in range(2):
                    even_jobs(i * 2 + 8 + half, lambda j: (
                        v(M_, M_Y + (4 * half + j) * S, [256, 16], [1, S]), v(PS, j * 512, [S, 16], [1, S])))

            stage_keys(0)
            with act.Fori(1, 4) as i:
                stage_keys(i)

            def exp_logits(n, e):
                act.wait_ge(lx_ok, n + 1)
                nc.scalar.activation(v(A_, A_SM + P, [1, NT * e]), v(A_, A_SM, [1, NT * e]), ACT.Exp).then_inc(le_ok, 1)

            for half in range(2):
                act.wait_ge(rh_done, half + 1)
                copy(wide(A_, A_RH + half * 512), bank(5 + half)).then_inc(rh_cp, 1)
            exp_logits(0, E0)
            for t in range(NT):
                act.wait_ge(r_done, t + 1)
                copy(wide(M_, M_U + t * HID), bank(4 + t % 2)).then_inc(r_cp, 1)
            act.wait_ge(rope_arg, 1)
            nc.scalar.activation(wide(A_, A_RP + 1024), wide(A_, A_RP), ACT.Sin).then_inc(rope_sin, 1)
            nc.scalar.activation(wide(A_, A_RP + 1536), wide(A_, A_RP), ACT.Sin, scale=0.5).then_inc(rope_sin, 1)
            act.wait_ge(x1_out, 16)
            with act.Fori(0, 4) as i:
                for par in range(2):
                    even_jobs(i * 2 + 16 + par, lambda j: (wide(M_, i * 1024 + (M_WQ + j * 4096 + par * 512)), bank(j)))

            def norm_tile(t, par):
                first = isinstance(t, int)
                if not first or t >= 2:
                    act.wait_ge(st_out[par], (t * 24 if par == 0 else t * 24 - 24))

                def turned(c):
                    act.wait_ge(rt_done, t * 10 + c + 1)
                    if c < 8:
                        o = v(A_, A_SQ + par * 4096 + c * 4 * S, [HQ * S, 4], [S, 4], [1, S])
                    else:
                        o = v(A_, A_SK + par * 1024 + (c - 8) * 4 * S, [HK * S, 4], [S, 4], [1, S])
                    copy(o, v(PS, (6 + c % 2) * 512, [S, 4], [P, 4], [1, S])).then_inc(rt_cp, 1)

                def normalise(c):
                    g = c % 2
                    act.wait_ge(nf_ok, t * 10 + c + 1)
                    if not first or t * 10 + c >= 2:
                        act.wait_ge(rot_ok, t * 10 + c - 1)
                    for a in range(4):
                        last = nc.scalar.activation(v(M_, M_XN + g * 512 + a * P, [1, P]), bank(c % 4, P, a * P), ACT.Copy,
                                                    scale=stat[:, 16 + g * 4 + a:17 + g * 4 + a])
                    last.then_inc(sc_ok, 1)

                for k in range(12):
                    g = k % 2
                    if k < 10:
                        act.wait_ge(pj_done, t * 12 + k + 1)
                        if not first or t * 10 + k >= 2:
                            act.wait_ge(nf_ok, t * 10 + k - 1)
                        if not first or t * 10 + k >= 1:
                            act.wait_ge(ms_ok, t * 10 + k)
                        for a in range(4):
                            last = nc.scalar.activation(v(M_, M_JK + a * P, [1, P]), bank(k % 4, P, a * P), ACT.Square,
                                                        accum_out=stat[:, g * 4 + a:g * 4 + a + 1])
                        last.then_inc(sq_ok, 1)
                        act.wait_ge(ms_ok, t * 10 + k + 1)
                        nc.scalar.activation(stat[:, 32 + g * 4:36 + g * 4], stat[:, g * 4:g * 4 + 4], ACT.Sqrt).then_inc(sd_ok, 1)
                    if 1 <= k <= 10:
                        normalise(k - 1)
                    if k >= 10:
                        act.wait_ge(pj_done, t * 12 + k + 1)
                        copy(wide(A_, A_SV + par * 1024 + (k - 10) * 512), bank(k % 4)).then_inc(v_cp, 1)
                    if k >= 3:
                        turned(k - 3)
                turned(9)

            norm_tile(0, 0)
            norm_tile(1, 1)
            with act.Fori(1, 4) as i:
                norm_tile(i * 2, 0)
                norm_tile(i * 2 + 1, 1)

            for par in range(2):
                act.wait_ge(st_out[par], 48 * 4)
            with act.Fori(0, 4) as i:
                for par in range(2):
                    even_jobs(i * 2 + 24 + par, lambda j: (wide(A_, i * 4096 + (par * 2048 + j * 512)), bank(j)))

            def expo(t, u):
                g = u % 2
                act.wait_ge(nm_ok, t * 32 + u + 1)
                s = v(M_, M_S + g * KEYS, [1, KEYS])
                nc.scalar.activation(s, s, ACT.Exp, bias=stat[:, 4 + g:5 + g], accum_out=stat[:, 8 + g:9 + g]).then_inc(e_ok, 1)

            def attend_tile(t, first=False, last_tile=False):
                for u in range(32):
                    if u + 1 < 32:
                        expo(t, u + 1)
                    act.wait_ge(pt_done, t * 32 + u + 1)
                    if not first or u >= 2:
                        act.wait_ge(o_done, t * 32 + u - 1)
                    copy(v(M_, M_P + (u % 2) * 640, [1, 640]), v(PS, 4 * 512, [1, 640])).then_inc(pt_cp, 1)
                if not last_tile:
                    expo(t + 1, 0)
                act.wait_ge(wo_done, t + 1)
                if not first:
                    act.wait_ge(at_done, t)
                copy(wide(M_, M_AT), bank(7)).then_inc(wo_cp, 1)

            expo(0, 0)
            attend_tile(0, first=True)
            with act.Fori(1, NT - 1) as t:
                attend_tile(t)
            attend_tile(NT - 1, last_tile=True)

            act.wait_ge(wo_done, NT)
            even_jobs(32, lambda j: (wide(A_, j * 512), bank(j)))
            even_jobs(33, lambda j: (wide(A_, 2048 + j * 512), bank(j)))
            exp_logits(1, E1)
            for n in range(8):
                act.wait_ge(ha_done, n + 1)
                if n >= 2:
                    act.wait_ge(z_ok, 16 + n - 1)
                copy(wide(A_, A_RH + (n % 2) * 512), bank(4 + n % 2)).then_inc(ha_cp, 1)

        @block.vector
        def _(dve):
            steps = [0]
            ve = nc.vector

            def link(ins):
                steps[0] += 1
                ins.then_inc(chain, 1)
                dve.wait_ge(chain, steps[0])

            def stt(o, a, s, b, op0, op1):
                return ve.scalar_tensor_tensor(out=o, in0=a, scalar=s, in1=b, op0=op0, op1=op1)

            def tt(o, a, b, op):
                return ve.tensor_tensor(o, a, b, op)

            def ts(o, a, s1, op0, s2=None, op1=None):
                return ve.tensor_scalar(o, a, s1, s2, op0, op1) if op1 is not None else ve.tensor_scalar(o, a, s1, None, op0)

            def exp_exact(dst, src, n, t0):
                y, k, r, q, p2 = (v(A_, A_T + t0 + 32 * a, [1, n]) for a in range(5))
                link(ts(y, src, 1.4426950408889634, ALU.mult, MAGIC, ALU.add))
                link(ts(k, y, MAGIC, ALU.subtract, -126.0, ALU.max))
                link(stt(r, k, -LN2_HI, src, ALU.mult, ALU.add))
                link(stt(r, k, -LN2_LO, r, ALU.mult, ALU.add))
                link(ts(q, r, 1.0 / 5040, ALU.mult))
                for c in (1.0 / 720, 1.0 / 120, 1.0 / 24, 1.0 / 6, 0.5, 1.0):
                    link(stt(q, q, c, r, ALU.add, ALU.mult))
                link(ts(v(A_, A_T + t0 + 32 * 4, [1, n]).bitcast(I32), k, 127.0, ALU.add, float(2 ** 23), ALU.mult))
                link(stt(dst, q, 1.0, p2, ALU.add, ALU.mult))

            def reduce_phase(ph, y, r, done):
                link(ts(y, ph, INV_TWO_PI, ALU.mult, MAGIC, ALU.add))
                link(ts(y, y, MAGIC, ALU.subtract))
                link(stt(r, y, -TWO_PI_HI, ph, ALU.mult, ALU.add))
                link(stt(r, y, -TWO_PI_LO, r, ALU.mult, ALU.add))
                ts(r, r, PI_F, ALU.min, -PI_F, ALU.max).then_inc(done, 1)

            dve.wait_ge(par_in, 64)
            ve.tensor_copy(v(A_, 576, [NSTATE, 2], [1, NSTATE], rows=16), v(A_, 512, [1, 2], [0, NSTATE], rows=16)).then_inc(par_t, 1)

            tf = tabi[:, :].bitcast(F32)

            def mk(offset, *dims):
                return bass.AP(tf.tensor, offset, [[tf.ap[0][0], P], *[list(d) for d in dims]])

            dve.wait_ge(len_in, 16)
            dve.wait_ge(cst_in, 32)
            link(ve.tensor_copy(lenf[:, :], leni[:, :]))
            for j in range(NJ):
                link(ts(maskf[:, j * B:(j + 1) * B], lenf[:, :], cst[:, C_F + j:C_F + j + 1], ALU.is_gt))
                link(ts(maskr[:, j * B:(j + 1) * B], lenf[:, :], cst[:, C_FR + j:C_FR + j + 1], ALU.is_gt))

            for t in range(NT):
                dve.wait_ge(xt_done, t + 1)
                for j in range(NJ):
                    last = tt(v(M_, M_U + j * TOK + t * BT4, [1, BT4], [B, S]), v(PS, (2 + t % 2) * 512 + j * P, [S, BT4], [1, S]),
                              mk(NJ * B + j * B + t * BT4, [1, BT4], [0, S]), ALU.mult)
                last.then_inc(xr_cp, 1)

            dve.wait_ge(par_c, 1)
            pc = lambda c, n=16: v(A_, A_PC + 16 * c, [1, n])
            tmp = lambda a, n=16: v(A_, A_T + 32 * a, [1, n])
            big = lambda a: v(A_, A_BIG + 768 * a, [1, 768])
            big3 = lambda a: v(A_, A_BIG + 768 * a, [NX, 16], [1, NX])
            link(ve.tensor_copy(pc(0, 80), bank(7, 80)))
            exp_exact(tmp(5, 32), pc(0, 32), 32, 0)
            ar, dt, zr, zi = tmp(5), v(A_, A_T + 32 * 5 + 16, [1, 16]), tmp(6), tmp(7)
            link(ts(ar, ar, -1.0, ALU.mult))
            link(tt(zr, ar, dt, ALU.mult))
            link(tt(zi, pc(2), dt, ALU.mult))
            over = lambda a: v(A_, A_T + 32 * a, [1, 16], [0, NX])
            steps3 = v(cst, C_M, [0, 16], [1, NX])
            tt(big3(4), over(6), steps3, ALU.mult).then_inc(exp_arg, 1)
            link(tt(big3(0), over(7), steps3, ALU.mult))
            reduce_phase(big(0), big(1), big(3), sin_arg)
            exp_exact(tmp(9), zr, 16, 0)
            dve.wait_ge(sin_ok, 2)
            s1 = v(A_, A_BIG + 768 + 1, [NX, 16])
            h1 = v(A_, A_BIG + 2 * 768 + 1, [NX, 16])
            link(tt(tmp(10), h1, h1, ALU.mult))
            link(tt(tmp(10), tmp(10), tmp(9), ALU.mult))
            link(ts(tmp(11), tmp(9), 1.0, ALU.subtract))
            link(stt(tmp(10), tmp(10), -2.0, tmp(11), ALU.mult, ALU.add))
            link(tt(tmp(11), s1, tmp(9), ALU.mult))
            link(tt(tmp(12), pc(3), tmp(10), ALU.mult))
            link(tt(tmp(13), pc(4), tmp(11), ALU.mult))
            link(tt(tmp(12), tmp(12), tmp(13), ALU.subtract))
            link(tt(tmp(13), pc(3), tmp(11), ALU.mult))
            link(tt(tmp(14), pc(4), tmp(10), ALU.mult))
            link(tt(tmp(13), tmp(13), tmp(14), ALU.add))
            link(tt(tmp(14), ar, ar, ALU.mult))
            link(tt(tmp(15), pc(2), pc(2), ALU.mult))
            link(tt(tmp(14), tmp(14), tmp(15), ALU.add))
            link(ve.reciprocal(tmp(14), tmp(14)))
            link(ts(tmp(14), tmp(14), 2.0, ALU.mult))
            link(tt(tmp(15), tmp(12), ar, ALU.mult))
            link(tt(tmp(16), tmp(13), pc(2), ALU.mult))
            link(tt(tmp(15), tmp(15), tmp(16), ALU.add))
            link(tt(tmp(15), tmp(15), tmp(14), ALU.mult))
            link(tt(tmp(16), tmp(12), pc(2), ALU.mult))
            link(tt(tmp(17), tmp(13), ar, ALU.mult))
            link(tt(tmp(16), tmp(16), tmp(17), ALU.subtract))
            link(tt(tmp(16), tmp(16), tmp(14), ALU.mult))
            link(tt(big(2), big(2), big(2), ALU.mult))
            link(ts(big(2), big(2), -2.0, ALU.mult, 1.0, ALU.add))
            dve.wait_ge(exp_ok, 1)
            link(tt(big(5), big(2), big(4), ALU.mult))
            link(stt(big(6), big(1), -1.0, big(4), ALU.mult, ALU.mult))
            qre = v(A_, A_BIG + 5 * 768 + KR, [NX, 16], [1, KQ])
            qni = v(A_, A_BIG + 6 * 768 + KR, [NX, 16], [1, KQ])
            sre, sni = (v(A_, A_T + 32 * a, [1, 16], [0, KQ]) for a in (15, 16))
            w0, w1 = v(A_, A_BIG, [KQ, 16], [1, KQ]), v(A_, A_BIG + 256, [KQ, 16], [1, KQ])
            fre, fni = v(A_, A_SR, [KQ, 16], [1, KQ]), v(A_, A_SR + 256, [KQ, 16], [1, KQ])
            link(tt(w0, qre, sre, ALU.mult))
            link(tt(w1, qni, sni, ALU.mult))
            link(tt(fre, w0, w1, ALU.subtract))
            link(tt(w0, qni, sre, ALU.mult))
            link(tt(w1, qre, sni, ALU.mult))
            link(tt(w0, w0, w1, ALU.add))
            ts(fni, w0, -1.0, ALU.mult).then_inc(taps_in, 1)
            dve.wait_ge(taps_cp, 1)
            dve.wait_ge(d_in, 16)
            k0 = v(A_, A_KQ, [KR, S], rows=1)
            tt(k0, k0, v(stat, 0, [1, S], rows=1), ALU.add).then_inc(taps_sb, 1)

            def odd_jobs(n, dst):
                for j in (1, 3):
                    dve.wait_ge(tp_done, n * 4 + j + 1)
                    ve.tensor_copy(*dst(j)).then_inc(tp_dve, 1)

            odd_jobs(0, lambda j: (dst_small(j), bank(j, 152)))
            odd_jobs(1, lambda j: (wide(M_, M_BW + j * 512), bank(j)))
            for i in range(2):
                odd_jobs(2 + i, lambda j: (wide(M_, M_BT + (4 * i + j) * 512), bank(j)))
            for i in range(2):
                odd_jobs(4 + i, lambda j: (wide(M_, M_WK + j * 1024 + i * 512), bank(j)))
            for i in range(2):
                odd_jobs(6 + i, lambda j: (wide(M_, M_WV + j * 1024 + i * 512), bank(j)))

            def stage_keys(i):
                if not isinstance(i, int):
                    dve.wait_ge(kst_out, i * 16)
                for half in range(2):
                    odd_jobs(i * 2 + 8 + half, lambda j: (
                        v(M_, M_Y + (4 * half + j) * S, [256, 16], [1, S]), v(PS, j * 512, [S, 16], [1, S])))

            stage_keys(0)
            with dve.Fori(1, 4) as i:
                stage_keys(i)

            dve.wait_ge(kst_out, 64)
            for g in range(8):
                dve.wait_ge(conv_done, g + 1)
                for q in range(4):
                    last = tt(v(M_, M_Y + g * 4 + q, [TOK, NJ], [S, B]), v(PS, (4 + g % 4) * 512 + q * P, [B, NJ], [1, B]),
                              mk(0, [B, NJ], [1, B]), ALU.mult)
                last.then_inc(conv_cp, 1)

            def route(n, e, eps, scale):
                a3 = lambda i: v(A_, A_SM + P * i, [e, NT], [1, e])
                c1 = lambda i: v(A_, A_SM + P * i, [1, NT])
                cb = lambda i: v(A_, A_SM + P * i, [1, NT], [0, e])
                num = v(cst, C_M, [0, NT], [1, e])
                dve.wait_ge(lg_done, n + 1)
                lg = v(PS, 4 * 512, [e, NT], [1, e])
                link(ve.tensor_reduce(c1(2), lg, AX_X, ALU.max))
                tt(a3(0), lg, cb(2), ALU.subtract).then_inc(lx_ok, 1)
                dve.wait_ge(le_ok, n + 1)
                link(ve.tensor_reduce(c1(3), a3(1), AX_X, ALU.add))
                link(ve.reciprocal(c1(3), c1(3)))
                link(tt(a3(4), a3(1), cb(3), ALU.mult))
                link(ve.tensor_reduce(c1(5), a3(4), AX_X, ALU.max))
                link(tt(a3(6), a3(4), cb(5), ALU.is_equal))
                link(stt(a3(6), a3(6), -64.0, num, ALU.mult, ALU.add))
                link(ve.tensor_reduce(c1(7), a3(6), AX_X, ALU.min))
                link(tt(a3(8), a3(6), cb(7), ALU.is_equal))
                link(stt(a3(9), a3(8), -2.0, a3(4), ALU.mult, ALU.add))
                link(ve.tensor_reduce(c1(10), a3(9), AX_X, ALU.max))
                link(tt(a3(11), a3(9), cb(10), ALU.is_equal))
                link(stt(a3(11), a3(11), -64.0, num, ALU.mult, ALU.add))
                link(ve.tensor_reduce(c1(12), a3(11), AX_X, ALU.min))
                link(tt(a3(11), a3(11), cb(12), ALU.is_equal))
                link(tt(a3(8), a3(8), a3(11), ALU.add))
                link(stt(c1(13), c1(5), eps, c1(10), ALU.add, ALU.add))
                link(ve.reciprocal(c1(13), c1(13)))
                link(stt(a3(8), a3(8), scale, a3(4), ALU.mult, ALU.mult))
                tt(a3(14), a3(8), cb(13), ALU.mult).then_inc(cw_ok, 1)
                dve.wait_ge(ct_done, n + 1)
                ve.tensor_copy(v(A_, A_CT, [1, TOK], rows=e), v(PS, 2 * 512, [1, TOK], rows=e)).then_inc(ct_cp, 1)

            route(0, E0, 1e-6, 0.5)
            dve.wait_ge(rh_cp, 2)
            for half in range(2):
                for a in range(E0 // 2):
                    n = half * 8 + a
                    dve.wait_ge(bc_done, n + 1)
                    tt(wide(A_ if half else M_, (A_Z1 if half else M_U) + a * 512), bank(2 + n % 2),
                       wide(A_, A_RH + half * 512), ALU.mult).then_inc(z_ok, 1)
            for half in range(2):
                for j in range(NJ):
                    n = half * 4 + j
                    dve.wait_ge(y_done, n + 1)
                    o = wide(x1T, j * TOK + half * 512)
                    stt(o, bank(4 + n % 4), biasc[:, j:j + 1], o, ALU.add, ALU.add).then_inc(x1_ok, 1)

            dve.wait_ge(seq_in, 16)
            dve.wait_ge(tab_in, 16)
            dve.wait_ge(pad_out, 16)
            for q in range(4):
                r = dict(p0=S * q, rows=S)
                link(ts(v(idxv, 0, [1, B * 4], **r), v(tabi, q, [4, B * 4], **r), float(PSIZE), ALU.mult, v(cst, C_S, [1, 1], **r), ALU.add))
                link(ve.tensor_copy(v(stat, 40, [1, NT], **r), v(seqi, q, [4, NT], **r)))
            ts(tabi[:, :], tabi[:, :], float(P), ALU.mult, cst[:, C_P:C_P + 1], ALU.add).then_inc(idx_ok, 1)
            link(ts(stat[:, 40:40 + NT], stat[:, 40:40 + NT], cst[:, C_S:C_S + 1], ALU.add))
            link(ve.tensor_copy(seqf[:, :], seqi[:, :]))
            dve.wait_ge(y_done, 8)
            rp = lambda a: v(A_, A_RP + a * 512, [64, NT], [1, 64])
            rw = lambda a: wide(A_, A_RP + a * 512)
            link(tt(rp(4), v(stat, 40, [1, NT], [0, 64]), v(cst, C_IF, [0, NT], [1, 64]), ALU.mult))
            reduce_phase(rw(4), rw(1), rw(0), rope_arg)
            dve.wait_ge(nw_in, 32)
            wq, wk = A_RP + 5 * 512, A_RP + 5 * 512 + D
            link(ts(v(A_, wq, [1, D]), v(A_, wq, [1, D]), SCALE, ALU.mult))
            dve.wait_ge(rope_sin, 2)
            link(tt(rw(3), rw(3), rw(3), ALU.mult))
            link(ts(rw(3), rw(3), -2.0, ALU.mult, 1.0, ALU.add))
            link(ts(rw(4), rw(2), -1.0, ALU.mult))
            for c, w in enumerate((wq, wk)):
                wl, wh = (v(A_, w + 64 * a, [0, NT], [1, 64]) for a in range(2))
                to = lambda a: v(A_, A_TB + c * 256 + a * 64, [512, NT], [1, 64])
                link(tt(to(0), rp(3), wl, ALU.mult))
                link(tt(to(1), rp(3), wh, ALU.mult))
                link(tt(to(2), rp(4), wh, ALU.mult))
                link(tt(to(3), rp(2), wl, ALU.mult))

            dve.wait_ge(x1_out, 16)
            with dve.Fori(0, 4) as i:
                for par in range(2):
                    odd_jobs(i * 2 + 16 + par, lambda j: (wide(M_, i * 1024 + (M_WQ + j * 4096 + par * 512)), bank(j)))

            def norm_tile(t):
                late = not isinstance(t, int)

                def factors(k):
                    n, g = t * 10 + k, k % 2
                    ms, sd = stat[:, g * 4:g * 4 + 4], stat[:, 32 + g * 4:36 + g * 4]
                    y, z = stat[:, 16 + 4 * g:20 + 4 * g], stat[:, 24 + 4 * g:28 + 4 * g]
                    dve.wait_ge(sq_ok, n + 1)
                    ts(ms, ms, 1.0 / D, ALU.mult, EPS, ALU.add).then_inc(ms_ok, 1)
                    if late or k >= 2:
                        dve.wait_ge(sc_ok, n - 1)
                    dve.wait_ge(sd_ok, n + 1)
                    ve.reciprocal(y, sd).then_inc(nw_ok, 1)
                    dve.wait_ge(nw_ok, n * 3 + 1)
                    tt(z, y, y, ALU.mult).then_inc(nw_ok, 1)
                    dve.wait_ge(nw_ok, n * 3 + 2)
                    stt(z, z, -0.5, ms, ALU.mult, ALU.mult).then_inc(nw_ok, 1)
                    dve.wait_ge(nw_ok, n * 3 + 3)
                    stt(y, z, 1.5, y, ALU.add, ALU.mult).then_inc(nf_ok, 1)

                def rotate(k):
                    n, g = t * 10 + k, k % 2
                    dve.wait_ge(sc_ok, n + 1)
                    if late or k >= 2:
                        dve.wait_ge(rt_done, n - 1)
                    if late or k >= 1:
                        dve.wait_ge(rot_ok, n)
                    tb = A_TB + (256 if k >= 8 else 0)
                    tt(v(M_, M_RA + g * 512, [P, 4], [1, P]), v(M_, M_XN + g * 512, [P, 4], [1, P]),
                       v(A_, t * 512 + tb, [0, 4], [1, P]), ALU.mult)
                    for a in range(2):
                        last = tt(v(M_, M_RB + 64 * a, [P, 4], [1, 64]), v(M_, M_XN + g * 512 + 64 - 64 * a, [P, 4], [1, 64]),
                                  v(A_, t * 512 + (tb + P + 64 * a), [0, 4], [1, 64]), ALU.mult)
                    last.then_inc(ab_ok, 1)
                    dve.wait_ge(ab_ok, n + 1)
                    ra = wide(M_, M_RA + g * 512)
                    tt(ra, ra, wide(M_, M_RB), ALU.add).then_inc(rot_ok, 1)

                for k in range(10):
                    factors(k)
                    if k >= 1:
                        rotate(k - 1)
                rotate(9)

            norm_tile(0)
            with dve.Fori(1, NT) as t:
                norm_tile(t)

            for par in range(2):
                dve.wait_ge(st_out[par], 48 * 4)
            with dve.Fori(0, 4) as i:
                for par in range(2):
                    odd_jobs(i * 2 + 24 + par, lambda j: (wide(A_, i * 4096 + (par * 2048 + j * 512)), bank(j)))

            dve.wait_ge(rt_cp, NT * 10)
            dve.wait_ge(v_cp, NT * 2)
            ve.memset(bank(5, P), 0.0).then_inc(pz_ok, 1)
            dve.wait_ge(tp_done, 128)

            mrow = v(M_, M_MR, [1, KEYS])

            def mask_max(t, u, first=False):
                g, k = u % 2, u // HK
                if u == 0:
                    ve.tensor_copy(seqc[:, :], v(seqf, t * BT4, [1, BT4])).then_inc(seqc_ok, 1)
                    dve.wait_ge(seqc_ok, t + 1)
                if u % HK == 0:
                    ts(mrow, v(cst, C_POS, [1, KEYS]), seqc[:, k:k + 1], ALU.is_ge, NEG, ALU.mult).then_inc(mrow_ok, 1)
                    dve.wait_ge(mrow_ok, t * BT4 + k + 1)
                dve.wait_ge(s_done, t * 32 + u + 1)
                if not first or u >= 2:
                    dve.wait_ge(pt_done, t * 32 + u - 1)
                ve.memset(stat[:, 60:61], 0.0)
                ve.tensor_tensor_reduce(v(M_, M_S + g * KEYS, [1, KEYS]), v(PS, g * 1024, [1, KEYS]), mrow, 1.0, -3.0e38,
                                        ALU.add, ALU.max, stat[:, g:g + 1]).then_inc(sm_ok, 1)
                dve.wait_ge(sm_ok, t * 32 + u + 1)
                ts(stat[:, 4 + g:5 + g], stat[:, g:g + 1], -1.0, ALU.mult).then_inc(nm_ok, 1)

            def output_cp(t):
                dve.wait_ge(at_done, t + 1)
                ve.tensor_copy(v(x1T, t * P, [TOK, NJ], [1, P]), v(PS, 7 * 512, [P, NJ], [1, P])).then_inc(at_cp, 1)

            def attend_tile(t, first=False, last_tile=False):
                def normalise(u):
                    g = u % 2
                    dve.wait_ge(e_ok, t * 32 + u + 1)
                    ve.reciprocal(stat[:, 12 + g:13 + g], stat[:, 8 + g:9 + g]).then_inc(rs_ok, 1)
                    dve.wait_ge(rs_ok, t * 32 + u + 1)
                    s = v(M_, M_S + g * KEYS, [1, KEYS])
                    ts(s, s, stat[:, 12 + g:13 + g], ALU.mult).then_inc(p_ok, 1)

                def outputs(u):
                    k, h = u // HK, u % HK
                    dve.wait_ge(o_done, t * 32 + u + 1)
                    if u == 0 and not first:
                        dve.wait_ge(wo_done, t)
                    ve.tensor_copy(v(M_, M_OT + h * REP * P + k * S, [P, REP], [1, S]), v(PS, 6 * 512, [S, REP], [1, S])).then_inc(o_cp, 1)

                for u in range(32):
                    if u + 1 < 32:
                        mask_max(t, u + 1, first)
                    normalise(u)
                    if u == 0 and not first:
                        output_cp(t - 1)
                    if u >= 2:
                        outputs(u - 2)
                outputs(30)
                outputs(31)
                if not last_tile:
                    mask_max(t + 1, 0)

            mask_max(0, 0, True)
            attend_tile(0, first=True)
            with dve.Fori(1, NT - 1) as t:
                attend_tile(t)
            attend_tile(NT - 1, last_tile=True)
            output_cp(NT - 1)

            odd_jobs(32, lambda j: (wide(A_, j * 512), bank(j)))
            odd_jobs(33, lambda j: (wide(A_, 2048 + j * 512), bank(j)))
            route(1, E1, 0.0, 1.0)
            for n in range(8):
                half, a = n // 4, n % 4
                dve.wait_ge(bc_done, 16 + n + 1)
                dve.wait_ge(ha_cp, n + 1)
                tt(wide(M_, M_V + half * 2048 + a * 512), bank(2 + n % 2), wide(A_, A_RH + (n % 2) * 512), ALU.mult).then_inc(z_ok, 1)
            dve.wait_ge(x1_back, 16)
            for t in range(NT):
                dve.wait_ge(ob_done, t + 1)
                o = wide(M_, M_KT + t * HID)
                tt(o, bank(6 + t % 2), o, ALU.add).then_inc(ob_cp, 1)


_INS = ['x', 'itok_B_8_3872', 'itok_Bx16_0_63', 'itok_B_207_1644', 'L0_cond_log_dt', 'L0_cond_C', 'L0_cond_log_A_real',
        'L0_cond_A_imag', 'L0_cond_D', 'L0_ffn_base_w', 'L0_ffn_base_b', 'L0_ffn_A', 'L0_ffn_B', 'L0_ffn_router_w',
        'L1_cond_Wq', 'L1_cond_Wk', 'L1_cond_Wv', 'L1_cond_Wo', 'L1_cond_q_norm_w', 'L1_cond_k_norm_w',
        'L1_cond_k_cache', 'L1_cond_v_cache', 'L1_ffn_gate_w', 'L1_ffn_lora_A', 'L1_ffn_lora_B']
SCRATCH_KIND = "Internal"


def kernel(**inputs):
    import concourse.bacc as _bacc
    from concourse.bass_utils import run_bass_kernel_spmd as _run

    nc = _bacc.Bacc("TRN2", target_bir_lowering=False, num_devices=1)
    arrays, args = {}, []
    for name, a in [*((n, inputs[n]) for n in _INS), ("const", constants())]:
        a = np.ascontiguousarray(a)
        arrays[f"in_{name}"] = a
        args.append(nc.dram_tensor(f"in_{name}", a.shape, mybir.dt.from_np(a.dtype), kind="ExternalInput").ap())
    out = nc.dram_tensor("out_0", (B, S, HID), F32, kind="ExternalOutput").ap()

    def scratch(name, shape):
        return nc.dram_tensor(f"scratch_{name}", shape, F32, kind=SCRATCH_KIND).ap()

    adaln_program(nc, *args, out, scratch)
    r = _run(nc, [arrays], core_ids=[0])
    return r.results[0]["out_0"]
```

```python
from contextlib import ExitStack

import numpy as np

import concourse.bass as bass
from concourse import mybir

ALU = mybir.AluOpType
ACT = mybir.ActivationFunctionType
AX_X = mybir.AxisListType.X
F32 = mybir.dt.float32
F32R = mybir.dt.float32r
I32 = mybir.dt.int32
U32 = mybir.dt.uint32


P = 128
B, S, HID = 32, 32, 512
TOK = B * S
NT = TOK // P
NJ = HID // P
BT4 = P // S
NSTATE = 64
E0, R0 = 16, 64
E1 = 8
D, HQ, HK = 128, 32, 8
PAGES, PSIZE, NPP = 64, 32, 16
L = NPP * PSIZE
KEYS = L + S
KR, KQ = 32, 16
KPAD = 640
SCALE = float(np.float32(1.0 / np.sqrt(D)))
EPS = 1e-6
MAGIC = 12582912.0
TWO_PI_HI = 6.28125
TWO_PI_LO = float(2.0 * np.pi - 6.28125)
INV_TWO_PI = float(1.0 / (2.0 * np.pi))
PI_F = float(np.float32(3.1415925))
LN2_HI = 0.693359375
LN2_LO = float(np.log(2.0) - 0.693359375)
FAR = 1e30

C_ID = 0
C_F = C_ID + P
C_FR = C_F + NJ
C_M = C_FR + NJ
C_S = C_M + KR + KQ
C_P = C_S + 1
C_IF = C_P + 1
C_POS = C_IF + D // 2
C_S0 = C_POS + KEYS
NCONST = C_S0 + (E0 // 2) * P


def constants():
    c = np.zeros((P, NCONST), np.float32)
    p = np.arange(P)
    c[:, C_ID:C_ID + P] = np.eye(P)
    for j in range(NJ):
        c[:, C_F + j] = j * P + p
        c[:, C_FR + j] = j * P + P - 1 - p
    c[:, C_M:C_M + KR] = np.arange(KR)
    c[:, C_M + KR:C_M + KR + KQ] = KR * np.arange(KQ)
    c[:, C_S] = p % S
    c[:, C_P] = p
    half = np.arange(0, D, 2, dtype=np.float32) / np.float32(D)
    c[:, C_IF:C_IF + D // 2] = np.float32(1.0) / np.power(np.float32(10000.0), half)
    c[:, C_POS:C_POS + L] = np.arange(L)
    c[:, C_POS + L:C_POS + KEYS] = -1
    for e in range(E0):
        c[e, C_S0 + e * R0:C_S0 + (e + 1) * R0] = 1
    return c


KB = 256
SLOT = 8 * KB
M_U, M_Y, M_BW, M_BT = 48 * KB, 64 * KB, 80 * KB, 88 * KB
M_W = (16 * KB, 64 * KB)
M_XH, M_TB, M_ST, M_XL = 32 * KB, 48 * KB, 80 * KB, 88 * KB
X_XN, X_RA, X_RB, X_JK = 0, 4 * KB, 8 * KB, 12 * KB
NCH = (HQ + 2 * HK) * D // 512
NROT = (HQ + HK) * D // 512 * NT
NST = NCH * NT
M_END = 114 * KB


def adaln_program(nc, x, len0, table, seqlens, log_dt, Cc, log_A, A_im, Dskip, base_w, base_b, ffnA, ffnB,
                  router_w, Wq, Wk, Wv, Wo, qnw, knw, k_cache, v_cache, gate_w, lora_A, lora_B, const, out, scratch):
    def dap(t, offset, dims):
        return bass.AP(t.tensor, offset, dims)

    kpad, kT, qT, knT, vn, woT, oT, x1d = (scratch(n, s) for n, s in (
        ("kpad", [S, KPAD]),
        ("kT", [PAGES * P, HK * PSIZE]),
        ("qT", [B, P, HQ * S]),
        ("knT", [B, P, HK * S]),
        ("vn", [B, S, HK * D]),
        ("woT", [HQ * D, HID]),
        ("oT", [B, P, HQ * S]),
        ("x1d", [TOK, HID]),
    ))

    with ExitStack() as ctx:
        def sb(name, cols, dt=F32, rows=P):
            return ctx.enter_context(nc.sbuf_tensor(name, [rows, cols], dt))

        def sem(name):
            return ctx.enter_context(nc.semaphore(name))

        cst = sb("cst", NCONST)
        A_ = sb("A_", 64 * KB)
        with ExitStack() as under:
            under.enter_context(nc.sbuf_tensor("slots_", [P, 16 * KB], F32))
            R_ = under.enter_context(nc.sbuf_tensor("R_", [P, M_END - 16 * KB], F32R))
        M_ = sb("M_", M_END)
        x1T = sb("x1T", NJ * TOK)
        small = sb("small", NJ * 152)
        leni = sb("leni", B, I32)
        lenf = sb("lenf", B)
        biasc = sb("biasc", NJ)
        seqi = sb("seqi", B, I32)
        seqf = sb("seqf", B)
        tabi = sb("tabi", B * NPP, I32)
        maskf = tabi[:, 0:NJ * B].bitcast(F32)
        maskr = tabi[:, NJ * B:2 * NJ * B].bitcast(F32)
        idxv = sb("idxv", B * 4, I32)
        idc = sb("idc", 2 * 20, I32)
        seqc = sb("seqc", 2)
        stat = sb("stat", 64)
        PS = ctx.enter_context(nc.psum_tensor("PS", [P, 8 * 512], F32))

        def v(t, offset, *dims, p0=0, rows=P, dt=None):
            pitch = t[:, :].ap[0][0]
            return bass.AP(t, p0 * pitch + offset, [[pitch, rows], *[list(d) for d in dims]])

        def bank(k, cols=512, off=0, rows=P):
            return PS[0:rows, k * 512 + off:k * 512 + off + cols]


        cst_in, len_in, seq_in, tab_in, x_in, par_in, d_in = (sem(n) for n in (
            "cst_in", "len_in", "seq_in", "tab_in", "x_in", "par_in", "d_in"))
        slot_in = [sem("slot_in0"), sem("slot_in1")]
        tp_done = sem("tp_done")
        tp_act, tp_dve = sem("tp_act"), sem("tp_dve")
        kst_out = [sem("kst_out0"), sem("kst_out1")]
        wj_act, wj_dve = sem("wj_act"), sem("wj_dve")
        xh_ok, xl_ok = sem("xh_ok"), sem("xl_ok")
        chain = sem("chain")
        par_t, par_c, exp_arg, exp_ok = (sem(n) for n in ("par_t", "par_c", "exp_arg", "exp_ok"))
        sin_arg, sin_ok = sem("sin_arg"), sem("sin_ok")
        taps_in, taps_ps, taps_cp, taps_sb, pad_out, taps_out = (sem(n) for n in (
            "taps_in", "taps_ps", "taps_cp", "taps_sb", "pad_out", "taps_out"))
        hank_in = [sem(f"hank_in{i}") for i in range(4)]
        xrev_ok = sem("xrev_ok")
        xf_done, xt_done, xf_cp, xr_cp = sem("xf_done"), sem("xt_done"), sem("xf_cp"), sem("xr_cp")
        conv_done, conv_cp = sem("conv_done"), sem("conv_cp")
        lg_done, cw_ok, ct_done, ct_cp = sem("lg_done"), sem("cw_ok"), sem("ct_done"), sem("ct_cp")
        lx_ok, le_ok = sem("lx_ok"), sem("le_ok")
        rh_done, rh_cp, bc_done, z_ok = sem("rh_done"), sem("rh_cp"), sem("bc_done"), sem("z_ok")
        y_done, x1_ok = sem("y_done"), sem("x1_ok")
        r_done, r_cp, x1_out, x1_back = sem("r_done"), sem("r_cp"), sem("x1_out"), sem("x1_back")
        rope_arg, rope_sin, nw_in = sem("rope_arg"), sem("rope_sin"), sem("nw_in")
        pj_done, sq_ok, ms_ok, sc_ok = (sem(n) for n in ("pj_done", "sq_ok", "ms_ok", "sc_ok"))
        sd_ok, nw_ok, nf_ok, rs_ok = sem("sd_ok"), sem("nw_ok"), sem("nf_ok"), sem("rs_ok")
        ab_ok, rot_ok, rt_done, rt_cp, v_cp = (sem(n) for n in ("ab_ok", "rot_ok", "rt_done", "rt_cp", "v_cp"))
        st_out = [sem("st_out0"), sem("st_out1")]
        idx_ok, tr_in = sem("idx_ok"), sem("tr_in")
        k_in, v_in = [sem("k_in0"), sem("k_in1")], [sem("v_in0"), sem("v_in1")]
        q_in, vn_in = [sem("q_in0"), sem("q_in1")], [sem("vn_in0"), sem("vn_in1")]
        idc_ok, mrow_ok, seqc_ok = sem("idc_ok"), sem("mrow_ok"), sem("seqc_ok")
        zero_ok, pz_ok = sem("zero_ok"), sem("pz_ok")
        s_done, sm_ok, e_ok, p_ok = (sem(n) for n in ("s_done", "sm_ok", "e_ok", "p_ok"))
        kh_ok, kl_ok = sem("kh_ok"), sem("kl_ok")
        wo_out, ot_out = sem("wo_out"), [sem("ot_out0"), sem("ot_out1")]
        hg_in = [sem("hg_in0"), sem("hg_in1")]
        hh_ok, hl_ok, hd_done = sem("hh_ok"), sem("hl_ok"), sem("hd_done")
        pt_done, pt_cp, o_done, o_cp = (sem(n) for n in ("pt_done", "pt_cp", "o_done", "o_cp"))
        at_cp = sem("at_cp")
        ha_done, ha_cp, ob_done, ob_cp, out_done = (sem(n) for n in ("ha_done", "ha_cp", "ob_done", "ob_cp", "out_done"))

        def raw(par, k, j, rows=P, t=None):
            return v(M_ if t is None else t, par * SLOT + k * 512 + j * P, [1, P], rows=rows)

        def slot_all(par, t=None):
            return v(M_ if t is None else t, par * SLOT, [512, 4], [1, 512])

        def next_slot(c):
            if isinstance(c, int) and c > 8:
                n = c + 21
                return n, n % 2, (176 if n % 2 == 0 else 120) + 8 * n
            return c * 2 + 13, 1, c * 16 + 224

        def blocks_before(c):
            return 52 + 4 * (c - 8) if isinstance(c, int) and c > 8 else c * 6 + 4

        def rounded(offset, cols=512):
            return v(R_, offset - 16 * KB, [1, cols])

        def spread_part(k, n, cols, rows):
            return v(R_, k * 4 * KB + n, [1, cols], rows=rows)

        def rounded_blocks(offset, n):
            return v(R_, offset - 16 * KB, [S, n], [1, S])

        def rows_of(w, first):
            return dap(w, first * 512, [[512, P], [P * 512, 4], [1, 512]])

        def dst_small(j):
            return small[:, j * 152:(j + 1) * 152]

        def wide(t, offset):
            return v(t, offset, [1, 512])

        A_PC, A_T, A_BIG = 1024, 1280, 2048
        A_EM = A_BIG + 5 * 768
        A_SR = A_BIG + 7 * 768
        A_X = 32 * KB
        A_KQ = 60 * KB
        NX = KR + KQ

        A_Z1, A_RH, A_SM = 0, 44 * KB, 48 * KB
        A_RP = 16 * KB
        A_KS, A_XT = (28 * KB, 56 * KB), 36 * KB
        A_TR = 54 * KB
        KG = 11
        A_KT, KTB, VAL = 0, 17 * 256, ((A_, 34 * KB), (M_, 72 * KB))
        M_S, M_P, M_MR = 0, 2 * KEYS, 2 * KEYS + 2 * 640
        M_OT, M_QT, M_QS = 56 * KB, 104 * KB, 33 * KB
        M_KS, RING = 16 * KB, 4
        A_OG, A_WG, M_HD, M_LA, M_LB = 0, 32 * KB, 16 * KB, 40 * KB, 48 * KB
        M_XB = 72 * KB

        block = ctx.enter_context(nc.Block())

        @block.sync
        def _(sp):
            sp.dma_start(v(A_, 0, [P, 2], [1, P], rows=16), dap(Cc, 0, [[P, 16], [16 * P, 2], [1, P]])).then_inc(par_in, 16)
            sp.dma_start(v(A_, 256, [NSTATE, 2], [1, NSTATE], rows=16), dap(log_A, 0, [[NSTATE, 16], [16 * NSTATE, 2], [1, NSTATE]])).then_inc(par_in, 16)
            sp.dma_start(v(A_, 384, [NSTATE, 2], [1, NSTATE], rows=16), dap(A_im, 0, [[NSTATE, 16], [16 * NSTATE, 2], [1, NSTATE]])).then_inc(par_in, 16)
            with nc.allow_non_contiguous_dma(reason="32 numbers"):
                sp.dma_start(v(A_, 512, [1, 2], rows=16), dap(log_dt, 0, [[1, 16], [16, 2]])).then_inc(par_in, 16)
            sp.dma_start(leni[:, :], dap(len0, 0, [[0, P], [1, B]])).then_inc(len_in, 16)
            sp.dma_start(v(stat, 0, [1, S], rows=1), dap(Dskip, 0, [[S, 1], [1, S]])).then_inc(d_in, 16)

            def slot(par, n, src, t=None):
                if not isinstance(n, int) or n >= 2:
                    sp.wait_ge(tp_done, n * 4 - 4)
                sp.dma_start(slot_all(par, t), src).then_inc(slot_in[par], 16)

            def slot_experts(par, n, w, first, t=None):
                sp.wait_ge(tp_done, n * 4 - 4)
                for e in range(8):
                    sp.dma_start(v(M_ if t is None else t, par * SLOT + e * R0, [512, 4], [1, R0]),
                                 dap(w, (first + e) * HID * R0, [[R0, P], [P * R0, 4], [1, R0]])).then_inc(slot_in[par], 16)

            sp.dma_start(v(M_, 0, [1, 512], rows=R0), ffnA).then_inc(slot_in[0], 16)
            sp.dma_start(v(M_, 0, [1, 512], p0=R0, rows=R0), ffnA).then_inc(slot_in[0], 16)
            sp.dma_start(v(M_, 512, [1, 512], rows=E0), router_w).then_inc(slot_in[0], 16)
            sp.dma_start(v(M_, 512, [1, 512], p0=E0, rows=E1), gate_w).then_inc(slot_in[0], 16)
            slot(1, 1, rows_of(base_w, 0))
            sp.dma_start(v(A_, A_X, [HID, NT], [1, HID]), dap(x, 0, [[HID, P], [P * HID, NT], [1, HID]])).then_inc(x_in, 16)
            for i in range(2):
                slot_experts(i, 2 + i, ffnB, 8 * i)

            def key_load(i, half):
                slot(half, i * 2 + 4 + half,
                     dap(k_cache, i * (512 * HK * D) + half * 512, [[HK * D, P], [P * HK * D, 4], [1, 512]]))

            def key_store(i, half):
                sp.wait_ge(tp_act, i * 4 + (10 + 2 * half))
                sp.wait_ge(tp_dve, i * 4 + (10 + 2 * half))
                sp.dma_start(dap(kT, i * (16 * P * 256) + half * 128, [[256, P], [P * 256, 16], [1, 128]]),
                             v(A_, A_KS[half], [128, 16], [1, 128])).then_inc(kst_out[half], 16)

            key_load(0, 0)
            key_load(0, 1)
            with sp.Fori(0, 3) as i:
                for half in range(2):
                    key_store(i, half)
                    key_load(i + 1, half)

            def queries(b, par, first=False):
                if not first:
                    sp.wait_ge(kl_ok, b * HK - HK)
                sp.dma_start(v(M_, M_QT + par * HQ * S, [1, HQ * S]), dap(qT, b * (P * HQ * S), [[HQ * S, P], [1, HQ * S]])).then_inc(q_in[par], 16)
                sp.dma_start(v(A_, A_KT + par * KTB + L * HK, [1, HK * S]), dap(knT, b * (P * HK * S), [[HK * S, P], [1, HK * S]])).then_inc(q_in[par], 16)
                for s in range(NPP if first else KG, NPP):
                    page = sp.value_load(v(A_, A_TR + s + b * NPP, [1, 1], rows=1).bitcast(I32), min_val=0, max_val=PAGES - 1)
                    sp.dma_start(v(A_, A_KT + par * KTB + s * 256, [1, 256]),
                                 dap(kT, page * (P * 256), [[256, P], [1, 256]])).then_inc(q_in[par], 16)

            def chunk_load(par, n, c):
                w, first = (Wq, c) if not isinstance(c, int) or c < 8 else (Wk, c - 8) if c < 10 else (Wv, c - 10)
                slot(par, n, dap(w, first * (512 * 512), [[512, P], [P * 512, 4], [1, 512]]))

            def wo_load(n, c):
                slot(0, n, dap(Wo, c * 512, [[HQ * D, P], [P * HQ * D, 4], [1, 512]]))

            for half in range(2):
                key_store(3, half)
                chunk_load(half, 12 + half, half)

            sp.wait_ge(r_cp, NT)
            sp.dma_start(dap(x1d, 0, [[HID, P], [P * HID, NT], [1, HID]]), v(A_, A_XT, [HID, NT], [1, HID])).then_inc(x1_out, 16)

            def pair_store(c, q):
                late = isinstance(c, int) and c >= 10
                if late:
                    sp.wait_ge(v_cp, (c - 10) * NT + 2 * q + 2)
                else:
                    sp.wait_ge(rt_cp, c * NT + (2 * q + 2))
                if late:
                    dst = dap(vn, q * (2 * P * HK * D) + (c - 10) * 512, [[HK * D, P], [P * HK * D, 2], [1, 512]])
                elif isinstance(c, int) and c >= 8:
                    dst = dap(knT, q * (8 * P * HK * S) + (c - 8) * 128, [[HK * S, P], [P * HK * S, 8], [1, 128]])
                else:
                    dst = dap(qT, c * 128 + q * (8 * P * HQ * S), [[HQ * S, P], [P * HQ * S, 8], [1, 128]])
                src = v(M_, M_ST + (q % 2) * 1024, *(([512, 2], [1, 512]) if late else ([128, 8], [1, 128])))
                sp.dma_start(dst, src).then_inc(st_out[q % 2], 16)

            def chunk_moves(c, last, load, load_wo=None):
                if last is not None:
                    pair_store(last, 2)
                    pair_store(last, 3)
                    if not isinstance(last, int) or last < 8:
                        sp.wait_ge(wj_act, last * 6 + 10)
                        sp.wait_ge(wj_dve, last * 6 + 10)
                        sp.dma_start(dap(woT, last * (4 * D * HID), [[HID, P], [P * HID, 4], [1, HID]]),
                                     v(A_, last * 2048, [HID, 4], [1, HID])).then_inc(wo_out, 16)
                if load is not None:
                    chunk_load(*load)
                pair_store(c, 0)
                pair_store(c, 1)
                if load_wo is not None:
                    wo_load(*load_wo)

            wo_load(14, 0)
            chunk_moves(0, None, (1, 15, 2), (16, 1))
            chunk_moves(1, 0, (1, 17, 3), (18, 2))
            with sp.Fori(1, 3) as i:
                for a in range(2):
                    chunk_moves(i * 2 + a, i * 2 + (a - 1), (1, i * 4 + (15 + 2 * a), i * 2 + (a + 2)), (i * 4 + (16 + 2 * a), i * 2 + (a + 1)))
            chunk_moves(6, 5, (1, 27, 8), (28, 7))
            chunk_moves(7, 6, (1, 29, 9))
            chunk_moves(8, 7, (0, 30, 10))
            chunk_moves(9, 8, (1, 31, 11))
            chunk_moves(10, 9, None)
            sp.wait_ge(rt_done, NROT)
            slot(0, 32, rows_of(lora_A, 0), x1T)
            slot_experts(1, 33, lora_B, 0, x1T)
            for par in range(2):
                sp.wait_ge(st_out[par], 16 * (NROT // 4 + 1))
            sp.wait_ge(wo_out, 128)
            queries(0, 0, True)
            queries(1, 1, True)
            chunk_moves(11, 10, None)
            pair_store(11, 2)
            pair_store(11, 3)

            for par in range(2):
                sp.wait_ge(st_out[par], 16 * NST // 4)

            def new_values(b, par):
                t, o = VAL[par]
                sp.dma_start(v(t, o + 4096, [1, HK * D], rows=S), dap(vn, b * (S * HK * D), [[HK * D, S], [1, HK * D]])).then_inc(vn_in[par], 16)

            def outputs(b, par):
                sp.wait_ge(o_cp, b * HK + HK)
                sp.dma_start(dap(oT, b * (P * HQ * S), [[HQ * S, P], [1, HQ * S]]), v(M_, M_OT + par * HQ * S, [1, HQ * S])).then_inc(ot_out[par], 16)

            sp.wait_ge(zero_ok, 2)
            sp.wait_ge(x1_out, 16)
            sp.wait_ge(tr_in, 16)
            for par in range(2):
                sp.wait_ge(kst_out[par], 64)
            new_values(0, 0)
            sp.wait_ge(zero_ok, 3)
            new_values(1, 1)
            with sp.Fori(1, B // 2) as i:
                for par in range(2):
                    b = i * 2 + par
                    queries(b, par)
                    sp.wait_ge(o_done, b * HK - HK)
                    outputs(i * 2 + (par - 2), par)
                    new_values(b, par)

            def heads(g, par):
                sp.dma_start(v(A_, A_WG + par * 2048, [HID, 4], [1, HID]),
                             dap(woT, g * (4 * D * HID), [[HID, P], [P * HID, 4], [1, HID]])).then_inc(hg_in[par], 16)
                sp.dma_start(v(A_, A_OG + par * 4096, [128, B - 2], [1, 128]),
                             dap(oT, g * 128, [[HQ * S, P], [P * HQ * S, B - 2], [1, 128]])).then_inc(hg_in[par], 16)

            def heads_end(g, par):
                sp.dma_start(v(A_, A_OG + par * 4096 + 128 * (B - 2), [128, 2], [1, 128]),
                             v(M_, M_OT + g * 128, [HQ * S, 2], [1, 128])).then_inc(hg_in[par], 16)

            sp.wait_ge(wo_out, 128)
            for par in range(2):
                sp.wait_ge(ot_out[par], 16 * (B // 2 - 1))
            sp.wait_ge(kl_ok, B * HK)
            sp.wait_ge(o_done, B * HK - HK)
            heads(0, 0)
            sp.wait_ge(o_cp, B * HK)
            heads_end(0, 0)
            heads(1, 1)
            heads_end(1, 1)
            sp.dma_start(v(M_, M_XB, [HID, NT], [1, HID]), dap(x1d, 0, [[HID, P], [P * HID, NT], [1, HID]])).then_inc(x1_back, 16)
            with sp.Fori(1, HQ // 8) as i:
                for par in range(2):
                    sp.wait_ge(hl_ok, i * 8 + (4 * par - 4))
                    heads(i * 2 + par, par)
                    heads_end(i * 2 + par, par)

            for t in range(NT):
                sp.wait_ge(ob_cp, t + 1)
                sp.dma_start(dap(out, t * P * HID, [[HID, P], [1, HID]]), v(M_, M_XB + t * HID, [1, HID])).then_inc(out_done, 16)
            sp.wait_ge(out_done, 16 * NT)

        @block.gpsimd
        def _(pool):
            pool.dma_start(cst[:, :], const).then_inc(cst_in, 16)
            with nc.allow_non_contiguous_dma(reason="a column of 512 numbers"):
                pool.dma_start(biasc[:, :], dap(base_b, 0, [[1, P], [P, NJ]])).then_inc(cst_in, 16)
            pool.dma_start(seqi[:, :], dap(seqlens, 0, [[0, P], [1, B]])).then_inc(seq_in, 16)

            pool.wait_ge(x_in, 16)
            for t in range(NT):
                nc.gpsimd.tensor_copy(v(M_, M_Y + t * HID, [P, NJ], [1, P]),
                                      v(A_, A_X + t * HID + P - 1, [P, NJ], [-1, P])).then_inc(xrev_ok, 1)

            zeros = idxv[0:S, 0:P - 1].bitcast(F32)
            nc.gpsimd.memset(zeros, 0.0).then_inc(zero_ok, 1)
            pool.wait_ge(zero_ok, 1)
            pool.dma_start(dap(kpad, 0, [[KPAD, S], [1, P - 1]]), zeros).then_inc(pad_out, 16)
            pool.wait_ge(taps_sb, 1)
            pool.dma_start(dap(kpad, P - 1, [[KR, KQ], [KPAD, S], [1, KR]]), v(A_, A_KQ, [KR, S], [1, KR], rows=KQ)).then_inc(taps_out, 16)
            pool.wait_ge(taps_out, 16)
            pool.wait_ge(pad_out, 16)
            for g in range(4):
                if g == 2:
                    pool.wait_ge(xt_done, NT)
                pool.dma_start(v(A_, g * 8 * 512, [512, 8], [1, 512]),
                               dap(kpad, g * 8 * KPAD, [[1, P], [KPAD, 8], [1, 512]])).then_inc(hank_in[g], 16)

            pool.wait_ge(conv_done, 8)
            pool.wait_ge(conv_cp, 8)
            pool.dma_start(tabi[:, :], dap(table, 0, [[0, P], [1, B * NPP]])).then_inc(tab_in, 16)
            pool.dma_start(v(A_, A_RP + 5 * 512, [1, D]), dap(qnw, 0, [[0, P], [1, D]])).then_inc(nw_in, 16)
            pool.dma_start(v(A_, A_RP + 5 * 512 + D, [1, D]), dap(knw, 0, [[0, P], [1, D]])).then_inc(nw_in, 16)

            with pool.Fori(0, NROT // 2) as i:
                for g in range(2):
                    pool.wait_ge(ab_ok, i * 2 + (g + 1))
                    nc.gpsimd.tensor_tensor(wide(x1T, X_RA + g * 512), wide(x1T, X_RA + g * 512),
                                            wide(x1T, X_RB + g * 512), ALU.add).then_inc(rot_ok, 1)

            pool.wait_ge(wo_out, 128)
            pool.dma_start(v(A_, A_TR, [1, B * NPP], rows=1).bitcast(I32), dap(table, 0, [[B * NPP, 1], [1, B * NPP]])).then_inc(tr_in, 16)
            nc.gpsimd.memset(v(A_, VAL[0][1] + 4096, [1, 1024]), 0.0).then_inc(zero_ok, 1)
            for par in range(2):
                pool.wait_ge(kst_out[par], 64)
            pool.wait_ge(idx_ok, 1)

            def gather_keys(b, par, first=False):
                if not first:
                    pool.wait_ge(kl_ok, b * HK - HK)
                    pool.wait_ge(k_in[par], b * (8 * KG) + (16 * (NPP - KG) - 8 * KG * par))
                    pool.wait_ge(v_in[par], b * 32 - 32 * par)
                nc.gpsimd.tensor_copy(idc[:, par * 20:par * 20 + NPP], v(tabi, b * NPP, [1, NPP])).then_inc(idc_ok, 1)
                nc.gpsimd.tensor_copy(idc[:, par * 20 + NPP:par * 20 + 20], v(idxv, b * 4, [1, 4])).then_inc(idc_ok, 1)
                pool.wait_ge(idc_ok, b * 2 + 2)
                nc.gpsimd.tensor_tensor(stat[:, 61:62], cst[:, 0:1], cst[:, 0:1], ALU.add)
                for s in range(NPP if first else KG):
                    nc.gpsimd.indirect_dma_start(
                        v(A_, A_KT + par * KTB + s * 256, [1, 256]), None, kT,
                        bass.IndirectOffsetOnAxis(ap=idc[:, par * 20 + s:par * 20 + s + 1].bitcast(U32), axis=0)).then_inc(k_in[par], 16)

            def gather_values(b, par, first=False):
                if not first:
                    pool.wait_ge(o_done, b * HK - HK)
                    nc.gpsimd.tensor_tensor(stat[:, 62:63], cst[:, 0:1], cst[:, 0:1], ALU.add)
                t, o = VAL[par]
                for s in range(4):
                    nc.gpsimd.indirect_dma_start(
                        v(t, o + s * 1024, [1, 1024]), None, v_cache.rearrange("a b c d -> (a b) (c d)"),
                        bass.IndirectOffsetOnAxis(ap=idc[:, par * 20 + 16 + s:par * 20 + 17 + s].bitcast(U32), axis=0)).then_inc(v_in[par], 16)

            gather_keys(0, 0, True)
            gather_values(0, 0, True)
            gather_keys(1, 1, True)
            pool.wait_ge(pj_done, NST)
            for par in range(2):
                pool.wait_ge(st_out[par], 16 * NST // 4)
            nc.gpsimd.memset(v(M_, VAL[1][1] + 4096, [1, 1024]), 0.0).then_inc(zero_ok, 1)
            gather_values(1, 1, True)
            with pool.Fori(1, B // 2) as i:
                for par in range(2):
                    gather_keys(i * 2 + par, par)
                    gather_values(i * 2 + par, par)

        @block.tensor
        def _(pe):
            def tp(o, i, rows=P):
                return nc.tensor.transpose(o, i, cst[0:rows, C_ID:C_ID + rows])

            def mm(o, l, r, start, stop):
                return nc.tensor.matmul(o, l, r, start=start, stop=stop)

            def slot_jobs(par, n, landed, small_slot=False, before=None, t=None):
                before = n if before is None else before
                pe.wait_ge(slot_in[par], landed)
                for j in range(4):
                    if before:
                        pe.wait_ge((tp_act, tp_dve)[j % 2], before * 2 - 1 + j // 2)
                    for k in range(2 if small_slot else 4):
                        rows = E0 + E1 if small_slot and k else P
                        last = tp(bank(j, rows, k * P), raw(par, k, j, rows, t), rows)
                    last.then_inc(tp_done, 1)

            pe.wait_ge(cst_in, 32)
            pe.wait_ge(par_in, 64)
            pe.wait_ge(par_t, 1)
            i16 = cst[0:16, C_ID:C_ID + 16]
            for c, src in enumerate((v(A_, 256, [1, P], rows=16), v(A_, 576, [1, P], rows=16), v(A_, 384, [1, P], rows=16),
                                     v(A_, 0, [2, P], rows=16), v(A_, 1, [2, P], rows=16))):
                last = nc.tensor.transpose(bank(7, 16, 16 * c), src, i16)
            last.then_inc(par_c, 1)

            slot_jobs(0, 0, 64, small_slot=True)

            pe.wait_ge(taps_in, 1)
            for g in range(2):
                for hh in range(16):
                    o = bank(5 + g, KR, hh * KR, rows=KQ)
                    for c in range(2):
                        last = mm(o, v(A_, A_SR + c * 256 + hh * KQ, [1, KQ], p0=64 * g, rows=64),
                                  v(A_, A_EM + c * 768 + hh * NX, [1, KR], p0=64 * g, rows=64), c == 0, c == 1)
            last.then_inc(taps_ps, 1)

            slot_jobs(1, 1, 16)
            pe.wait_ge(tp_act, 4)
            pe.wait_ge(tp_dve, 4)

            pe.wait_ge(x_in, 16)
            for t in range(NT):
                q = t % 2
                if t >= 2:
                    pe.wait_ge(xf_cp, t - 1)
                for j in range(NJ):
                    last = tp(bank(q, P, j * P), v(A_, A_X + t * HID + j * P, [1, P]))
                last.then_inc(xf_done, 1)
                pe.wait_ge(xrev_ok, t + 1)
                if t >= 2:
                    pe.wait_ge(xr_cp, t - 1)
                for j in range(NJ):
                    last = tp(bank(2 + q, P, j * P), v(M_, M_Y + t * HID + j * P, [1, P]))
                last.then_inc(xt_done, 1)

            pe.wait_ge(xf_cp, NT)
            pe.wait_ge(xr_cp, NT)
            for n, landed in ((2, 192), (3, 144)):
                slot_jobs(n % 2, n, landed)

            for h in range(S):
                g, q = h // 4, h % 4
                if q == 0:
                    if g == 0:
                        pe.wait_ge(taps_sb, 1)
                    if g >= 4:
                        pe.wait_ge(conv_cp, g - 3)
                if h % 8 == 0:
                    pe.wait_ge(hank_in[h // 8], 16)
                for d in range(NJ):
                    last = mm(bank(4 + g % 4, (NJ - d) * B, q * P + d * B),
                              v(A_, h * 512 + d * P, [1, P]),
                              v(M_, M_U + h * B, [TOK, NJ - d], [1, B]), d == 0, d == NJ - 1)
                if q == 3:
                    last.then_inc(conv_done, 1)

            pe.wait_ge(conv_cp, 8)
            for t in range(NT):
                for j in range(NJ):
                    last = mm(bank(4, E0, t * E0), v(M_, M_Y + j * TOK + t * P, [1, P]),
                              v(small, j * 152 + P, [1, E0]), j == 0, j == NJ - 1)
            last.then_inc(lg_done, 1)
            for half in range(2):
                for j in range(NJ):
                    last = mm(bank(5 + half), v(small, j * 152, [1, P]),
                              v(M_, M_Y + j * TOK + half * 512, [1, 512]), j == 0, j == NJ - 1)
                last.then_inc(rh_done, 1)

            def weights_to_experts(n, e):
                pe.wait_ge(cw_ok, n + 1)
                for t in range(NT):
                    last = tp(bank(2 + t // 4, P, (t % 4) * P, rows=e), v(A_, A_SM + 14 * P + t * e, [1, e]))
                last.then_inc(ct_done, 1)

            pe.wait_ge(tp_act, 8)
            pe.wait_ge(tp_dve, 8)

            def base_product(half, j):
                for i in range(NJ):
                    mm(bank(4 + j), v(M_, M_BW + i * 512 + j * P, [1, P]), v(M_, M_Y + i * TOK + half * 512, [1, 512]), i == 0, False)

            def spread_weights(n, half, a, e):
                for part in (1, 2):
                    last = mm(bank(2 + n % 2), spread_part(0, a * P, P, e), spread_part(part, half * 512, 512, e), part == 1, part == 2)
                last.then_inc(bc_done, 1)

            base_product(0, 3)
            pe.wait_ge(lx_ok, 1)
            base_product(0, 0)
            weights_to_experts(0, E0)
            pe.wait_ge(ct_cp, 1)
            for half in range(2):
                for a in range(E0 // 2):
                    n = half * 8 + a
                    if n >= 2:
                        pe.wait_ge(z_ok, n - 1)
                    spread_weights(n, half, a, E0)
            for half in range(2):
                pe.wait_ge(z_ok, half * 8 + 8)
                for j in range(NJ):
                    n = half * 4 + j
                    if n == 0:
                        pe.wait_ge(rh_cp, 2)
                    if n >= 4:
                        pe.wait_ge(x1_ok, n - 3)
                    o = bank(4 + n % 4)
                    if n not in (0, 3):
                        base_product(half, j)
                    for a in range(E0 // 2):
                        last = mm(o, v(M_, M_BT + a * 512 + j * P, [1, P]),
                                  v(A_ if half else M_, (A_Z1 if half else M_U) + a * 512, [1, 512]), False, a == E0 // 2 - 1)
                    last.then_inc(y_done, 1)
                    if n == 0:
                        pe.wait_ge(z_ok, 16)
                    slot_jobs(n % 2, 4 + n, (208 if n % 2 == 0 else 152) + 8 * n)

            def weight_job(par, j, landed, act=None, dve=None):
                if j == 0:
                    pe.wait_ge(slot_in[par], landed)
                if act is not None:
                    pe.wait_ge(wj_act, act)
                    pe.wait_ge(wj_dve, dve)
                for k in range(4):
                    last = tp(bank(4 + j % 2, P, k * P), raw(par, k, j))
                last.then_inc(tp_done, 1)

            pe.wait_ge(x1_ok, 8)
            for j in range(4):
                weight_job(0, j, 272, *((j - 1, j - 1) if j >= 2 else ()))
            for t in range(NT):
                if t >= 2:
                    pe.wait_ge(r_cp, t - 1)
                for j in range(NJ):
                    last = tp(bank(6 + t % 2, P, j * P), v(x1T, j * TOK + t * P, [1, P]))
                last.then_inc(r_done, 1)

            pe.wait_ge(r_cp, NT)
            pe.wait_ge(tp_act, 24)
            pe.wait_ge(tp_dve, 24)
            pe.wait_ge(xl_ok, 1)

            def turn(s, g, first):
                pe.wait_ge(rot_ok, s + 1)
                if not first:
                    pe.wait_ge(rt_cp, s - 1)
                for a in range(4):
                    last = tp(bank(6 + g, P, a * P), v(x1T, X_RA + g * 512 + a * P, [1, P]))
                last.then_inc(rt_done, 1)

            def project_chunk(c, par):
                known = isinstance(c, int)
                base = blocks_before(c)
                for t in range(NT):
                    s = c * NT + t
                    if t == 0:
                        ready = base if known and (c == 0 or c > 8) else base - 2
                        pe.wait_ge(wj_act, ready)
                        pe.wait_ge(wj_dve, ready)
                    if known and s - 4 >= NROT:
                        pe.wait_ge(v_cp, s - 3 - NROT)
                    elif not known or s >= 4:
                        pe.wait_ge(sc_ok, s - 3)
                    for j in range(NJ):
                        xh, xl = (rounded(a + j * TOK + t * P, P) for a in (M_XH, M_XL))
                        wh, wl = (rounded(M_W[par] + a + j * 512) for a in (0, 8 * KB))
                        mm(bank(t % 4), xh, wh, j == 0, False)
                        mm(bank(t % 4), xh, wl, False, False)
                        last = mm(bank(t % 4), xl, wh, False, j == NJ - 1)
                    last.then_inc(pj_done, 1)
                    if not known or 0 <= s - 3 < NROT:
                        turn(s - 3, (t + 1) % 2, known and s < 5)
                    if t < 4 and not (known and c == NCH - 1):
                        b = base + max(0, t - 1)
                        weight_job(next_slot(c)[1], t, next_slot(c)[2], b, b)
                    if t >= 4 and (not known or c < 8):
                        b = (3, 4, 5, 5)[t - 4]
                        weight_job(0, t - 4, c * 16 + 288, base + b, base + (4 if t == 6 else b))

            project_chunk(0, 0)
            project_chunk(1, 1)
            with pe.Fori(1, 4) as i:
                project_chunk(i * 2, 0)
                project_chunk(i * 2 + 1, 1)
            for c in range(8, NCH):
                project_chunk(c, c % 2)

            pe.wait_ge(sc_ok, NROT)
            pe.wait_ge(v_cp, NST - NROT)
            pe.wait_ge(rt_cp, NROT)
            pe.wait_ge(pz_ok, 1)

            def scores(i, u):
                n = i * 16 + u
                pe.wait_ge(kl_ok, n + 1)
                if not isinstance(n, int) or n >= 2:
                    pe.wait_ge(sm_ok, n - 1)
                qh, ql = (rounded(M_QS + (u % RING) * 2 * P + a, P) for a in (0, P))
                for o, first, cols in ((bank(2 * (u % 2), 9 * S, 512 - 9 * S), 0, 9 * S), (bank(2 * (u % 2) + 1, 8 * S), 9 * S, 8 * S)):
                    kh, kl = (rounded(M_KS + (u % RING) * 2 * KEYS + a + first, cols) for a in (0, KEYS))
                    mm(o, qh, kh, True, False)
                    mm(o, qh, kl, False, False)
                    last = mm(o, ql, kh, False, True)
                last.then_inc(s_done, 1)

            def turn(i, u):
                n = i * 16 + u
                pe.wait_ge(p_ok, n + 1)
                if not isinstance(n, int) or n >= 1:
                    pe.wait_ge(pt_cp, n)
                for c in range(4):
                    tp(bank(4, P, c * P), v(M_, M_S + (u % 2) * KEYS + c * P, [1, P]))
                tp(bank(5, P, 0, rows=S), v(M_, M_S + (u % 2) * KEYS + L, [1, S])).then_inc(pt_done, 1)

            def values(i, u):
                n = i * 16 + u
                par, h = (u // HK) % 2, u % HK
                if h == 0:
                    pe.wait_ge(v_in[par], i * 64 + 64)
                    pe.wait_ge(vn_in[par], i * 16 + 16)
                pe.wait_ge(pt_cp, n + 1)
                if not isinstance(n, int) or n >= 2:
                    pe.wait_ge(o_cp, n - 1)
                t, o = VAL[par]
                for c in range(5):
                    last = mm(bank(6 + u % 2, P), v(t, o + c * 1024 + h * D, [1, D]),
                              v(M_, M_P + (u % 2) * 640 + c * P, [1, P]), c == 0, c == 4)
                last.then_inc(o_done, 1)

            def two_batches(i):
                for u in range(16):
                    n = i * 16 + u
                    if not isinstance(n, int) or n + 2 < B * HK:
                        scores(i, u + 2)
                    turn(i, u)
                    if u >= 1:
                        values(i, u - 1)
                    elif not isinstance(i, int) or i >= 1:
                        values(i - 1, 15)

            scores(0, 0)
            scores(0, 1)
            two_batches(0)
            with pe.Fori(1, B // 2 - 1) as i:
                two_batches(i)
            two_batches(B // 2 - 1)
            values(B // 2 - 1, 15)

            slot_jobs(0, 32, 432, before=12, t=x1T)
            slot_jobs(1, 33, 496, before=13, t=x1T)

            pe.wait_ge(o_cp, B * HK)
            pe.wait_ge(tp_act, 28)
            pe.wait_ge(tp_dve, 28)

            def project_head(m, r, start, stop):
                pe.wait_ge(hl_ok, m + 1)
                wh, wl, oh, ol = (M_HD + r * 3072 + a for a in (0, 512, 1024, 2048))
                for j in range(NJ):
                    for half in range(2):
                        o = bank(j * 2 + half)
                        mm(o, rounded(wh + j * P, P), rounded(oh + half * 512), start, False)
                        mm(o, rounded(wl + j * P, P), rounded(oh + half * 512), False, False)
                        last = mm(o, rounded(wh + j * P, P), rounded(ol + half * 512), False, stop)
                last.then_inc(hd_done, 1)

            project_head(0, 0, True, False)
            project_head(1, 1, False, False)
            with pe.Fori(1, HQ // 2 - 1) as i:
                for r in range(2):
                    project_head(i * 2 + r, r, False, False)
            project_head(HQ - 2, 0, False, False)
            project_head(HQ - 1, 1, False, True)

            pe.wait_ge(at_cp, 8)
            for t in range(NT):
                for j in range(NJ):
                    last = mm(bank(4, E1, t * E1), v(x1T, j * TOK + t * P, [1, P]),
                              v(small, j * 152 + P + E0, [1, E1]), j == 0, j == NJ - 1)
            last.then_inc(lg_done, 1)

            def ranks(n):
                for j in range(NJ):
                    last = mm(bank(5 + n % 2), v(M_, M_LA + j * 512 + (n % 4) * P, [1, P]),
                              v(x1T, j * TOK + (n // 4) * 512, [1, 512]), j == 0, j == NJ - 1)
                last.then_inc(ha_done, 1)

            ranks(0)
            ranks(1)
            weights_to_experts(1, E1)
            pe.wait_ge(ct_cp, 2)
            for half in range(2):
                for a in range(E1 // 2):
                    n = half * 4 + a
                    if n >= 2:
                        pe.wait_ge(z_ok, 16 + n - 1)
                        ranks(n)
                    spread_weights(n, half, a, E1)
            for t in range(NT):
                half = t // 4
                pe.wait_ge(z_ok, 16 + half * 4 + 4)
                if t >= 2:
                    pe.wait_ge(ob_cp, t - 1)
                for a in range(E1 // 2):
                    last = mm(bank(t % 2), v(A_, half * 2048 + a * 512 + (t % 4) * P, [1, P]),
                              v(M_, M_LB + a * 512, [1, 512]), a == 0, a == E1 // 2 - 1)
                last.then_inc(ob_done, 1)

        @block.scalar
        def _(act):
            def copy(o, i):
                return nc.scalar.activation(o, i, ACT.Copy)

            def even_jobs(n, dst):
                for j in (0, 2):
                    act.wait_ge(tp_done, n * 4 + j + 1)
                    copy(*dst(j)).then_inc(tp_act, 1)

            act.wait_ge(exp_arg, 1)
            nc.scalar.activation(v(A_, A_BIG + 4 * 768, [1, 768]), v(A_, A_BIG + 4 * 768, [1, 768]), ACT.Exp).then_inc(exp_ok, 1)
            act.wait_ge(sin_arg, 1)
            nc.scalar.activation(v(A_, A_BIG + 768, [1, 768]), v(A_, A_BIG + 3 * 768, [1, 768]), ACT.Sin).then_inc(sin_ok, 1)
            nc.scalar.activation(v(A_, A_BIG + 2 * 768, [1, 768]), v(A_, A_BIG + 3 * 768, [1, 768]), ACT.Sin, scale=0.5).then_inc(sin_ok, 1)
            even_jobs(0, lambda j: (dst_small(j), bank(j, 152)))
            act.wait_ge(taps_ps, 1)
            copy(v(A_, A_KQ, [1, S * KR], rows=KQ), v(PS, 5 * 512, [1, S * KR], rows=KQ)).then_inc(taps_cp, 1)
            even_jobs(1, lambda j: (wide(M_, M_BW + j * 512), bank(j)))

            for t in range(NT):
                act.wait_ge(xf_done, t + 1)
                copy(v(x1T, t * P, [TOK, NJ], [1, P]), v(PS, (t % 2) * 512, [P, NJ], [1, P])).then_inc(xf_cp, 1)

            for i in range(2):
                even_jobs(2 + i, lambda j: (wide(M_, M_BT + (4 * i + j) * 512), bank(j)))

            def stage_keys(m):
                half = m % 2
                if m >= 2:
                    act.wait_ge(kst_out[half], 16 * (m // 2))
                even_jobs(4 + m, lambda j: (v(A_, A_KS[half] + j * S, [128, 16], [1, S]), v(PS, j * 512, [S, 16], [1, S])))

            def exp_logits(n, e):
                act.wait_ge(lx_ok, n + 1)
                nc.scalar.activation(v(A_, A_SM + P, [1, NT * e]), v(A_, A_SM, [1, NT * e]), ACT.Exp).then_inc(le_ok, 1)

            for half in range(2):
                act.wait_ge(rh_done, half + 1)
                copy(wide(A_, A_RH + half * 512), bank(5 + half)).then_inc(rh_cp, 1)
            exp_logits(0, E0)
            act.wait_ge(rope_arg, 1)
            nc.scalar.activation(wide(A_, A_RP + 1024), wide(A_, A_RP), ACT.Sin).then_inc(rope_sin, 1)
            nc.scalar.activation(wide(A_, A_RP + 1536), wide(A_, A_RP), ACT.Sin, scale=0.5).then_inc(rope_sin, 1)
            for n in range(8):
                act.wait_ge(x1_ok, n + 1)
                o = (n % 4) * TOK + (n // 4) * 512
                copy(rounded(M_XH + o), wide(x1T, o)).then_inc(xh_ok, 1)
                stage_keys(n)

            def chunk_job(n, par, j):
                act.wait_ge(tp_done, n * 4 + (j + 1))
                copy(rounded(M_W[par] + j * 512), bank(4 + j % 2)).then_inc(wj_act, 1)

            for j in range(4):
                chunk_job(12, 0, j)
            for t in range(NT):
                act.wait_ge(r_done, t + 1)
                copy(wide(A_, A_XT + t * HID), bank(6 + t % 2)).then_inc(r_cp, 1)

            def project_chunk(c, par):
                known = isinstance(c, int)

                def normalise(s, g, b, early):
                    act.wait_ge(nf_ok, s + 1)
                    if not early:
                        act.wait_ge(ab_ok, s - 1)
                    for a in range(4):
                        last = nc.scalar.activation(v(x1T, X_XN + g * 512 + a * P, [1, P]), bank(b, P, a * P), ACT.Copy,
                                                    scale=stat[:, 16 + g * 4 + a:17 + g * 4 + a])
                    last.then_inc(sc_ok, 1)

                def stage_free(cc, t):
                    if t % 2 == 0 and not (isinstance(cc, int) and cc == 0 and t < 4):
                        act.wait_ge(st_out[(t // 2) % 2], cc * 32 + 16 * (t // 4))

                def turned(s, cc, t):
                    act.wait_ge(rt_done, s + 1)
                    stage_free(cc, t)
                    copy(v(M_, M_ST + ((t // 2) % 2) * 1024 + (t % 2) * 512, [P, 4], [S, 4], [1, S]),
                         v(PS, (6 + t % 2) * 512, [S, 4], [P, 4], [1, S])).then_inc(rt_cp, 1)

                for t in range(NT):
                    s, g = c * NT + t, t % 2
                    act.wait_ge(pj_done, s + 1)
                    if not known or s < NROT:
                        if not known or s >= 2:
                            act.wait_ge(nf_ok, s - 1)
                        if not known or s >= 1:
                            act.wait_ge(ms_ok, s)
                        for a in range(4):
                            last = nc.scalar.activation(v(x1T, X_JK + a * P, [1, P]), bank(t % 4, P, a * P), ACT.Square,
                                                        accum_out=stat[:, g * 4 + a:g * 4 + a + 1])
                        last.then_inc(sq_ok, 1)
                        act.wait_ge(ms_ok, s + 1)
                        nc.scalar.activation(stat[:, 32 + g * 4:36 + g * 4], stat[:, g * 4:g * 4 + 4], ACT.Sqrt).then_inc(sd_ok, 1)
                    if not known or 0 <= s - 1 < NROT:
                        normalise(s - 1, 1 - g, (t - 1) % 4, known and s < 3)
                    if not known or 0 <= s - 3 < NROT:
                        turned(s - 3, c if t >= 3 else c - 1, (t - 3) % NT)
                    if known and s >= NROT:
                        stage_free(c, t)
                        copy(wide(M_, M_ST + ((t // 2) % 2) * 1024 + (t % 2) * 512), bank(t % 4)).then_inc(v_cp, 1)
                    if t < 4 and not (known and c == NCH - 1):
                        chunk_job(next_slot(c)[0], 1 - par, t)
                    if t >= 4 and (not known or c < 8) and t % 2 == 0:
                        act.wait_ge(tp_done, c * 8 + (56 + t - 3))
                        copy(wide(A_, c * 2048 + (t - 4) * 512), bank(4)).then_inc(wj_act, 1)

            project_chunk(0, 0)
            project_chunk(1, 1)
            act.wait_ge(x1_out, 16)
            for half in range(2):
                act.wait_ge(kst_out[half], 64)
            with act.Fori(1, 4) as i:
                project_chunk(i * 2, 0)
                project_chunk(i * 2 + 1, 1)
            for c in range(8, NCH):
                project_chunk(c, c % 2)

            QIN = 16 * (2 + NPP - KG)

            def split(i, u):
                n = i * 16 + u
                par, h = (u // HK) % 2, u % HK
                known = isinstance(n, int)
                if h == 0:
                    ii = i + u // 16
                    act.wait_ge(k_in[par], ii * (16 * KG) + 16 * NPP)
                    act.wait_ge(q_in[par], ii * QIN + 32)
                if not known or n >= RING:
                    act.wait_ge(s_done, n - (RING - 1))
                copy(rounded(M_QS + (u % RING) * 2 * P, P), v(M_, M_QT + par * HQ * S + h * P, [1, P]))
                copy(rounded_blocks(M_KS + (u % RING) * 2 * KEYS, KEYS // S),
                     v(A_, A_KT + par * KTB + h * S, [256, KEYS // S], [1, S])).then_inc(kh_ok, 1)

            def expo(i, u):
                g = u % 2
                act.wait_ge(sm_ok, i * 16 + u + 1)
                s = v(M_, M_S + g * KEYS, [1, KEYS])
                nc.scalar.activation(s, s, ACT.Exp, bias=stat[:, g:1 + g], scale=-1.0, accum_out=stat[:, 8 + g:9 + g]).then_inc(e_ok, 1)

            def turned(i, u):
                n = i * 16 + u
                act.wait_ge(pt_done, n + 1)
                if not isinstance(n, int) or n >= 2:
                    act.wait_ge(o_done, n - 1)
                copy(v(M_, M_P + (u % 2) * 640, [1, 640]), v(PS, 4 * 512, [1, 640])).then_inc(pt_cp, 1)

            def output(i, u):
                u, i = (u, i) if u >= 0 else (u + 16, i - 1)
                par, h = (u // HK) % 2, u % HK
                act.wait_ge(o_done, i * 16 + u + 1)
                if h == 0 and not (isinstance(i, int) and i == 0):
                    act.wait_ge(ot_out[par], i * 16)
                copy(v(M_, M_OT + par * HQ * S + h * P, [1, P]), bank(6 + u % 2, P)).then_inc(o_cp, 1)

            def two_batches(i):
                known = isinstance(i, int)
                for u in range(16):
                    if not known or i * 16 + u + 1 < B * HK:
                        expo(i, u + 1)
                    if not known or i * 16 + u >= 2:
                        output(i, u - 2)
                    turned(i, u)
                    if not known or i * 16 + u + RING < B * HK:
                        split(i, u + RING)

            for u in range(RING):
                split(0, u)
            expo(0, 0)
            two_batches(0)
            with act.Fori(1, B // 2 - 1) as i:
                two_batches(i)
            two_batches(B // 2 - 1)
            output(B // 2 - 1, 14)
            output(B // 2 - 1, 15)

            even_jobs(32, lambda j: (wide(M_, M_LA + j * 512), bank(j)))
            even_jobs(33, lambda j: (wide(M_, M_LB + j * 512), bank(j)))

            def round_head(g, par, hh, first=False):
                m, r = g * 4 + hh, hh % 2
                if hh == 0:
                    act.wait_ge(hg_in[par], (g - par) * 24 + 48)
                if not first:
                    act.wait_ge(hd_done, m - 1)
                o = M_HD + r * 3072
                copy(rounded(o), wide(A_, A_WG + par * 2048 + hh * 512)).then_inc(hh_ok, 1)
                copy(rounded_blocks(o + 1024, B), v(A_, A_OG + par * 4096 + hh * S, [128, B], [1, S])).then_inc(hh_ok, 1)

            for par in range(2):
                for hh in range(4):
                    round_head(par, par, hh, par == 0 and hh < 2)
            with act.Fori(1, HQ // 8) as i:
                for par in range(2):
                    for hh in range(4):
                        round_head(i * 2 + par, par, hh)
            act.wait_ge(hd_done, HQ)
            for k in (0, 2, 4, 6):
                copy(wide(x1T, k * 512), bank(k)).then_inc(at_cp, 1)

            exp_logits(1, E1)
            for n in range(8):
                act.wait_ge(ha_done, n + 1)
                if n >= 2:
                    act.wait_ge(z_ok, 16 + n - 1)
                copy(wide(A_, A_RH + (n % 2) * 512), bank(5 + n % 2)).then_inc(ha_cp, 1)

        @block.vector
        def _(dve):
            steps = [0]
            ve = nc.vector

            def link(ins):
                steps[0] += 1
                ins.then_inc(chain, 1)
                dve.wait_ge(chain, steps[0])

            def stt(o, a, s, b, op0, op1):
                return ve.scalar_tensor_tensor(out=o, in0=a, scalar=s, in1=b, op0=op0, op1=op1)

            def tt(o, a, b, op):
                return ve.tensor_tensor(o, a, b, op)

            def ts(o, a, s1, op0, s2=None, op1=None):
                return ve.tensor_scalar(o, a, s1, s2, op0, op1) if op1 is not None else ve.tensor_scalar(o, a, s1, None, op0)

            def exp_exact(dst, src, n, t0):
                y, k, r, q, p2 = (v(A_, A_T + t0 + 32 * a, [1, n]) for a in range(5))
                link(ts(y, src, 1.4426950408889634, ALU.mult, MAGIC, ALU.add))
                link(ts(k, y, MAGIC, ALU.subtract, -126.0, ALU.max))
                link(stt(r, k, -LN2_HI, src, ALU.mult, ALU.add))
                link(stt(r, k, -LN2_LO, r, ALU.mult, ALU.add))
                link(ts(q, r, 1.0 / 5040, ALU.mult))
                for c in (1.0 / 720, 1.0 / 120, 1.0 / 24, 1.0 / 6, 0.5, 1.0):
                    link(stt(q, q, c, r, ALU.add, ALU.mult))
                link(ts(v(A_, A_T + t0 + 32 * 4, [1, n]).bitcast(I32), k, 127.0, ALU.add, float(2 ** 23), ALU.mult))
                link(stt(dst, q, 1.0, p2, ALU.add, ALU.mult))

            def reduce_phase(ph, y, r, done):
                link(ts(y, ph, INV_TWO_PI, ALU.mult, MAGIC, ALU.add))
                link(ts(y, y, MAGIC, ALU.subtract))
                link(stt(r, y, -TWO_PI_HI, ph, ALU.mult, ALU.add))
                link(stt(r, y, -TWO_PI_LO, r, ALU.mult, ALU.add))
                ts(r, r, PI_F, ALU.min, -PI_F, ALU.max).then_inc(done, 1)

            dve.wait_ge(par_in, 64)
            ve.tensor_copy(v(A_, 576, [NSTATE, 2], [1, NSTATE], rows=16), v(A_, 512, [1, 2], [0, NSTATE], rows=16)).then_inc(par_t, 1)

            tf = tabi[:, :].bitcast(F32)

            def mk(offset, *dims):
                return bass.AP(tf.tensor, offset, [[tf.ap[0][0], P], *[list(d) for d in dims]])

            dve.wait_ge(cst_in, 32)
            dve.wait_ge(par_c, 1)
            pc = lambda c, n=16: v(A_, A_PC + 16 * c, [1, n])
            tmp = lambda a, n=16: v(A_, A_T + 32 * a, [1, n])
            big = lambda a: v(A_, A_BIG + 768 * a, [1, 768])
            big3 = lambda a: v(A_, A_BIG + 768 * a, [NX, 16], [1, NX])
            link(ve.tensor_copy(pc(0, 80), bank(7, 80)))
            exp_exact(tmp(5, 32), pc(0, 32), 32, 0)
            ar, dt, zr, zi = tmp(5), v(A_, A_T + 32 * 5 + 16, [1, 16]), tmp(6), tmp(7)
            link(ts(ar, ar, -1.0, ALU.mult))
            link(tt(zr, ar, dt, ALU.mult))
            link(tt(zi, pc(2), dt, ALU.mult))
            over = lambda a: v(A_, A_T + 32 * a, [1, 16], [0, NX])
            steps3 = v(cst, C_M, [0, 16], [1, NX])
            tt(big3(4), over(6), steps3, ALU.mult).then_inc(exp_arg, 1)
            link(tt(big3(0), over(7), steps3, ALU.mult))
            reduce_phase(big(0), big(1), big(3), sin_arg)
            exp_exact(tmp(9), zr, 16, 0)
            dve.wait_ge(sin_ok, 2)
            s1 = v(A_, A_BIG + 768 + 1, [NX, 16])
            h1 = v(A_, A_BIG + 2 * 768 + 1, [NX, 16])
            link(tt(tmp(10), h1, h1, ALU.mult))
            link(tt(tmp(10), tmp(10), tmp(9), ALU.mult))
            link(ts(tmp(11), tmp(9), 1.0, ALU.subtract))
            link(stt(tmp(10), tmp(10), -2.0, tmp(11), ALU.mult, ALU.add))
            link(tt(tmp(11), s1, tmp(9), ALU.mult))
            link(tt(tmp(12), pc(3), tmp(10), ALU.mult))
            link(tt(tmp(13), pc(4), tmp(11), ALU.mult))
            link(tt(tmp(12), tmp(12), tmp(13), ALU.subtract))
            link(tt(tmp(13), pc(3), tmp(11), ALU.mult))
            link(tt(tmp(14), pc(4), tmp(10), ALU.mult))
            link(tt(tmp(13), tmp(13), tmp(14), ALU.add))
            link(tt(tmp(14), ar, ar, ALU.mult))
            link(tt(tmp(15), pc(2), pc(2), ALU.mult))
            link(tt(tmp(14), tmp(14), tmp(15), ALU.add))
            link(ve.reciprocal(tmp(14), tmp(14)))
            link(ts(tmp(14), tmp(14), 2.0, ALU.mult))
            link(tt(tmp(15), tmp(12), ar, ALU.mult))
            link(tt(tmp(16), tmp(13), pc(2), ALU.mult))
            link(tt(tmp(15), tmp(15), tmp(16), ALU.add))
            link(tt(tmp(15), tmp(15), tmp(14), ALU.mult))
            link(tt(tmp(16), tmp(12), pc(2), ALU.mult))
            link(tt(tmp(17), tmp(13), ar, ALU.mult))
            link(tt(tmp(16), tmp(16), tmp(17), ALU.subtract))
            link(tt(tmp(16), tmp(16), tmp(14), ALU.mult))
            link(tt(big(2), big(2), big(2), ALU.mult))
            link(ts(big(2), big(2), -2.0, ALU.mult, 1.0, ALU.add))
            dve.wait_ge(exp_ok, 1)
            link(tt(big(5), big(2), big(4), ALU.mult))
            link(stt(big(6), big(1), -1.0, big(4), ALU.mult, ALU.mult))
            qre = v(A_, A_BIG + 5 * 768 + KR, [NX, 16], [1, KQ])
            qni = v(A_, A_BIG + 6 * 768 + KR, [NX, 16], [1, KQ])
            sre, sni = (v(A_, A_T + 32 * a, [1, 16], [0, KQ]) for a in (15, 16))
            w0, w1 = v(A_, A_BIG, [KQ, 16], [1, KQ]), v(A_, A_BIG + 256, [KQ, 16], [1, KQ])
            fre, fni = v(A_, A_SR, [KQ, 16], [1, KQ]), v(A_, A_SR + 256, [KQ, 16], [1, KQ])
            link(tt(w0, qre, sre, ALU.mult))
            link(tt(w1, qni, sni, ALU.mult))
            link(tt(fre, w0, w1, ALU.subtract))
            link(tt(w0, qni, sre, ALU.mult))
            link(tt(w1, qre, sni, ALU.mult))
            link(tt(w0, w0, w1, ALU.add))
            ts(fni, w0, -1.0, ALU.mult).then_inc(taps_in, 1)
            def odd_jobs(n, dst):
                for j in (1, 3):
                    dve.wait_ge(tp_done, n * 4 + j + 1)
                    ve.tensor_copy(*dst(j)).then_inc(tp_dve, 1)

            odd_jobs(0, lambda j: (dst_small(j), bank(j, 152)))

            dve.wait_ge(len_in, 16)
            dve.wait_ge(cst_in, 32)
            link(ve.tensor_copy(lenf[:, :], leni[:, :]))
            for j in range(NJ):
                link(ts(maskf[:, j * B:(j + 1) * B], lenf[:, :], cst[:, C_F + j:C_F + j + 1], ALU.is_gt))
                link(ts(maskr[:, j * B:(j + 1) * B], lenf[:, :], cst[:, C_FR + j:C_FR + j + 1], ALU.is_gt))

            dve.wait_ge(taps_cp, 1)
            dve.wait_ge(d_in, 16)
            k0 = v(A_, A_KQ, [KR, S], rows=1)
            tt(k0, k0, v(stat, 0, [1, S], rows=1), ALU.add).then_inc(taps_sb, 1)

            odd_jobs(1, lambda j: (wide(M_, M_BW + j * 512), bank(j)))

            for t in range(NT):
                dve.wait_ge(xt_done, t + 1)
                for j in range(NJ):
                    last = tt(v(M_, M_U + j * TOK + t * BT4, [1, BT4], [B, S]), v(PS, (2 + t % 2) * 512 + j * P, [S, BT4], [1, S]),
                              mk(NJ * B + j * B + t * BT4, [1, BT4], [0, S]), ALU.mult)
                last.then_inc(xr_cp, 1)

            for i in range(2):
                odd_jobs(2 + i, lambda j: (wide(M_, M_BT + (4 * i + j) * 512), bank(j)))

            def stage_keys(m):
                half = m % 2
                if m >= 2:
                    dve.wait_ge(kst_out[half], 16 * (m // 2))
                odd_jobs(4 + m, lambda j: (v(A_, A_KS[half] + j * S, [128, 16], [1, S]), v(PS, j * 512, [S, 16], [1, S])))

            dve.wait_ge(xt_done, NT)
            for g in range(8):
                dve.wait_ge(conv_done, g + 1)
                for q in range(4):
                    last = tt(v(M_, M_Y + g * 4 + q, [TOK, NJ], [S, B]), v(PS, (4 + g % 4) * 512 + q * P, [B, NJ], [1, B]),
                              mk(0, [B, NJ], [1, B]), ALU.mult)
                last.then_inc(conv_cp, 1)

            def route(n, e, eps, scale):
                a3 = lambda i: v(A_, A_SM + P * i, [e, NT], [1, e])
                c1 = lambda i: v(A_, A_SM + P * i, [1, NT])
                cb = lambda i: v(A_, A_SM + P * i, [1, NT], [0, e])
                num = v(cst, C_M, [0, NT], [1, e])
                dve.wait_ge(lg_done, n + 1)
                lg = v(PS, 4 * 512, [e, NT], [1, e])
                link(ve.tensor_reduce(c1(2), lg, AX_X, ALU.max))
                tt(a3(0), lg, cb(2), ALU.subtract).then_inc(lx_ok, 1)
                dve.wait_ge(le_ok, n + 1)
                link(ve.tensor_reduce(c1(3), a3(1), AX_X, ALU.add))
                link(ve.reciprocal(c1(3), c1(3)))
                link(tt(a3(4), a3(1), cb(3), ALU.mult))
                link(ve.tensor_reduce(c1(5), a3(4), AX_X, ALU.max))
                link(tt(a3(6), a3(4), cb(5), ALU.is_equal))
                link(stt(a3(6), a3(6), -64.0, num, ALU.mult, ALU.add))
                link(ve.tensor_reduce(c1(7), a3(6), AX_X, ALU.min))
                link(tt(a3(8), a3(6), cb(7), ALU.is_equal))
                link(stt(a3(9), a3(8), -2.0, a3(4), ALU.mult, ALU.add))
                link(ve.tensor_reduce(c1(10), a3(9), AX_X, ALU.max))
                link(tt(a3(11), a3(9), cb(10), ALU.is_equal))
                link(stt(a3(11), a3(11), -64.0, num, ALU.mult, ALU.add))
                link(ve.tensor_reduce(c1(12), a3(11), AX_X, ALU.min))
                link(tt(a3(11), a3(11), cb(12), ALU.is_equal))
                link(tt(a3(8), a3(8), a3(11), ALU.add))
                link(stt(c1(13), c1(5), eps, c1(10), ALU.add, ALU.add))
                link(ve.reciprocal(c1(13), c1(13)))
                link(stt(a3(8), a3(8), scale, a3(4), ALU.mult, ALU.mult))
                tt(a3(14), a3(8), cb(13), ALU.mult).then_inc(cw_ok, 1)
                dve.wait_ge(ct_done, n + 1)
                ct = v(PS, 2 * 512, [1, TOK], rows=e)
                ve.tensor_copy(spread_part(0, 0, e * R0, e), v(cst, C_S0, [1, e * R0], rows=e))
                link(ve.tensor_copy(spread_part(1, 0, TOK, e), ct))
                tt(spread_part(2, 0, TOK, e), ct, spread_part(1, 0, TOK, e).bitcast(F32), ALU.subtract).then_inc(ct_cp, 1)

            route(0, E0, 1e-6, 0.5)
            dve.wait_ge(rh_cp, 2)
            for half in range(2):
                for a in range(E0 // 2):
                    n = half * 8 + a
                    dve.wait_ge(bc_done, n + 1)
                    tt(wide(A_ if half else M_, (A_Z1 if half else M_U) + a * 512), bank(2 + n % 2),
                       wide(A_, A_RH + half * 512), ALU.mult).then_inc(z_ok, 1)
            dve.wait_ge(seq_in, 16)
            dve.wait_ge(tab_in, 16)
            dve.wait_ge(pad_out, 16)
            for q in range(4):
                r = dict(p0=S * q, rows=S)
                link(ts(v(idxv, 0, [1, B * 4], **r), v(tabi, q, [4, B * 4], **r), float(PSIZE), ALU.mult, v(cst, C_S, [1, 1], **r), ALU.add))
                link(ve.tensor_copy(v(stat, 40, [1, NT], **r), v(seqi, q, [4, NT], **r)))
            ts(tabi[:, :], tabi[:, :], float(P), ALU.mult, cst[:, C_P:C_P + 1], ALU.add).then_inc(idx_ok, 1)
            link(ts(stat[:, 40:40 + NT], stat[:, 40:40 + NT], cst[:, C_S:C_S + 1], ALU.add))
            link(ve.tensor_copy(seqf[:, :], seqi[:, :]))
            rp = lambda a: v(A_, A_RP + a * 512, [64, NT], [1, 64])
            rw = lambda a: wide(A_, A_RP + a * 512)
            link(tt(rp(4), v(stat, 40, [1, NT], [0, 64]), v(cst, C_IF, [0, NT], [1, 64]), ALU.mult))
            reduce_phase(rw(4), rw(1), rw(0), rope_arg)
            dve.wait_ge(nw_in, 32)
            wq, wk = A_RP + 5 * 512, A_RP + 5 * 512 + D
            link(ts(v(A_, wq, [1, D]), v(A_, wq, [1, D]), -SCALE, ALU.mult))
            dve.wait_ge(rope_sin, 2)
            link(tt(rw(3), rw(3), rw(3), ALU.mult))
            link(ts(rw(3), rw(3), -2.0, ALU.mult, 1.0, ALU.add))
            link(ts(rw(4), rw(2), -1.0, ALU.mult))

            def tables(c, w):
                wl, wh = (v(A_, w + 64 * a, [0, NT], [1, 64]) for a in range(2))
                to = lambda a: v(M_, M_TB + c * 256 + a * 64, [512, NT], [1, 64])
                tt(to(0), rp(3), wl, ALU.mult)
                tt(to(1), rp(3), wh, ALU.mult)
                tt(to(2), rp(4), wh, ALU.mult)
                link(tt(to(3), rp(2), wl, ALU.mult))

            for n in range(8):
                dve.wait_ge(y_done, n + 1)
                o = wide(x1T, (n % 4) * TOK + (n // 4) * 512)
                stt(o, bank(4 + n % 4), biasc[:, n % 4:n % 4 + 1], o, ALU.add, ALU.add).then_inc(x1_ok, 1)
                stage_keys(n)
                if n == 3:
                    tables(0, wq)
                    tables(1, wk)

            def chunk_job(n, par, j, count):
                dve.wait_ge(tp_done, n * 4 + (j + 1))
                dve.wait_ge(wj_act, count)
                tt(rounded(M_W[par] + 8 * KB + j * 512), bank(4 + j % 2), rounded(M_W[par] + j * 512).bitcast(F32),
                   ALU.subtract).then_inc(wj_dve, 1)

            for j in range(4):
                chunk_job(12, 0, j, j + 1)
            dve.wait_ge(r_done, NT)
            dve.wait_ge(xh_ok, 8)
            for j in range(NJ):
                last = tt(rounded(M_XL + j * TOK, TOK), v(x1T, j * TOK, [1, TOK]), rounded(M_XH + j * TOK, TOK).bitcast(F32),
                          ALU.subtract)
            last.then_inc(xl_ok, 1)

            def project_chunk(c, par):
                known = isinstance(c, int)

                def factors(s, g, early):
                    ms, sd = stat[:, g * 4:g * 4 + 4], stat[:, 32 + g * 4:36 + g * 4]
                    y, z = stat[:, 16 + 4 * g:20 + 4 * g], stat[:, 24 + 4 * g:28 + 4 * g]
                    dve.wait_ge(sq_ok, s + 1)
                    ts(ms, ms, 1.0 / D, ALU.mult, EPS, ALU.add).then_inc(ms_ok, 1)
                    if not early:
                        dve.wait_ge(sc_ok, s - 1)
                    dve.wait_ge(sd_ok, s + 1)
                    ve.reciprocal(y, sd).then_inc(nw_ok, 1)
                    dve.wait_ge(nw_ok, s * 3 + 1)
                    tt(z, y, y, ALU.mult).then_inc(nw_ok, 1)
                    dve.wait_ge(nw_ok, s * 3 + 2)
                    stt(z, z, -0.5, ms, ALU.mult, ALU.mult).then_inc(nw_ok, 1)
                    dve.wait_ge(nw_ok, s * 3 + 3)
                    stt(y, z, 1.5, y, ALU.add, ALU.mult).then_inc(nf_ok, 1)

                def rotate(s, g, t, early, keys):
                    dve.wait_ge(sc_ok, s + 1)
                    if not early:
                        dve.wait_ge(rt_done, s - 1)
                        dve.wait_ge(rot_ok, s - 1)
                    tb = M_TB + t * 512 + (256 if keys else 0)
                    tt(v(x1T, X_RA + g * 512, [P, 4], [1, P]), v(x1T, X_XN + g * 512, [P, 4], [1, P]),
                       v(M_, tb, [0, 4], [1, P]), ALU.mult)
                    for a in range(2):
                        last = tt(v(x1T, X_RB + g * 512 + 64 * a, [P, 4], [1, 64]), v(x1T, X_XN + g * 512 + 64 - 64 * a, [P, 4], [1, 64]),
                                  v(M_, tb + P + 64 * a, [0, 4], [1, 64]), ALU.mult)
                    last.then_inc(ab_ok, 1)

                for t in range(NT):
                    s, g = c * NT + t, t % 2
                    if not known or s < NROT:
                        factors(s, g, known and s < 2)
                    if not known or 0 <= s - 1 < NROT:
                        rotate(s - 1, 1 - g, (t - 1) % NT, known and s < 3, known and s - 1 >= 64)
                    if t < 4 and not (known and c == NCH - 1):
                        chunk_job(next_slot(c)[0], 1 - par, t, blocks_before(c) + (t + 1))
                    if t >= 4 and (not known or c < 8) and t % 2 == 1:
                        dve.wait_ge(tp_done, c * 8 + (56 + t - 3))
                        ve.tensor_copy(wide(A_, c * 2048 + (t - 4) * 512), bank(5)).then_inc(wj_dve, 1)

            project_chunk(0, 0)
            project_chunk(1, 1)
            dve.wait_ge(x1_out, 16)
            for half in range(2):
                dve.wait_ge(kst_out[half], 64)
            with dve.Fori(1, 4) as i:
                project_chunk(i * 2, 0)
                project_chunk(i * 2 + 1, 1)
            for c in range(8, NCH):
                project_chunk(c, c % 2)

            dve.wait_ge(rt_cp, NROT)
            dve.wait_ge(v_cp, NST - NROT)
            dve.wait_ge(wj_act, 64)
            ve.memset(bank(5, P), 0.0).then_inc(pz_ok, 1)
            dve.wait_ge(tp_done, 128)

            mrow = v(M_, M_MR, [1, KEYS])

            def split(i, u):
                par, h = (u // HK) % 2, u % HK
                dve.wait_ge(kh_ok, i * 16 + u + 1)
                o = M_QS + (u % RING) * 2 * P
                tt(rounded(o + P, P), v(M_, M_QT + par * HQ * S + h * P, [1, P]), rounded(o, P).bitcast(F32), ALU.subtract)
                o = M_KS + (u % RING) * 2 * KEYS
                tt(rounded_blocks(o + KEYS, KEYS // S), v(A_, A_KT + par * KTB + h * S, [256, KEYS // S], [1, S]),
                   rounded_blocks(o, KEYS // S).bitcast(F32), ALU.subtract).then_inc(kl_ok, 1)

            def mask_min(i, u):
                g, k, n = u % 2, (u // HK) % 2, i * 16 + u
                if u % 16 == 0:
                    ii = i + u // 16
                    ve.tensor_copy(seqc[:, :], v(seqf, ii * 2, [1, 2])).then_inc(seqc_ok, 1)
                    dve.wait_ge(seqc_ok, ii + 1)
                if u % HK == 0:
                    ts(mrow, v(cst, C_POS, [1, KEYS]), seqc[:, k:k + 1], ALU.is_ge, FAR, ALU.mult).then_inc(mrow_ok, 1)
                    dve.wait_ge(mrow_ok, i * 2 + u // HK + 1)
                dve.wait_ge(s_done, n + 1)
                if not isinstance(n, int) or n >= 2:
                    dve.wait_ge(pt_done, n - 1)
                ve.memset(stat[:, 58 + g:59 + g], 0.0)
                ve.tensor_tensor_reduce(v(M_, M_S + g * KEYS, [1, KEYS]), v(PS, g * 1024 + 512 - 9 * S, [1, KEYS]), mrow, 1.0, 3.0e38,
                                        ALU.add, ALU.min, stat[:, g:g + 1]).then_inc(sm_ok, 1)

            def normalise(i, u):
                g, n = u % 2, i * 16 + u
                dve.wait_ge(e_ok, n + 1)
                ve.reciprocal(stat[:, 12 + g:13 + g], stat[:, 8 + g:9 + g]).then_inc(rs_ok, 1)
                dve.wait_ge(rs_ok, n + 1)
                s = v(M_, M_S + g * KEYS, [1, KEYS])
                ts(s, s, stat[:, 12 + g:13 + g], ALU.mult).then_inc(p_ok, 1)

            def two_batches(i):
                known = isinstance(i, int)
                for u in range(16):
                    if not known or i * 16 + u + 1 < B * HK:
                        mask_min(i, u + 1)
                    normalise(i, u)
                    if not known or i * 16 + u + RING - 1 < B * HK:
                        split(i, u + RING - 1)

            for u in range(RING - 1):
                split(0, u)
            mask_min(0, 0)
            two_batches(0)
            with dve.Fori(1, B // 2 - 1) as i:
                two_batches(i)
            two_batches(B // 2 - 1)

            odd_jobs(32, lambda j: (wide(M_, M_LA + j * 512), bank(j)))
            odd_jobs(33, lambda j: (wide(M_, M_LB + j * 512), bank(j)))

            def split_head(g, par, hh):
                m, o = g * 4 + hh, M_HD + (hh % 2) * 3072
                dve.wait_ge(hh_ok, m * 2 + 1)
                tt(rounded(o + 512), wide(A_, A_WG + par * 2048 + hh * 512), rounded(o).bitcast(F32), ALU.subtract)
                dve.wait_ge(hh_ok, m * 2 + 2)
                tt(rounded_blocks(o + 2048, B), v(A_, A_OG + par * 4096 + hh * S, [128, B], [1, S]),
                   rounded_blocks(o + 1024, B).bitcast(F32), ALU.subtract).then_inc(hl_ok, 1)

            for par in range(2):
                for hh in range(4):
                    split_head(par, par, hh)
            with dve.Fori(1, HQ // 8) as i:
                for par in range(2):
                    for hh in range(4):
                        split_head(i * 2 + par, par, hh)
            dve.wait_ge(hd_done, HQ)
            for k in (1, 3, 5, 7):
                ve.tensor_copy(wide(x1T, k * 512), bank(k)).then_inc(at_cp, 1)

            route(1, E1, 0.0, 1.0)
            for n in range(8):
                half, a = n // 4, n % 4
                dve.wait_ge(bc_done, 16 + n + 1)
                dve.wait_ge(ha_cp, n + 1)
                tt(wide(A_, half * 2048 + a * 512), bank(2 + n % 2), wide(A_, A_RH + (n % 2) * 512), ALU.mult).then_inc(z_ok, 1)
            dve.wait_ge(x1_back, 16)
            for t in range(NT):
                dve.wait_ge(ob_done, t + 1)
                o = wide(M_, M_XB + t * HID)
                tt(o, bank(t % 2), o, ALU.add).then_inc(ob_cp, 1)


_INS = ['x', 'itok_B_8_3872', 'itok_Bx16_0_63', 'itok_B_207_1644', 'L0_cond_log_dt', 'L0_cond_C', 'L0_cond_log_A_real',
        'L0_cond_A_imag', 'L0_cond_D', 'L0_ffn_base_w', 'L0_ffn_base_b', 'L0_ffn_A', 'L0_ffn_B', 'L0_ffn_router_w',
        'L1_cond_Wq', 'L1_cond_Wk', 'L1_cond_Wv', 'L1_cond_Wo', 'L1_cond_q_norm_w', 'L1_cond_k_norm_w',
        'L1_cond_k_cache', 'L1_cond_v_cache', 'L1_ffn_gate_w', 'L1_ffn_lora_A', 'L1_ffn_lora_B']
SCRATCH_KIND = "Internal"


def kernel(**inputs):
    import concourse.bacc as _bacc
    from concourse.bass_utils import run_bass_kernel_spmd as _run

    nc = _bacc.Bacc("TRN2", target_bir_lowering=False, num_devices=1)
    arrays, args = {}, []
    for name, a in [*((n, inputs[n]) for n in _INS), ("const", constants())]:
        a = np.ascontiguousarray(a)
        arrays[f"in_{name}"] = a
        args.append(nc.dram_tensor(f"in_{name}", a.shape, mybir.dt.from_np(a.dtype), kind="ExternalInput").ap())
    out = nc.dram_tensor("out_0", (B, S, HID), F32, kind="ExternalOutput").ap()

    def scratch(name, shape):
        return nc.dram_tensor(f"scratch_{name}", shape, F32, kind=SCRATCH_KIND).ap()

    adaln_program(nc, *args, out, scratch)
    r = _run(nc, [arrays], core_ids=[0])
    return r.results[0]["out_0"]
```
